# Optimizing a Trainium2 kernel written in Bass

```python
import numpy as np
import jax
import jax.numpy as jnp

def _softmax(x, axis=-1):
    return jax.nn.softmax(x, axis=axis)

def _gelu(x):
    return jax.nn.gelu(x, approximate=True)

def _silu(x):
    return jax.nn.silu(x)

def _sigmoid(x):
    return jax.nn.sigmoid(x)

def _layernorm(x, axis=-1, eps=1e-05):
    m = jnp.mean(x, axis=axis, keepdims=True)
    v = jnp.var(x, axis=axis, keepdims=True)
    return (x - m) / jnp.sqrt(v + eps)

def _scatter_add(tgt, idx, src, axis=0):
    return tgt.at[idx].add(src)

def _segment_sum(src, seg, n):
    return jax.ops.segment_sum(src, seg, n)
kernel_name = 'mk_cond_seq_d2_seqx_r2_79ede9'

def setup_inputs(seed: int=0):
    np.random.seed(seed)
    _w = jnp.asarray

    def _rec_inputs():
        import jax
        import jax.numpy as jnp
        _rk = jax.random.key(seed)
        x = 7.22e-05 + 1 * jax.random.normal(jax.random.fold_in(_rk, 1), (64, 128, 512), jnp.float32)
        _lenS = 128 - jax.random.randint(jax.random.fold_in(_rk, 7), (64,), 0, max(1, 128 // 4) + 1, jnp.int32)
        _lenS2 = 128 - jax.random.randint(jax.random.fold_in(_rk, 8), (64,), 0, max(1, 128 // 4) + 1, jnp.int32)
        cond_2048 = 0.00782532 + 1.00527 * jax.random.normal(jax.random.fold_in(_rk, 11), (64, 1024), jnp.float32)
        _validS = jnp.arange(128)[None, :] < _lenS[:, None]
        _validS2 = jnp.arange(128)[None, :] < _lenS2[:, None]
        _causal = jnp.tril(jnp.ones((128, 128), dtype=bool))
        mask_BxSx1_fk1 = jnp.where(jnp.ones((64, 128, 1), dtype=bool), 1.0, 0.0).astype(jnp.float32)
        mask_BxS_ff1 = jnp.where(jnp.ones((64, 128), dtype=bool), 1.0, 0.0).astype(jnp.float32)
        return (x, cond_2048, mask_BxSx1_fk1, mask_BxS_ff1)
    x, cond_2048, mask_BxSx1_fk1, mask_BxS_ff1 = _rec_inputs()

    def _L0_cond_setup():
        import jax, jax.numpy as jnp
        import numpy as np
        B, T, D, H, TE = (4, 1024, 512, 8, 1024)
        EPS = 1e-05

        def _ln(x, w, b):
            m = jnp.mean(x, axis=-1, keepdims=True)
            v = jnp.mean((x - m) ** 2, axis=-1, keepdims=True)
            return (x - m) * jax.lax.rsqrt(v + EPS) * w + b
        key = jax.random.key(seed)
        ks = jax.random.split(key, 16)
        s = 0.02
        inp = {'x': jax.random.normal(ks[0], (B, T, D), jnp.float32), 'emb': jax.random.normal(ks[1], (B, TE), jnp.float32), 'src_mask': (jax.random.uniform(ks[2], (B, T, 1)) > 0.2).astype(jnp.float32), 'num_head': H, 'ln_w': jnp.ones((D,), jnp.float32), 'ln_b': jnp.zeros((D,), jnp.float32), 'Wq': jax.random.normal(ks[3], (D, D), jnp.float32) * s, 'bq': jnp.zeros((D,), jnp.float32), 'Wk': jax.random.normal(ks[4], (D, D), jnp.float32) * s, 'bk': jnp.zeros((D,), jnp.float32), 'Wv': jax.random.normal(ks[5], (D, D), jnp.float32) * s, 'bv': jnp.zeros((D,), jnp.float32), 'W_emb': jax.random.normal(ks[6], (TE, 2 * D), jnp.float32) * s, 'b_emb': jnp.zeros((2 * D,), jnp.float32), 'ln2_w': jnp.ones((D,), jnp.float32), 'ln2_b': jnp.zeros((D,), jnp.float32), 'W_out': jax.random.normal(ks[7], (D, D), jnp.float32) * s, 'b_out': jnp.zeros((D,), jnp.float32)}
        return inp
    _L0_cond_all = _L0_cond_setup()
    _L0_cond_in = {k: v for k, v in _L0_cond_all.items() if k in ('ln_w', 'ln_b', 'Wq', 'bq', 'Wk', 'bk', 'Wv', 'bv', 'W_emb', 'b_emb', 'ln2_w', 'ln2_b', 'W_out', 'b_out')}
    del _L0_cond_all

    def _L1_cond_setup():
        import jax, jax.numpy as jnp
        import numpy as np
        B, T, D, H, TE = (8, 512, 512, 16, 1024)
        LN_EPS = 1e-05

        def layer_norm(x, w, b):
            m = jnp.mean(x, axis=-1, keepdims=True)
            v = jnp.var(x, axis=-1, keepdims=True)
            return (x - m) / jnp.sqrt(v + LN_EPS) * w + b
        key = jax.random.key(seed)
        ks = jax.random.split(key, 8)
        s = lambda k, sh: jax.random.normal(k, sh, jnp.float32) * 0.02
        return dict(x=jax.random.normal(ks[0], (B, T, D), jnp.float32), emb=jax.random.normal(ks[1], (B, TE), jnp.float32), src_mask=jnp.ones((B, T), jnp.float32), norm_w=jnp.ones((D,), jnp.float32), norm_b=jnp.zeros((D,), jnp.float32), q_w=s(ks[2], (D, D)), q_b=jnp.zeros((D,), jnp.float32), k_w=s(ks[3], (D, D)), k_b=jnp.zeros((D,), jnp.float32), v_w=s(ks[4], (D, D)), v_b=jnp.zeros((D,), jnp.float32), emb_w=s(ks[5], (TE, 2 * D)), emb_b=jnp.zeros((2 * D,), jnp.float32), sb_norm_w=jnp.ones((D,), jnp.float32), sb_norm_b=jnp.zeros((D,), jnp.float32), out_w=s(ks[6], (D, D)), out_b=jnp.zeros((D,), jnp.float32))
    _L1_cond_all = _L1_cond_setup()
    _L1_cond_in = {k: v for k, v in _L1_cond_all.items() if k in ('norm_w', 'norm_b', 'q_w', 'q_b', 'k_w', 'k_b', 'v_w', 'v_b', 'emb_w', 'emb_b', 'sb_norm_w', 'sb_norm_b', 'out_w', 'out_b')}
    del _L1_cond_all
    return {'x': x, 'cond_2048': cond_2048, 'mask_BxSx1_fk1': mask_BxSx1_fk1, 'mask_BxS_ff1': mask_BxS_ff1, 'L0_cond_ln_w': _L0_cond_in['ln_w'], 'L0_cond_ln_b': _L0_cond_in['ln_b'], 'L0_cond_Wq': _L0_cond_in['Wq'], 'L0_cond_bq': _L0_cond_in['bq'], 'L0_cond_Wk': _L0_cond_in['Wk'], 'L0_cond_bk': _L0_cond_in['bk'], 'L0_cond_Wv': _L0_cond_in['Wv'], 'L0_cond_bv': _L0_cond_in['bv'], 'L0_cond_W_emb': _L0_cond_in['W_emb'], 'L0_cond_b_emb': _L0_cond_in['b_emb'], 'L0_cond_ln2_w': _L0_cond_in['ln2_w'], 'L0_cond_ln2_b': _L0_cond_in['ln2_b'], 'L0_cond_W_out': _L0_cond_in['W_out'], 'L0_cond_b_out': _L0_cond_in['b_out'], 'L1_cond_norm_w': _L1_cond_in['norm_w'], 'L1_cond_norm_b': _L1_cond_in['norm_b'], 'L1_cond_q_w': _L1_cond_in['q_w'], 'L1_cond_q_b': _L1_cond_in['q_b'], 'L1_cond_k_w': _L1_cond_in['k_w'], 'L1_cond_k_b': _L1_cond_in['k_b'], 'L1_cond_v_w': _L1_cond_in['v_w'], 'L1_cond_v_b': _L1_cond_in['v_b'], 'L1_cond_emb_w': _L1_cond_in['emb_w'], 'L1_cond_emb_b': _L1_cond_in['emb_b'], 'L1_cond_sb_norm_w': _L1_cond_in['sb_norm_w'], 'L1_cond_sb_norm_b': _L1_cond_in['sb_norm_b'], 'L1_cond_out_w': _L1_cond_in['out_w'], 'L1_cond_out_b': _L1_cond_in['out_b']}

def reference(x, cond_2048, mask_BxSx1_fk1, mask_BxS_ff1, L0_cond_ln_w, L0_cond_ln_b, L0_cond_Wq, L0_cond_bq, L0_cond_Wk, L0_cond_bk, L0_cond_Wv, L0_cond_bv, L0_cond_W_emb, L0_cond_b_emb, L0_cond_ln2_w, L0_cond_ln2_b, L0_cond_W_out, L0_cond_b_out, L1_cond_norm_w, L1_cond_norm_b, L1_cond_q_w, L1_cond_q_b, L1_cond_k_w, L1_cond_k_b, L1_cond_v_w, L1_cond_v_b, L1_cond_emb_w, L1_cond_emb_b, L1_cond_sb_norm_w, L1_cond_sb_norm_b, L1_cond_out_w, L1_cond_out_b):
    import jax
    import jax.numpy as jnp

    def _L0_cond_ref(x, emb, src_mask, num_head, ln_w, ln_b, Wq, bq, Wk, bk, Wv, bv, W_emb, b_emb, ln2_w, ln2_b, W_out, b_out):
        import jax, jax.numpy as jnp
        import numpy as np
        B, T, D, H, TE = (4, 1024, 512, 8, 1024)
        EPS = 1e-05

        def _ln(x, w, b):
            m = jnp.mean(x, axis=-1, keepdims=True)
            v = jnp.mean((x - m) ** 2, axis=-1, keepdims=True)
            return (x - m) * jax.lax.rsqrt(v + EPS) * w + b
        b, t, d = x.shape
        h = num_head
        dh = d // h
        xn = _ln(x, ln_w, ln_b)
        q = xn @ Wq + bq
        k = xn @ Wk + bk + (1.0 - src_mask) * -1000000.0
        q = jax.nn.softmax(q.reshape(b, t, h, dh), axis=-1)
        k = jax.nn.softmax(k.reshape(b, t, h, dh), axis=1)
        v = ((xn @ Wv + bv) * src_mask).reshape(b, t, h, dh)
        att = jnp.einsum('bnhd,bnhl->bhdl', k, v)
        y = jnp.einsum('bnhd,bhdl->bnhl', q, att).reshape(b, t, d)
        emb_out = (jax.nn.silu(emb) @ W_emb + b_emb)[:, None, :]
        scale, shift = jnp.split(emb_out, 2, axis=2)
        hh = _ln(y, ln2_w, ln2_b) * (1.0 + scale) + shift
        hh = jax.nn.silu(hh) @ W_out + b_out
        return x + hh

    def _L1_cond_ref(x, emb, src_mask, norm_w, norm_b, q_w, q_b, k_w, k_b, v_w, v_b, emb_w, emb_b, sb_norm_w, sb_norm_b, out_w, out_b):
        import jax, jax.numpy as jnp
        import numpy as np
        B, T, D, H, TE = (8, 512, 512, 16, 1024)
        LN_EPS = 1e-05

        def layer_norm(x, w, b):
            m = jnp.mean(x, axis=-1, keepdims=True)
            v = jnp.var(x, axis=-1, keepdims=True)
            return (x - m) / jnp.sqrt(v + LN_EPS) * w + b
        Bx, Tx, Dx = x.shape
        xn = layer_norm(x, norm_w, norm_b)
        q = (xn @ q_w + q_b).reshape(Bx, Tx, H, -1)
        k = (xn @ k_w + k_b).reshape(Bx, Tx, H, -1)
        att = jnp.einsum('bnhl,bmhl->bnmh', q, k)
        mask = src_mask.reshape(Bx, 1, Tx, 1)
        att = att + (1.0 - mask) * -1000000.0
        att = jax.nn.softmax(att, axis=2)
        v = ((xn @ v_w + v_b) * src_mask[:, :, None]).reshape(Bx, Tx, H, -1)
        y = jnp.einsum('bnmh,bmhl->bnhl', att, v).reshape(Bx, Tx, Dx)
        e = jax.nn.silu(emb) @ emb_w + emb_b
        scale, shift = jnp.split(e[:, None, :], 2, axis=2)
        h = layer_norm(y, sb_norm_w, sb_norm_b) * (1.0 + scale) + shift
        h = jax.nn.silu(h) @ out_w + out_b
        return x + h
    x = _L0_cond_ref(x, cond_2048, mask_BxSx1_fk1, 8, L0_cond_ln_w, L0_cond_ln_b, L0_cond_Wq, L0_cond_bq, L0_cond_Wk, L0_cond_bk, L0_cond_Wv, L0_cond_bv, L0_cond_W_emb, L0_cond_b_emb, L0_cond_ln2_w, L0_cond_ln2_b, L0_cond_W_out, L0_cond_b_out)
    x = _L1_cond_ref(x, cond_2048, mask_BxS_ff1, L1_cond_norm_w, L1_cond_norm_b, L1_cond_q_w, L1_cond_q_b, L1_cond_k_w, L1_cond_k_b, L1_cond_v_w, L1_cond_v_b, L1_cond_emb_w, L1_cond_emb_b, L1_cond_sb_norm_w, L1_cond_sb_norm_b, L1_cond_out_w, L1_cond_out_b)
    return x

_drawn_inputs = setup_inputs


def setup_inputs(seed=0):
    import zlib

    import numpy as np

    out = dict(_drawn_inputs(seed))
    spreads = {'L0_cond_ln_w': (1.0, 0.586),
     'L0_cond_ln_b': (0.0, 0.1),
     'L0_cond_bq': (0.0, 0.8),
     'L0_cond_bk': (0.0, 0.8),
     'L0_cond_bv': (0.0, 0.1),
     'L0_cond_b_emb': (0.0, 0.1),
     'L0_cond_ln2_w': (1.0, 0.2),
     'L0_cond_ln2_b': (0.0, 0.1),
     'L0_cond_b_out': (0.0, 0.1),
     'L1_cond_norm_w': (1.0, 0.2),
     'L1_cond_norm_b': (0.0, 0.1),
     'L1_cond_q_b': (0.0, 0.294),
     'L1_cond_k_b': (0.0, 0.8),
     'L1_cond_v_b': (0.0, 0.1),
     'L1_cond_emb_b': (0.0, 0.1),
     'L1_cond_sb_norm_w': (1.0, 0.2),
     'L1_cond_sb_norm_b': (0.0, 0.1),
     'L1_cond_out_b': (0.0, 0.1)}
    factors = {'L0_cond_Wq': 8.0, 'L0_cond_Wk': 5.728}
    for name, (base, spread) in spreads.items():
        noise = np.random.default_rng([zlib.crc32(name.encode()), seed]).standard_normal(out[name].shape)
        drawn = base * np.exp(spread * noise) if base else spread * noise
        out[name] = jnp.asarray(drawn.astype(out[name].dtype))
    for name, factor in factors.items():
        out[name] = (out[name] * factor).astype(out[name].dtype)
    return out
```

```python
from contextlib import ExitStack

import concourse.bass as bass
from concourse import mybir

F32 = mybir.dt.float32
F32R = mybir.dt.float32r
ALU = mybir.AluOpType
ACT = mybir.ActivationFunctionType
AX_X = mybir.AxisListType.X

P = 128
PAIR = 2
RING = 3
RB = 64
BIG = -1000000.0
EPS = 1e-5

ROW_MASK = 96
ROW_SHIFT = 98
K_SCORE = 98
K_SHIFTED = 99


def seq(per, pair, k):
    return pair * per + k


def f32(ap):
    return ap.bitcast(F32)


def build(nc, T, out):
    x_d, cond_d = T["x"], T["cond_2048"]
    B, S, D = x_d.shape
    TE = cond_d.shape[1]
    NP = B // PAIR
    C = D // P
    H0, H1 = 8, 16
    HC = H1 // C
    D0, D1 = D // H0, D // H1
    KE = TE // P
    assert S == P and D1 == 32 and D0 == 64 and NP > 4

    x1_d = nc.dram_tensor("x_between_layers", [B, S, D], F32).ap()
    mask_d = nc.dram_tensor("mask_parts", [2, B, S], F32).ap()

    root = ExitStack()
    with root:
        def sem(name):
            return root.enter_context(nc.semaphore(name))

        def sb(ctx, name, shape, dt=F32):
            return ctx.enter_context(nc.sbuf_tensor(name, shape, dt))

        ps = [root.enter_context(nc.psum_tensor(f"bank{i}", [P, 512], F32)) for i in range(8)]

        w_hi = sb(root, "w_hi", [P, 4, C, D], F32R)
        w_lo = sb(root, "w_lo", [P, 4, C, D], F32R)
        ident = sb(root, "ident", [P, P])
        ones = sb(root, "ones", [RB, P], F32R)
        bias_rows = sb(root, "bias_rows", [RB, 3, D], F32R)
        half_gain = sb(root, "half_gain", [P, 2, C, B])
        half_shift = sb(root, "half_shift", [P, 2, C, B])
        vec = sb(root, "vec", [P, 64])
        mask_col = sb(root, "mask_col", [P, 2, B])
        mask_hi = sb(root, "mask_hi", [B, 2, P], F32R)
        mask_lo = sb(root, "mask_lo", [B, 2, P], F32R)
        eps = sb(root, "eps", [P, 2])
        neg_half = sb(root, "neg_half", [P, 2])

        vec_rows = {}
        at = 0
        for name in ("L0_cond_ln_w", "L0_cond_ln_b", "L0_cond_ln2_w", "L0_cond_ln2_b", "L0_cond_b_emb",
                     "L1_cond_norm_w", "L1_cond_norm_b", "L1_cond_sb_norm_w", "L1_cond_sb_norm_b",
                     "L1_cond_emb_b", "L1_cond_q_b", "L1_cond_k_b"):
            n = T[name].shape[0] // P
            vec_rows[name] = (at, n)
            at += n
        n_vec = at

        def vcol(name, c):
            r = vec_rows[name][0] + c
            return vec[:, r:r + 1]

        setup_common(nc, T, sem, sb, ps, ident, ones, half_gain, half_shift, vec, vec_rows, n_vec, vcol,
                     mask_col, mask_hi, mask_lo, mask_d, eps, neg_half, B, D, C, KE)

        with ExitStack() as ctx:
            key_bias = sb(ctx, "key_bias", [P, D], F32R)
            mask_rows = sb(ctx, "mask_rows", [P, B * P], F32R)
            setup_weights(nc, 0, [("L0_cond_Wq", "L0_cond_bq"), ("L0_cond_Wk", "L0_cond_bk"),
                                  ("L0_cond_Wv", "L0_cond_bv"), ("L0_cond_W_out", "L0_cond_b_out")],
                          "L0_cond_ln_w", "L0_cond_ln_b", T, sem, sb, ps, w_hi, w_lo, bias_rows, vec, vec_rows,
                          vcol, D, C, key_bias=key_bias)
            layer0(nc, ctx, sem, sb, ps, x_d, x1_d, w_hi, w_lo, ident, ones, bias_rows, key_bias, mask_rows,
                   half_gain, half_shift, mask_col, mask_hi, mask_lo, eps, neg_half, B, NP, D, C, H0, D0)

        with ExitStack() as ctx:
            qk_bias = sb(ctx, "qk_bias", [P, 2, C])
            setup_weights(nc, 1, [("L1_cond_q_w", "L1_cond_q_b"), ("L1_cond_k_w", "L1_cond_k_b"),
                                  ("L1_cond_v_w", "L1_cond_v_b"), ("L1_cond_out_w", "L1_cond_out_b")],
                          "L1_cond_norm_w", "L1_cond_norm_b", T, sem, sb, ps, w_hi, w_lo, bias_rows, vec, vec_rows,
                          vcol, D, C, qk_bias=qk_bias)
            layer1(nc, ctx, sem, sb, ps, x1_d, out, w_hi, w_lo, ident, ones, bias_rows, qk_bias,
                   half_gain, half_shift, mask_col, mask_d, eps, neg_half, B, NP, D, C, HC, H1, D1)


def setup_common(nc, T, sem, sb, ps, ident, ones, half_gain, half_shift, vec, vec_rows, n_vec, vcol,
                 mask_col, mask_hi, mask_lo, mask_d, eps, neg_half, B, D, C, KE):
    with ExitStack() as ctx:
        vec_in = sb(ctx, "vec_in", [n_vec, P])
        mask_in = sb(ctx, "mask_in", [B, 2, P])
        mask_term = sb(ctx, "mask_term", [B, 2, P])
        mask_top = sb(ctx, "mask_top", [B, 2])
        cond = sb(ctx, "cond", [B, KE * P])
        cond_half = sb(ctx, "cond_half", [B, KE * P])
        cond_tanh = sb(ctx, "cond_tanh", [B, KE * P])
        cond_silu = sb(ctx, "cond_silu", [B, KE * P])
        cond_T = sb(ctx, "cond_T", [P, KE, B])
        w_emb = [sb(ctx, f"w_emb{n}", [P, KE, 2 * D]) for n in range(2)]
        one_scale = sb(ctx, "one_scale", [P, 2, C, B])
        shift = sb(ctx, "shift", [P, 2, C, B])

        small_in = sem("small_in")
        emb_in = [sem("emb_in0"), sem("emb_in1")]
        zeroed = sem("zeroed")
        ident_ready = sem("ident_ready")
        consts_ready = sem("consts_ready")
        vec_ps, vec_ready = sem("vec_ps"), sem("vec_ready")
        mask_ps, mask_step, mask_out = sem("mask_ps"), sem("mask_step"), sem("mask_out")
        tanh_ready, cond_step = sem("tanh_ready"), sem("cond_step")
        cond_ps, cond_ready = sem("cond_ps"), sem("cond_ready")
        emb_ps, emb_step = sem("emb_ps"), sem("emb_step")

        loads = [(cond[:], T["cond_2048"]),
                 (mask_in[:, 0, :], T["mask_BxSx1_fk1"].rearrange("b s o -> b (s o)")),
                 (mask_in[:, 1, :], T["mask_BxS_ff1"])]
        for name, (r, n) in vec_rows.items():
            loads.append((vec_in[r:r + n, :], T[name].rearrange("(c p) -> c p", p=P)))

        block = ctx.enter_context(nc.Block())

        @block.sync
        def _(sp):
            for dst, src in loads:
                sp.dma_start(dst, src).then_inc(small_in, 16)
            for n, name in enumerate(("L0_cond_W_emb", "L1_cond_emb_w")):
                sp.dma_start(w_emb[n][:], T[name].rearrange("(k p) n -> p k n", p=P)).then_inc(emb_in[n], 16)
            sp.wait_ge(mask_step, 6)
            for n, part in enumerate((mask_hi, mask_lo)):
                sp.dma_start(mask_d[n], f32(part[:, 1, :])).then_inc(mask_out, 16)
            sp.wait_ge(mask_out, 32)

        @block.gpsimd
        def _(pool):
            nc.gpsimd.memset(ident[:], 0.0).then_inc(zeroed, 1)
            pool.wait_ge(zeroed, 1)
            nc.gpsimd.affine_select(out=ident[:], in_=ident[:], compare_op=ALU.not_equal, fill=1.0, base=0,
                                    pattern=[[-1, P]], channel_multiplier=1).then_inc(ident_ready, 1)
            nc.gpsimd.memset(eps[:], EPS)
            nc.gpsimd.memset(neg_half[:], -0.5)
            nc.gpsimd.memset(f32(ones[:]), 1.0).then_inc(consts_ready, 1)

        @block.scalar
        def _(act):
            act.wait_ge(small_in, 16 * len(loads))
            nc.scalar.activation(cond_tanh[:], cond[:], ACT.Tanh, scale=0.5).then_inc(tanh_ready, 1)
            act.wait_ge(vec_ps, 1)
            nc.scalar.activation(vec[:, 0:n_vec], ps[0][:, 0:n_vec], ACT.Copy).then_inc(vec_ready, 1)
            act.wait_ge(mask_ps, 1)
            nc.scalar.activation(mask_col[:], ps[1][:, 0:2 * B].rearrange("p (l b) -> p l b", l=2), ACT.Copy)
            act.wait_ge(cond_ps, 1)
            nc.scalar.activation(cond_T[:], ps[2][:, 0:KE * B].rearrange("p (k b) -> p k b", k=KE),
                                 ACT.Copy).then_inc(cond_ready, 1)

        @block.vector
        def _(dve):
            dve.wait_ge(small_in, 16 * len(loads))
            nc.vector.tensor_scalar(cond_half[:], cond[:], 0.5, None, ALU.mult).then_inc(cond_step, 1)
            nc.vector.tensor_scalar(mask_term[:], mask_in[:], -1.0, 1.0, ALU.mult, ALU.add).then_inc(mask_step, 1)
            dve.wait_ge(mask_step, 1)
            nc.vector.tensor_scalar(mask_term[:], mask_term[:], BIG, None, ALU.mult).then_inc(mask_step, 1)
            dve.wait_ge(mask_step, 2)
            nc.vector.reduce_max(mask_top[:], mask_term[:], AX_X).then_inc(mask_step, 1)
            dve.wait_ge(mask_step, 3)
            for n in range(2):
                last = nc.vector.tensor_scalar(mask_term[:, n, :], mask_term[:, n, :], mask_top[:, n:n + 1], None,
                                               ALU.subtract)
            last.then_inc(mask_step, 1)
            dve.wait_ge(mask_step, 4)
            nc.vector.tensor_copy(mask_hi[:], mask_term[:]).then_inc(mask_step, 1)
            dve.wait_ge(mask_step, 5)
            nc.vector.tensor_tensor(mask_lo[:], mask_term[:], f32(mask_hi[:]), ALU.subtract).then_inc(mask_step, 1)
            dve.wait_ge(tanh_ready, 1)
            dve.wait_ge(cond_step, 1)
            nc.vector.scalar_tensor_tensor(cond_silu[:], cond_tanh[:], 1.0, cond_half[:], ALU.add,
                                           ALU.mult).then_inc(cond_step, 1)
            dve.wait_ge(vec_ready, 1)
            for n, pre in enumerate((("L0_cond_b_emb", "L0_cond_ln2_w", "L0_cond_ln2_b"),
                                     ("L1_cond_emb_b", "L1_cond_sb_norm_w", "L1_cond_sb_norm_b"))):
                be, gw, gb = pre
                dve.wait_ge(emb_ps, n + 1)
                for c in range(C):
                    nc.vector.tensor_scalar(one_scale[:, n, c, :], ps[4 + n][:, c * B:(c + 1) * B], vcol(be, c),
                                            1.0, ALU.add, ALU.add)
                    last = nc.vector.tensor_scalar(shift[:, n, c, :], ps[4 + n][:, (C + c) * B:(C + c + 1) * B],
                                                   vcol(be, C + c), None, ALU.add)
                last.then_inc(emb_step, 1)
                dve.wait_ge(emb_step, 3 * n + 1)
                for c in range(C):
                    nc.vector.tensor_scalar(half_gain[:, n, c, :], one_scale[:, n, c, :], vcol(gw, c), 0.5,
                                            ALU.mult, ALU.mult)
                    last = nc.vector.scalar_tensor_tensor(shift[:, n, c, :], one_scale[:, n, c, :], vcol(gb, c),
                                                          shift[:, n, c, :], ALU.mult, ALU.add)
                last.then_inc(emb_step, 1)
                dve.wait_ge(emb_step, 3 * n + 2)
                nc.vector.tensor_scalar(half_shift[:, n], shift[:, n], 0.5, None, ALU.mult).then_inc(emb_step, 1)

        @block.tensor
        def _(pe):
            pe.wait_ge(ident_ready, 1)
            pe.wait_ge(small_in, 16 * len(loads))
            nc.tensor.transpose(ps[0][:, 0:n_vec], vec_in[:], ident[0:n_vec, 0:n_vec]).then_inc(vec_ps, 1)
            for n in range(2):
                last = nc.tensor.transpose(ps[1][:, n * B:(n + 1) * B], mask_in[:, n, :], ident[0:B, 0:B])
            last.then_inc(mask_ps, 1)
            pe.wait_ge(cond_step, 2)
            for k in range(KE):
                last = nc.tensor.transpose(ps[2][:, k * B:(k + 1) * B], cond_silu[:, k * P:(k + 1) * P],
                                           ident[0:B, 0:B])
            last.then_inc(cond_ps, 1)
            pe.wait_ge(cond_ready, 1)
            for n in range(2):
                pe.wait_ge(emb_in[n], 16)
                for f in range(2 * C):
                    for k in range(KE):
                        last = nc.tensor.matmul(ps[4 + n][:, f * B:(f + 1) * B], w_emb[n][:, k, f * P:(f + 1) * P],
                                                cond_T[:, k, :], start=(k == 0), stop=(k == KE - 1))
                last.then_inc(emb_ps, 1)


def setup_weights(nc, layer, mats, lnw, lnb, T, sem, sb, ps, w_hi, w_lo, bias_rows, vec, vec_rows, vcol, D, C,
                  key_bias=None, qk_bias=None):
    with ExitStack() as ctx:
        raw = [sb(ctx, f"raw{layer}_{n}", [P, C, D]) for n in range(4)]
        bias_in = sb(ctx, f"bias_in{layer}", [1, 4, D])
        bias_f = sb(ctx, f"bias_f{layer}", [1, 4, D])
        raw_in = [sem(f"raw_in{layer}_{n}") for n in range(4)]
        bias_loaded = sem(f"bias_loaded{layer}")
        bias_ps = sem(f"bias_ps{layer}")
        cleared = sem(f"cleared{layer}")
        bias_step = sem(f"bias_step{layer}")
        folded, split = sem(f"folded{layer}"), sem(f"split{layer}")
        off = vec_rows[lnb][0]
        rows_of = {0: 0, 2: 1, 3: 2}

        block = ctx.enter_context(nc.Block())

        @block.sync
        def _(sp):
            for n, (w, b) in enumerate(mats):
                sp.dma_start(bias_in[:, n, :], T[b].rearrange("(o d) -> o d", o=1)).then_inc(bias_loaded, 16)
            for n, (w, b) in enumerate(mats):
                sp.dma_start(raw[n][:], T[w].rearrange("(c p) n -> p c n", p=P)).then_inc(raw_in[n], 16)

        @block.gpsimd
        def _(pool):
            nc.gpsimd.memset(f32(bias_rows[:]), 0.0).then_inc(cleared, 1)
            if key_bias is not None:
                nc.gpsimd.memset(f32(key_bias[:]), 0.0).then_inc(cleared, 1)
                pool.wait_ge(cleared, 2)
                nc.gpsimd.memset(f32(key_bias[64:65, :]), 1.0)
                nc.gpsimd.memset(f32(key_bias[96:97, :]), 1.0).then_inc(cleared, 1)

        @block.tensor
        def _(pe):
            for n in range(3):
                pe.wait_ge(raw_in[n], 16)
                if qk_bias is not None and n < 2:
                    for f in range(C):
                        for c in range(C):
                            last = nc.tensor.matmul(ps[n][:, f:f + 1], raw[n][:, c, f * P:(f + 1) * P],
                                                    vec[:, off + c:off + c + 1], start=(c == 0), stop=(c == C - 1))
                else:
                    for c in range(C):
                        last = nc.tensor.matmul(ps[n][0:1, :], vec[:, off + c:off + c + 1], raw[n][:, c, :],
                                                start=(c == 0), stop=(c == C - 1))
                last.then_inc(bias_ps, 1)

        @block.scalar
        def _(act):
            for n in range(4):
                act.wait_ge(folded, n + 1)
                nc.scalar.activation(w_hi[:, n], raw[n][:], ACT.Copy).then_inc(split, 1)

        @block.vector
        def _(dve):
            dve.wait_ge(bias_loaded, 64)
            dve.wait_ge(cleared, 3 if key_bias is not None else 1)
            done = 0
            for n in range(4):
                dve.wait_ge(raw_in[n], 16)
                if qk_bias is not None and n < 2:
                    dve.wait_ge(bias_ps, n + 1)
                    r = vec_rows[mats[n][1]][0]
                    nc.vector.tensor_tensor(qk_bias[:, n, :], ps[n][:, 0:C], vec[:, r:r + C], ALU.add)
                else:
                    if n < 3:
                        dve.wait_ge(bias_ps, n + 1)
                        nc.vector.tensor_tensor(bias_f[:, n, :], ps[n][0:1, :], bias_in[:, n, :],
                                                ALU.add).then_inc(bias_step, 1)
                    else:
                        nc.vector.tensor_copy(bias_f[:, n, :], bias_in[:, n, :]).then_inc(bias_step, 1)
                    hi, lo = ((key_bias[0:1, :], key_bias[32:33, :]) if n == 1 else
                              (bias_rows[0:1, rows_of[n], :], bias_rows[32:33, rows_of[n], :]))
                    done += 1
                    dve.wait_ge(bias_step, done)
                    nc.vector.tensor_copy(hi, bias_f[:, n, :]).then_inc(bias_step, 1)
                    done += 1
                    dve.wait_ge(bias_step, done)
                    nc.vector.tensor_tensor(lo, bias_f[:, n, :], f32(hi), ALU.subtract)
                for c in range(C):
                    if n < 3:
                        last = nc.vector.tensor_scalar(raw[n][:, c, :], raw[n][:, c, :], vcol(lnw, c), None, ALU.mult)
                if n < 3:
                    last.then_inc(folded, 1)
                else:
                    nc.vector.tensor_copy(raw[n][:], raw[n][:]).then_inc(folded, 1)
                dve.wait_ge(split, n + 1)
                nc.vector.tensor_tensor(w_lo[:, n], raw[n][:], f32(w_hi[:, n]), ALU.subtract)


def project_rows(nc, w_hi, w_lo, m, a_hi, a_lo, b, bank, C, ones, bias):
    yield nc.tensor.matmul(bank[:, :], ones[:], bias, start=True, stop=False)
    for c in range(C):
        yield nc.tensor.matmul(bank[:, :], a_hi[:, c, b, :], w_hi[:, m, c, :], start=False, stop=False)
        yield nc.tensor.matmul(bank[:, :], a_lo[:, c, b, :], w_hi[:, m, c, :], start=False, stop=False)
        yield nc.tensor.matmul(bank[:, :], a_hi[:, c, b, :], w_lo[:, m, c, :], start=False, stop=(c == C - 1))


def project_features(nc, w_hi, w_lo, m, f, a_hi, a_lo, dst, C, first):
    fs = slice(f * P, (f + 1) * P)
    for c in range(C):
        nc.tensor.matmul(dst, w_hi[:, m, c, fs], a_hi[:, c], start=(first and c == 0), stop=False)
        nc.tensor.matmul(dst, w_hi[:, m, c, fs], a_lo[:, c], start=False, stop=False)
        last = nc.tensor.matmul(dst, w_lo[:, m, c, fs], a_hi[:, c], start=False, stop=(c == C - 1))
    return last


def run(steps):
    last = None
    for last in steps:
        pass
    return last


def bodies(eng, NP, body):
    body(0, True, True, False)
    with eng.Fori(1, NP - 2) as i:
        body(i, False, True, False)
    body(NP - 2, False, False, False)
    body(NP - 1, False, False, True)


def layer0(nc, ctx, sem, sb, ps, x_d, x1_d, w_hi, w_lo, ident, ones, bias_rows, key_bias, mask_rows,
           half_gain, half_shift, mask_col, mask_hi, mask_lo, eps, neg_half, B, NP, D, C, H, DH):
    Q, K, V, O = range(4)
    BQ, BV, BO = range(3)
    HB = 2
    DV = P + 1
    DY = P + HB
    xr = sb(ctx, "xr", [P, RING, PAIR, D])
    xn = sb(ctx, "xn", [P, PAIR, D])
    xT_hi = sb(ctx, "xT_hi", [P, C, PAIR, P], F32R)
    xT_lo = sb(ctx, "xT_lo", [P, C, PAIR, P], F32R)
    k_neg = sb(ctx, "k_neg", [P, C, PAIR])
    k_exp = sb(ctx, "k_exp", [P, C, PAIR, P])
    q_max = sb(ctx, "q_max", [P, PAIR, H])
    q_exp = sb(ctx, "q_exp", [P, PAIR, D])
    qT = sb(ctx, "qT", [P, PAIR, C, P])
    k_rows = sb(ctx, "k_rows", [P, PAIR, C, P])
    v = sb(ctx, "v", [P, PAIR, C, DV])
    k_sum = sb(ctx, "k_sum", [P, PAIR, C])
    q_sum = sb(ctx, "q_sum", [P, PAIR, H])
    att = sb(ctx, "att", [P, PAIR, C, DY])
    z = sb(ctx, "z", [P, PAIR, D])
    g = sb(ctx, "g", [P, PAIR, C, P])
    th = sb(ctx, "th", [P, PAIR, C, P])
    hs = sb(ctx, "hs", [P, PAIR, C, P])
    h_hi = sb(ctx, "h_hi", [P, C, PAIR, P], F32R)
    h_lo = sb(ctx, "h_lo", [P, C, PAIR, P], F32R)
    x1 = sb(ctx, "x1", [P, PAIR, D])
    stats = sb(ctx, "stats", [P, PAIR, 6])
    stats_y = sb(ctx, "stats_y", [P, PAIR, 6])
    mv = sb(ctx, "mv", [P, PAIR, 2])
    mv_y = sb(ctx, "mv_y", [P, PAIR, 2])
    ve = sb(ctx, "ve", [P, PAIR])
    ve_y = sb(ctx, "ve_y", [P, PAIR])
    rstd = sb(ctx, "rstd", [P, PAIR])
    rstd_y = sb(ctx, "rstd_y", [P, PAIR])
    gains = sb(ctx, "gains", [P, 2, C, PAIR])
    mask_now = sb(ctx, "mask_now", [P, PAIR])
    seen = sb(ctx, "seen", [P, 1])

    s = {n: sem("l0_" + n) for n in (
        "preset", "rows_preset", "rows_in", "masks", "x_in", "stats", "var", "var_eps", "rstd", "xn", "xT_ps", "xT_hi", "xT_lo",
        "kT_ps", "k_neg", "k_exp", "q_ps", "q_max", "q_less", "q_exp", "v_ps", "v", "q_tr", "k_tr", "qT", "k_rows",
        "att_ps", "k_sum", "att", "y_ps", "q_sum", "y", "y_stats", "y_var", "y_var_eps", "y_rstd", "z", "z_ps", "gains",
        "g", "tanh", "silu", "h_hi", "h_lo", "o_ps", "x1", "stored")}

    block = ctx.enter_context(nc.Block())

    @block.sync
    def _(sp):
        sp.wait_ge(s["rows_preset"], 1)
        for r, part in ((64, mask_hi), (96, mask_lo)):
            sp.dma_start(f32(mask_rows[r:r + 1, :]).rearrange("o (b t) -> o b t", t=P), f32(part[:, 0, :]))\
                .then_inc(s["rows_in"], 16)

        def load(pair, slot):
            sp.dma_start(xr[:, slot], x_d[bass.ds(pair * PAIR, PAIR)].rearrange("b t d -> t b d")).then_inc(s["x_in"], 16)

        load(0, 0)
        load(1, 1)

        def store(prev):
            for b in range(PAIR):
                sp.wait_ge(s["x1"], seq(PAIR, prev, b + 1))
                sp.dma_start(x1_d[prev * PAIR + b], x1[:, b]).then_inc(s["stored"], 16)
            sp.wait_ge(s["stored"], seq(16 * PAIR, prev, 16 * PAIR))

        def body(i, first, more, last):
            if not first:
                store(i - 1)
            if more:
                sp.wait_ge(s["x_in"], seq(16, i, 32))
                load(i + 2, (i + 2) % RING)

        bodies(sp, NP, body)
        store(NP - 1)

    @block.gpsimd
    def _(pool):
        nc.gpsimd.memset(f32(mask_rows[:]), 1.0).then_inc(s["rows_preset"], 1)

        def inverse_root(n, var, e, to, var_eps_sem, rstd_sem, pair):
            nc.gpsimd.tensor_tensor(e[:], var[:, :, 1], eps[:], ALU.add).then_inc(var_eps_sem, 1)
            pool.wait_ge(var_eps_sem, seq(1, pair, 1))
            nc.gpsimd.tensor_tensor(to[:], e[:], neg_half[:], ALU.pow).then_inc(rstd_sem, 1)

        def end(prev):
            pool.wait_ge(s["y_var"], seq(1, prev, 1))
            inverse_root(0, mv_y, ve_y, rstd_y, s["y_var_eps"], s["y_rstd"], prev)
            nc.gpsimd.tensor_copy(gains[:, 0], half_gain[:, 0, :, bass.ds(prev * PAIR, PAIR)])
            nc.gpsimd.tensor_copy(gains[:, 1], half_shift[:, 0, :, bass.ds(prev * PAIR, PAIR)]).then_inc(s["gains"], 1)

        def norm(pair):
            pool.wait_ge(s["var"], seq(1, pair, 1))
            inverse_root(1, mv, ve, rstd, s["var_eps"], s["rstd"], pair)

        def low_parts(prev):
            for b in range(PAIR):
                pool.wait_ge(s["h_hi"], seq(PAIR, prev, b + 1))
                nc.gpsimd.tensor_tensor(h_lo[:, :, b, :], hs[:, b], f32(h_hi[:, :, b, :]),
                                        ALU.subtract).then_inc(s["h_lo"], 1)

        norm(0)

        def body(i, first, more, last):
            if not first:
                end(i - 1)
            if not last:
                norm(i + 1)
            if not first:
                low_parts(i - 1)

        bodies(pool, NP, body)
        end(NP - 1)
        low_parts(NP - 1)

    @block.vector
    def _(dve):
        nc.vector.memset(v[:], 1.0)
        nc.vector.memset(att[:], 0.0).then_inc(s["preset"], 1)
        dve.wait_ge(s["preset"], 1)
        nc.vector.memset(att[0:64, :, :, P:P + 1], 1.0)
        nc.vector.memset(att[64:128, :, :, P + 1:P + 2], 1.0).then_inc(s["preset"], 1)

        def row_stats(pair, slot):
            dve.wait_ge(s["x_in"], seq(16, pair, 16) if not isinstance(pair, int) or pair > 0 else 32)
            for b in range(PAIR):
                nc.vector.bn_stats(stats[:, b], xr[:, slot, b]).then_inc(s["stats"], 1)
            dve.wait_ge(s["stats"], seq(PAIR, pair, PAIR))
            nc.vector.tensor_copy(seen[:], eps[:, 0:1])
            for b in range(PAIR):
                last = nc.vector.bn_aggr(mv[:, b], stats[:, b])
            last.then_inc(s["var"], 1)

        def norm(pair, slot):
            dve.wait_ge(s["rstd"], seq(1, pair, 1))
            for b in range(PAIR):
                nc.vector.tensor_scalar(xn[:, b], xr[:, slot, b], mv[:, b, 0:1], rstd[:, b:b + 1], ALU.subtract,
                                        ALU.mult).then_inc(s["xn"], 1)

        def x_low(pair, banks):
            for b in range(PAIR):
                dve.wait_ge(s["xT_hi"], seq(PAIR, pair, b + 1))
                nc.vector.tensor_tensor(xT_lo[:, :, b, :], banks[b][:, :].rearrange("p (c t) -> p c t", c=C),
                                        f32(xT_hi[:, :, b, :]), ALU.subtract).then_inc(s["xT_lo"], 1)

        def end_norm(prev):
            dve.wait_ge(s["y_rstd"], seq(1, prev, 1))
            for b in range(PAIR):
                nc.vector.tensor_scalar(z[:, b], z[:, b], mv_y[:, b, 0:1], rstd_y[:, b:b + 1], ALU.subtract,
                                        ALU.mult).then_inc(s["z"], 1)

        def end_gate(prev):
            dve.wait_ge(s["gains"], seq(1, prev, 1))
            for b in range(PAIR):
                dve.wait_ge(s["z_ps"], seq(PAIR, prev, b + 1))
                for c in range(C):
                    last = nc.vector.tensor_scalar(g[:, b, c, :], ps[6 + b][:, c * P:(c + 1) * P],
                                                   gains[:, 0, c, b:b + 1], gains[:, 1, c, b:b + 1], ALU.mult, ALU.add)
                last.then_inc(s["g"], 1)
            for b in range(PAIR):
                dve.wait_ge(s["tanh"], seq(PAIR, prev, b + 1))
                nc.vector.scalar_tensor_tensor(hs[:, b], th[:, b], 1.0, g[:, b], ALU.add,
                                               ALU.mult).then_inc(s["silu"], 1)

        def end_add(prev, slot):
            if isinstance(prev, int) and prev > 0:
                dve.wait_ge(s["stored"], seq(16 * PAIR, prev - 1, 16 * PAIR))
            for b in range(PAIR):
                dve.wait_ge(s["o_ps"], seq(PAIR, prev, b + 1))
                nc.vector.tensor_tensor(x1[:, b], ps[b][:, :], xr[:, slot, b], ALU.add).then_inc(s["x1"], 1)

        def key_maxima(i):
            for j in range(2):
                dve.wait_ge(s["kT_ps"], seq(2, i, j + 1))
                nc.vector.tensor_reduce(k_neg[:, 2 * j:2 * j + 2, :],
                                        ps[j][:, :].rearrange("p (c b t) -> p c b t", c=2, b=PAIR), AX_X, ALU.max,
                                        negate=True).then_inc(s["k_neg"], 1)

        def query_shift(i, b):
            q3 = ps[2 + b][:, :].rearrange("p (h d) -> p h d", h=H)
            dve.wait_ge(s["q_ps"], seq(PAIR, i, b + 1))
            nc.vector.reduce_max(q_max[:, b], q3, AX_X).then_inc(s["q_max"], 1)
            dve.wait_ge(s["q_max"], seq(PAIR, i, b + 1))
            nc.vector.tensor_tensor(q_exp[:, b].rearrange("p (h d) -> p h d", h=H), q3,
                                    q_max[:, b].unsqueeze(2).broadcast_to([P, H, DH]),
                                    ALU.subtract).then_inc(s["q_less"], 1)

        def attend(i):
            for b in range(PAIR):
                dve.wait_ge(s["k_tr"], seq(PAIR, i, b + 1))
                nc.vector.tensor_copy(k_rows[:, b], ps[(7, 5)[b]][:, :].rearrange("p (c t) -> p c t", c=C))\
                    .then_inc(s["k_rows"], 1)

        def weights_of(i):
            for b in range(PAIR):
                banks = ((0, 1), (6, 7))[b]
                dve.wait_ge(s["att_ps"], seq(PAIR, i, b + 1))
                for j in range(2):
                    a = ps[banks[j]][:, 0:2 * DV].rearrange("p (c d) -> p c d", c=2)
                    last = nc.vector.reciprocal(k_sum[:, b, 2 * j:2 * j + 2], a[:, :, P])
                last.then_inc(s["k_sum"], 1)
                dve.wait_ge(s["k_sum"], seq(PAIR, i, b + 1))
                for j in range(2):
                    a = ps[banks[j]][:, 0:2 * DV].rearrange("p (c d) -> p c d", c=2)
                    for r in range(2):
                        rows, cols = slice(64 * r, 64 * r + 64), slice(64 * r, 64 * r + 64)
                        last = nc.vector.tensor_tensor(
                            att[rows, b, 2 * j:2 * j + 2, cols], a[rows, :, cols],
                            k_sum[rows, b, 2 * j:2 * j + 2].unsqueeze(2).broadcast_to([64, 2, 64]), ALU.mult)
                last.then_inc(s["att"], 1)

        def outputs(i):
            for b in range(PAIR):
                banks = ((4, 5), (2, 3))[b]
                dve.wait_ge(s["y_ps"], seq(PAIR, i, b + 1))
                for j in range(2):
                    a = ps[banks[j]][:, 0:2 * DY].rearrange("p (c d) -> p c d", c=2)
                    last = nc.vector.reciprocal(q_sum[:, b, 4 * j:4 * j + 4].rearrange("p (c r) -> p c r", c=2),
                                                a[:, :, P:P + 2])
                last.then_inc(s["q_sum"], 1)
                dve.wait_ge(s["q_sum"], seq(PAIR, i, b + 1))
                for j in range(2):
                    a = ps[banks[j]][:, 0:2 * DY].rearrange("p (c d) -> p c d", c=2)
                    for c in range(2):
                        last = nc.vector.tensor_tensor(
                            z[:, b, (2 * j + c) * P:(2 * j + c + 1) * P].rearrange("p (r d) -> p r d", r=2),
                            a[:, c, 0:P].rearrange("p (r d) -> p r d", r=2),
                            q_sum[:, b, 4 * j + 2 * c:4 * j + 2 * c + 2].unsqueeze(2).broadcast_to([P, 2, DH]),
                            ALU.mult)
                last.then_inc(s["y"], 1)
                dve.wait_ge(s["y"], seq(PAIR, i, b + 1))
                nc.vector.bn_stats(stats_y[:, b], z[:, b]).then_inc(s["y_stats"], 1)
            dve.wait_ge(s["y_stats"], seq(PAIR, i, PAIR))
            nc.vector.tensor_copy(seen[:], eps[:, 0:1])
            for b in range(PAIR):
                last = nc.vector.bn_aggr(mv_y[:, b], stats_y[:, b])
            last.then_inc(s["y_var"], 1)

        row_stats(0, 0)
        norm(0, 0)
        x_low(0, (ps[2], ps[3]))

        def body(i, first, more, last):
            if not first:
                end_norm(i - 1)
            key_maxima(i)
            if not last:
                row_stats(i + 1, (i + 1) % RING)
            query_shift(i, 0)
            query_shift(i, 1)
            if not first:
                end_gate(i - 1)
            if not last:
                norm(i + 1, (i + 1) % RING)
            if not first:
                end_add(i - 1, (i - 1) % RING)
            attend(i)
            if not last:
                x_low(i + 1, (ps[2], ps[3]))
            weights_of(i)
            outputs(i)

        bodies(dve, NP, body)
        end_norm(NP - 1)
        end_gate(NP - 1)
        end_add(NP - 1, (NP - 1) % RING)

    @block.scalar
    def _(act):
        def x_high(pair, banks):
            for b in range(PAIR):
                act.wait_ge(s["xT_ps"], seq(PAIR, pair, b + 1))
                nc.scalar.activation(xT_hi[:, :, b, :], banks[b][:, :].rearrange("p (c t) -> p c t", c=C),
                                     ACT.Copy).then_inc(s["xT_hi"], 1)

        def key_exps(i):
            for j in range(2):
                act.wait_ge(s["k_neg"], seq(2, i, j + 1))
                for c in (2 * j, 2 * j + 1):
                    for b in range(PAIR):
                        at = (c - 2 * j) * PAIR * P + b * P
                        last = nc.scalar.activation(k_exp[:, c, b, :], ps[j][:, at:at + P], ACT.Exp,
                                                    bias=k_neg[:, c, b:b + 1])
                last.then_inc(s["k_exp"], 1)

        def query_exps(i):
            for b in range(PAIR):
                act.wait_ge(s["q_less"], seq(PAIR, i, b + 1))
                nc.scalar.activation(q_exp[:, b], q_exp[:, b], ACT.Exp).then_inc(s["q_exp"], 1)

        def tanhs(prev):
            for b in range(PAIR):
                act.wait_ge(s["g"], seq(PAIR, prev, b + 1))
                nc.scalar.activation(th[:, b], g[:, b], ACT.Tanh).then_inc(s["tanh"], 1)

        def h_high(prev):
            for b in range(PAIR):
                act.wait_ge(s["silu"], seq(PAIR, prev, b + 1))
                nc.scalar.activation(h_hi[:, :, b, :], hs[:, b], ACT.Copy).then_inc(s["h_hi"], 1)

        def values(i, b):
            act.wait_ge(s["v_ps"], seq(PAIR, i, b + 1))
            nc.scalar.activation(v[:, b, :, 0:P], ps[4 + b][:, :].rearrange("p (c d) -> p c d", c=C), ACT.Copy,
                                 scale=mask_now[:, b:b + 1]).then_inc(s["v"], 1)

        def query_T(i):
            for b in range(PAIR):
                act.wait_ge(s["q_tr"], seq(PAIR, i, b + 1))
                nc.scalar.activation(qT[:, b], ps[(6, 4)[b]][:, :].rearrange("p (c t) -> p c t", c=C),
                                     ACT.Copy).then_inc(s["qT"], 1)

        act.wait_ge(s["preset"], 2)
        x_high(0, (ps[2], ps[3]))

        def body(i, first, more, last):
            nc.scalar.activation(mask_now[:], mask_col[:, 0, bass.ds(i * PAIR, PAIR)], ACT.Copy)\
                .then_inc(s["masks"], 1)
            key_exps(i)
            query_exps(i)
            if not first:
                tanhs(i - 1)
            act.wait_ge(s["masks"], seq(1, i, 1))
            values(i, 0)
            if not first:
                h_high(i - 1)
            values(i, 1)
            query_T(i)
            if not last:
                x_high(i + 1, (ps[2], ps[3]))

        bodies(act, NP, body)
        tanhs(NP - 1)
        h_high(NP - 1)

    @block.tensor
    def _(pe):
        pe.wait_ge(s["preset"], 2)
        pe.wait_ge(s["rows_in"], 32)

        def x_transposed(pair):
            for b in range(PAIR):
                pe.wait_ge(s["xn"], seq(PAIR, pair, b + 1))
                for c in range(C):
                    last = nc.tensor.transpose(ps[2 + b][:, c * P:(c + 1) * P], xn[:, b, c * P:(c + 1) * P], ident[:])
                last.then_inc(s["xT_ps"], 1)

        def z_transposed(prev):
            for b in range(PAIR):
                pe.wait_ge(s["z"], seq(PAIR, prev, b + 1))
                for c in range(C):
                    last = nc.tensor.transpose(ps[6 + b][:, c * P:(c + 1) * P], z[:, b, c * P:(c + 1) * P], ident[:])
                last.then_inc(s["z_ps"], 1)

        def out_rows(prev):
            for b in range(PAIR):
                pe.wait_ge(s["h_lo"], seq(PAIR, prev, b + 1))
                run(project_rows(nc, w_hi, w_lo, O, h_hi, h_lo, b, ps[b], C, ones,
                                 bias_rows[:, BO, :])).then_inc(s["o_ps"], 1)

        x_transposed(0)

        def body(i, first, more, last):
            pe.wait_ge(s["xT_lo"], seq(PAIR, i, PAIR))
            for f in range(C):
                dst = ps[f // 2][:, (f % 2) * PAIR * P:(f % 2 + 1) * PAIR * P]
                nc.tensor.matmul(dst, key_bias[:, f * P:(f + 1) * P], mask_rows[:, bass.ds(i * (PAIR * P), PAIR * P)],
                                 start=True, stop=False)
                done = project_features(nc, w_hi, w_lo, K, f, xT_hi, xT_lo, dst, C, False)
                if f % 2:
                    done.then_inc(s["kT_ps"], 1)
            if not first:
                pe.wait_ge(s["y"], seq(PAIR, i - 1, PAIR))
            for b in range(PAIR):
                run(project_rows(nc, w_hi, w_lo, Q, xT_hi, xT_lo, b, ps[2 + b], C, ones,
                                 bias_rows[:, BQ, :])).then_inc(s["q_ps"], 1)
            if not first:
                z_transposed(i - 1)
            for b in range(PAIR):
                run(project_rows(nc, w_hi, w_lo, V, xT_hi, xT_lo, b, ps[4 + b], C, ones,
                                 bias_rows[:, BV, :])).then_inc(s["v_ps"], 1)
            pe.wait_ge(s["k_exp"], seq(2, i, 2))
            if not first:
                out_rows(i - 1)
            for b in range(PAIR):
                pe.wait_ge(s["q_exp"], seq(PAIR, i, b + 1))
                pe.wait_ge(s["v"], seq(PAIR, i, b + 1 if b == 0 else PAIR))
                for c in range(C):
                    done = nc.tensor.transpose(ps[(6, 4)[b]][:, c * P:(c + 1) * P], q_exp[:, b, c * P:(c + 1) * P],
                                               ident[:])
                done.then_inc(s["q_tr"], 1)
                for c in range(C):
                    done = nc.tensor.transpose(ps[(7, 5)[b]][:, c * P:(c + 1) * P], k_exp[:, c, b, :], ident[:])
                done.then_inc(s["k_tr"], 1)
            if not last:
                x_transposed(i + 1)
            for b in range(PAIR):
                banks = ((0, 1), (6, 7))[b]
                if b == 0 and not first:
                    pe.wait_ge(s["x1"], seq(PAIR, i - 1, PAIR))
                pe.wait_ge(s["k_rows"], seq(PAIR, i, b + 1))
                pe.wait_ge(s["qT"], seq(PAIR, i, b + 1))
                for c in range(C):
                    done = nc.tensor.matmul(ps[banks[c // 2]][:, (c % 2) * DV:(c % 2 + 1) * DV], k_rows[:, b, c, :],
                                            v[:, b, c, :], start=True, stop=True)
                done.then_inc(s["att_ps"], 1)
            if not last:
                pe.wait_ge(s["xT_lo"], seq(PAIR, i + 1, PAIR))
            for b in range(PAIR):
                banks = ((4, 5), (2, 3))[b]
                pe.wait_ge(s["att"], seq(PAIR, i, b + 1))
                for c in range(C):
                    done = nc.tensor.matmul(ps[banks[c // 2]][:, (c % 2) * DY:(c % 2 + 1) * DY], qT[:, b, c, :],
                                            att[:, b, c, :], start=True, stop=True)
                done.then_inc(s["y_ps"], 1)

        bodies(pe, NP, body)
        z_transposed(NP - 1)
        out_rows(NP - 1)


def layer1(nc, ctx, sem, sb, ps, x1_d, out, w_hi, w_lo, ident, ones, bias_rows, qk_bias,
           half_gain, half_shift, mask_col, mask_d, eps, neg_half, B, NP, D, C, HC, H, DH):
    Q, K, V, O = range(4)
    BV, BO = 1, 2
    DV = DH + 1
    HB = 512 // P
    HY = H // 2
    xr = sb(ctx, "xr1", [P, RING, PAIR, D])
    xn = sb(ctx, "xn1", [P, PAIR, D])
    xT_hi = sb(ctx, "xT_hi1", [P, C, PAIR, P], F32R)
    xT_lo = sb(ctx, "xT_lo1", [P, C, PAIR, P], F32R)
    parts = sb(ctx, "parts", [P, 4, C, PAIR, P], F32R)
    Q_LO, Q_HI, K_HI, K_LO = range(4)
    HI, LO = (Q_HI, K_HI), (Q_LO, K_LO)
    stack = sb(ctx, "stack", [P, 2, HC, C, PAIR, P], F32R)
    v = sb(ctx, "v1", [P, PAIR, H, DV])
    top = sb(ctx, "top", [P, PAIR, H])
    top_T = sb(ctx, "top_T", [H, PAIR, P], F32R)
    prob = sb(ctx, "prob", [P, PAIR, H, P])
    p_sum = sb(ctx, "p_sum", [P, PAIR, H])
    z = sb(ctx, "z1", [P, PAIR, D])
    g = sb(ctx, "g1", [P, PAIR, C, P])
    th = sb(ctx, "th1", [P, PAIR, C, P])
    hs = sb(ctx, "hs1", [P, PAIR, C, P])
    h_hi = sb(ctx, "h_hi1", [P, C, PAIR, P], F32R)
    h_lo = sb(ctx, "h_lo1", [P, C, PAIR, P], F32R)
    y_out = sb(ctx, "y_out", [P, PAIR, D])
    stats = sb(ctx, "stats1", [P, PAIR, 6])
    stats_y = sb(ctx, "stats_y1", [P, PAIR, 6])
    mv = sb(ctx, "mv1", [P, PAIR, 2])
    mv_y = sb(ctx, "mv_y1", [P, PAIR, 2])
    ve = sb(ctx, "ve1", [P, PAIR])
    ve_y = sb(ctx, "ve_y1", [P, PAIR])
    rstd = sb(ctx, "rstd1", [P, PAIR])
    rstd_y = sb(ctx, "rstd_y1", [P, PAIR])
    gains = sb(ctx, "gains1", [P, 2, C, PAIR])
    mask_now = sb(ctx, "mask_now1", [P, PAIR])
    seen = sb(ctx, "seen1", [P, 1])

    s = {n: sem("l1_" + n) for n in (
        "preset", "x_in", "stats", "var", "var_eps", "rstd", "xn", "xT_ps", "xT_hi", "xT_lo", "masks",
        "qk_ps", "qk_hi", "qk_lo", "stack", "v_ps", "v", "s_ps", "top", "top_ps", "top_T",
        "shift0", "shift1", "w_ps", "prob", "y_ps", "p_sum", "y", "y_stats", "y_var", "y_var_eps", "y_rstd", "z",
        "z_ps", "gains", "g", "tanh", "silu", "h_hi", "h_lo", "o_ps", "out", "stored")}
    STACK_DMAS = HC * 3 + 1
    QK_BANKS = ((2, 3), (0, 1))
    W_BANKS = (4, 5, 6, 7)
    Y_BANKS = ((4, 5), (6, 7))
    V_BANKS = (0, 6)
    S_BANKS = (2, 3, 0, 1)
    Z_BANKS = (4, 5)
    O_BANKS = (4, 5)
    X_BANKS = (7, 6)
    T_BANKS = (7, 6)

    block = ctx.enter_context(nc.Block())

    @block.sync
    def _(sp):
        sp.wait_ge(s["preset"], 2)

        def load(pair, slot):
            sp.dma_start(xr[:, slot], x1_d[bass.ds(pair * PAIR, PAIR)].rearrange("b t d -> t b d")).then_inc(s["x_in"], 16)

        load(0, 0)
        load(1, 1)

        def restack(i, first):
            if not first:
                sp.wait_ge(s["w_ps"], seq(PAIR * C, i - 1, PAIR * C))
            sp.dma_start(f32(stack[ROW_MASK:ROW_MASK + 2, 1]).rearrange("r a c b t -> r (a c) (b t)"),
                         mask_d[:, bass.ds(i * PAIR, PAIR)].rearrange("r b t -> r (b t)").unsqueeze(1)
                         .broadcast_to([2, H, PAIR * P])).then_inc(s["stack"], 16)
            sp.wait_ge(s["qk_lo"], seq(2 * C, i, 2 * C))
            for a in range(HC):
                rows = slice(DH * a, DH * a + DH)
                for r, (q, k) in enumerate(((Q_HI, K_HI), (Q_LO, K_HI), (Q_HI, K_LO))):
                    sp.dma_start(f32(stack[DH * r:DH * r + DH, :, a]),
                                 f32(parts[rows, q:k + 1:k - q])).then_inc(s["stack"], 16)

        def shift(i, b):
            sp.wait_ge(s["top_T"], seq(PAIR, i, b + 1))
            sp.dma_start(f32(stack[ROW_SHIFT:ROW_SHIFT + 1, 0, :, :, b, :]).rearrange("o a c t -> o (a c) t"),
                         f32(top_T[:, b, :])).then_inc(s[f"shift{b}"], 16)

        def store(prev, b):
            sp.wait_ge(s["out"], seq(PAIR, prev + 1, b + 1))
            sp.dma_start(out[prev * PAIR + b], y_out[:, b]).then_inc(s["stored"], 16)

        def body(i, first, more, last):
            restack(i, first)
            if not first:
                store(i - 1, 0)
            shift(i, 0)
            shift(i, 1)
            if not first:
                store(i - 1, 1)
                sp.wait_ge(s["stored"], seq(16 * PAIR, i - 1, 16 * PAIR))
            if more:
                sp.wait_ge(s["x_in"], seq(16, i, 32))
                load(i + 2, (i + 2) % RING)

        bodies(sp, NP, body)
        store(NP - 1, 0)
        store(NP - 1, 1)
        sp.wait_ge(s["stored"], seq(16 * PAIR, NP - 1, 16 * PAIR))

    @block.gpsimd
    def _(pool):
        nc.gpsimd.memset(f32(stack[ROW_MASK:ROW_MASK + 3]), 1.0).then_inc(s["preset"], 1)

        def end_rstd(prev, b):
            pool.wait_ge(s["y_var"], seq(PAIR, prev, b + 1))
            nc.gpsimd.tensor_tensor(ve_y[:, b:b + 1], mv_y[:, b, 1:2], eps[:, 0:1], ALU.add).then_inc(s["y_var_eps"], 1)
            pool.wait_ge(s["y_var_eps"], seq(PAIR, prev, b + 1))
            nc.gpsimd.tensor_tensor(rstd_y[:, b:b + 1], ve_y[:, b:b + 1], neg_half[:, 0:1],
                                    ALU.pow).then_inc(s["y_rstd"], 1)

        def end_gains(prev):
            nc.gpsimd.tensor_copy(gains[:, 0], half_gain[:, 1, :, bass.ds(prev * PAIR, PAIR)])
            nc.gpsimd.tensor_copy(gains[:, 1], half_shift[:, 1, :, bass.ds(prev * PAIR, PAIR)]).then_inc(s["gains"], 1)

        def norm(pair):
            pool.wait_ge(s["var"], seq(1, pair, 1))
            nc.gpsimd.tensor_tensor(ve[:], mv[:, :, 1], eps[:], ALU.add).then_inc(s["var_eps"], 1)
            pool.wait_ge(s["var_eps"], seq(1, pair, 1))
            nc.gpsimd.tensor_tensor(rstd[:], ve[:], neg_half[:], ALU.pow).then_inc(s["rstd"], 1)

        def low_part(prev, b):
            pool.wait_ge(s["h_hi"], seq(PAIR, prev, b + 1))
            nc.gpsimd.tensor_tensor(h_lo[:, :, b, :], hs[:, b], f32(h_hi[:, :, b, :]), ALU.subtract).then_inc(s["h_lo"], 1)

        norm(0)

        def body(i, first, more, last):
            if not last:
                norm(i + 1)
            if not first:
                end_rstd(i - 1, 0)
                end_gains(i - 1)
                end_rstd(i - 1, 1)
                low_part(i - 1, 0)
                low_part(i - 1, 1)

        bodies(pool, NP, body)
        end_rstd(NP - 1, 0)
        end_gains(NP - 1)
        end_rstd(NP - 1, 1)
        low_part(NP - 1, 0)
        low_part(NP - 1, 1)

    @block.vector
    def _(dve):
        nc.vector.memset(v[:], 1.0).then_inc(s["preset"], 1)
        nc.vector.memset(seen[:], 0.0).then_inc(s["out"], PAIR)

        def row_stats(pair, slot):
            dve.wait_ge(s["x_in"], seq(16, pair, 16) if not isinstance(pair, int) or pair > 0 else 32)
            for b in range(PAIR):
                nc.vector.bn_stats(stats[:, b], xr[:, slot, b]).then_inc(s["stats"], 1)
            dve.wait_ge(s["stats"], seq(PAIR, pair, PAIR))
            nc.vector.tensor_copy(seen[:], eps[:, 0:1])
            for b in range(PAIR):
                last = nc.vector.bn_aggr(mv[:, b], stats[:, b])
            last.then_inc(s["var"], 1)

        def norm(pair, slot):
            dve.wait_ge(s["rstd"], seq(1, pair, 1))
            for b in range(PAIR):
                nc.vector.tensor_scalar(xn[:, b], xr[:, slot, b], mv[:, b, 0:1], rstd[:, b:b + 1], ALU.subtract,
                                        ALU.mult).then_inc(s["xn"], 1)

        def x_low(pair, b):
            dve.wait_ge(s["xT_hi"], seq(PAIR, pair, b + 1))
            nc.vector.tensor_tensor(xT_lo[:, :, b, :], ps[X_BANKS[b]][:, :].rearrange("p (c t) -> p c t", c=C),
                                    f32(xT_hi[:, :, b, :]), ALU.subtract).then_inc(s["xT_lo"], 1)

        def qk_low(i, n):
            for c in range(C):
                if c % 2 == 0:
                    dve.wait_ge(s["qk_hi"], seq(2 * C, i, (1 - n) * C + c + 2))
                at = (c % 2) * PAIR * P
                nc.vector.scalar_tensor_tensor(
                    parts[:, LO[n], c].rearrange("p b t -> p (b t)"), ps[QK_BANKS[n][c // 2]][:, at:at + PAIR * P],
                    qk_bias[:, n, c:c + 1], f32(parts[:, HI[n], c]).rearrange("p b t -> p (b t)"), ALU.add,
                    ALU.subtract).then_inc(s["qk_lo"], 1)

        def maxima(i, b):
            for j in range(C):
                dve.wait_ge(s["s_ps"], seq(PAIR * C, i, b * C + j + 1))
                nc.vector.tensor_reduce(top[:, b, :].rearrange("p (a c) -> p a c", c=C)[:, :, j],
                                        ps[S_BANKS[j]][:, :].rearrange("p (h t) -> p h t", h=HB), AX_X, ALU.max,
                                        negate=True).then_inc(s["top"], 1)

        def end_outputs(prev, b):
            banks = Y_BANKS[b]
            dve.wait_ge(s["y_ps"], seq(PAIR, prev, b + 1))
            for j in range(2):
                a = ps[banks[j]][:, 0:HY * DV].rearrange("p (h d) -> p h d", h=HY)
                last = nc.vector.reciprocal(p_sum[:, b, HY * j:HY * j + HY], a[:, :, DH])
            last.then_inc(s["p_sum"], 1)
            dve.wait_ge(s["p_sum"], seq(PAIR, prev, b + 1))
            for j in range(2):
                a = ps[banks[j]][:, 0:HY * DV].rearrange("p (h d) -> p h d", h=HY)
                last = nc.vector.tensor_tensor(
                    z[:, b, HY * DH * j:HY * DH * (j + 1)].rearrange("p (h d) -> p h d", h=HY), a[:, :, 0:DH],
                    p_sum[:, b, HY * j:HY * j + HY].unsqueeze(2).broadcast_to([P, HY, DH]), ALU.mult)
            last.then_inc(s["y"], 1)
            dve.wait_ge(s["y"], seq(PAIR, prev, b + 1))
            nc.vector.bn_stats(stats_y[:, b], z[:, b]).then_inc(s["y_stats"], 1)
            dve.wait_ge(s["y_stats"], seq(PAIR, prev, b + 1))
            nc.vector.tensor_copy(seen[:], eps[:, 0:1])
            nc.vector.bn_aggr(mv_y[:, b], stats_y[:, b]).then_inc(s["y_var"], 1)

        def end_norm(prev, b):
            dve.wait_ge(s["y_rstd"], seq(PAIR, prev, b + 1))
            nc.vector.tensor_scalar(z[:, b], z[:, b], mv_y[:, b, 0:1], rstd_y[:, b:b + 1], ALU.subtract,
                                    ALU.mult).then_inc(s["z"], 1)

        def end_gate(prev, b):
            if b == 0:
                dve.wait_ge(s["gains"], seq(1, prev, 1))
            dve.wait_ge(s["z_ps"], seq(PAIR, prev, b + 1))
            for c in range(C):
                last = nc.vector.tensor_scalar(g[:, b, c, :], ps[Z_BANKS[b]][:, c * P:(c + 1) * P],
                                               gains[:, 0, c, b:b + 1], gains[:, 1, c, b:b + 1], ALU.mult, ALU.add)
            last.then_inc(s["g"], 1)

        def end_silu(prev, b):
            dve.wait_ge(s["tanh"], seq(PAIR, prev, b + 1))
            nc.vector.scalar_tensor_tensor(hs[:, b], th[:, b], 1.0, g[:, b], ALU.add, ALU.mult).then_inc(s["silu"], 1)

        def end_add(prev, slot, b):
            if isinstance(prev, int) and prev > 0:
                dve.wait_ge(s["stored"], seq(16 * PAIR, prev - 1, 16 * PAIR))
            dve.wait_ge(s["o_ps"], seq(PAIR, prev, b + 1))
            nc.vector.tensor_tensor(y_out[:, b], ps[O_BANKS[b]][:, :], xr[:, slot, b], ALU.add).then_inc(s["out"], 1)

        row_stats(0, 0)
        norm(0, 0)
        x_low(0, 0)
        x_low(0, 1)

        def body(i, first, more, last):
            qk_low(i, 1)
            if not last:
                row_stats(i + 1, (i + 1) % RING)
            qk_low(i, 0)
            if not last:
                norm(i + 1, (i + 1) % RING)
            if not first:
                for b in range(PAIR):
                    end_outputs(i - 1, b)
                    end_norm(i - 1, b)
                end_gate(i - 1, 0)
                end_gate(i - 1, 1)
                end_silu(i - 1, 0)
            maxima(i, 0)
            if not first:
                end_silu(i - 1, 1)
            maxima(i, 1)
            if not last:
                x_low(i + 1, 0)
                x_low(i + 1, 1)
            if not first:
                end_add(i - 1, (i - 1) % RING, 0)
                end_add(i - 1, (i - 1) % RING, 1)

        bodies(dve, NP, body)
        for b in range(PAIR):
            end_outputs(NP - 1, b)
            end_norm(NP - 1, b)
        for b in range(PAIR):
            end_gate(NP - 1, b)
        for b in range(PAIR):
            end_silu(NP - 1, b)
        for b in range(PAIR):
            end_add(NP - 1, (NP - 1) % RING, b)

    @block.scalar
    def _(act):
        def x_high(pair, b):
            act.wait_ge(s["xT_ps"], seq(PAIR, pair, b + 1))
            nc.scalar.activation(xT_hi[:, :, b, :], ps[X_BANKS[b]][:, :].rearrange("p (c t) -> p c t", c=C),
                                 ACT.Copy).then_inc(s["xT_hi"], 1)

        def qk_high(i, n, chunks):
            for c in chunks:
                if c % 2 == 0:
                    act.wait_ge(s["qk_ps"], seq(C, i, (1 - n) * 2 + c // 2 + 1))
                at = (c % 2) * PAIR * P
                nc.scalar.activation(parts[:, HI[n], c].rearrange("p b t -> p (b t)"),
                                     ps[QK_BANKS[n][c // 2]][:, at:at + PAIR * P], ACT.Identity,
                                     bias=qk_bias[:, n, c:c + 1]).then_inc(s["qk_hi"], 1)

        def exps(prev, b):
            for j in range(C):
                act.wait_ge(s["w_ps"], seq(PAIR * C, prev, b * C + j + 1))
                nc.scalar.activation(prob[:, b, HB * j:HB * j + HB, :],
                                     ps[W_BANKS[j]][:, :].rearrange("p (h t) -> p h t", h=HB),
                                     ACT.Exp).then_inc(s["prob"], 1)

        def values(i, b):
            act.wait_ge(s["v_ps"], seq(PAIR, i, b + 1))
            nc.scalar.activation(v[:, b, :, 0:DH], ps[V_BANKS[b]][:, :].rearrange("p (h d) -> p h d", h=H), ACT.Copy,
                                 scale=mask_now[:, b:b + 1]).then_inc(s["v"], 1)

        def tanh(prev, b):
            act.wait_ge(s["g"], seq(PAIR, prev, b + 1))
            nc.scalar.activation(th[:, b], g[:, b], ACT.Tanh).then_inc(s["tanh"], 1)

        def h_high(prev, b):
            act.wait_ge(s["silu"], seq(PAIR, prev, b + 1))
            nc.scalar.activation(h_hi[:, :, b, :], hs[:, b], ACT.Copy).then_inc(s["h_hi"], 1)

        def shift_out(i, b):
            act.wait_ge(s["top_ps"], seq(PAIR, i, b + 1))
            nc.scalar.activation(top_T[:, b, :], ps[T_BANKS[b]][0:H, 0:P], ACT.Copy).then_inc(s["top_T"], 1)

        act.wait_ge(s["preset"], 2)
        x_high(0, 0)
        x_high(0, 1)

        def body(i, first, more, last):
            nc.scalar.activation(mask_now[:], mask_col[:, 1, bass.ds(i * PAIR, PAIR)], ACT.Copy).then_inc(s["masks"], 1)
            qk_high(i, 1, (0, 1))
            if not first:
                exps(i - 1, 0)
            qk_high(i, 1, (2, 3))
            if not first:
                exps(i - 1, 1)
            qk_high(i, 0, range(C))
            act.wait_ge(s["masks"], seq(1, i, 1))
            values(i, 0)
            if not first:
                tanh(i - 1, 0)
                tanh(i - 1, 1)
                h_high(i - 1, 0)
                h_high(i - 1, 1)
            values(i, 1)
            if not last:
                x_high(i + 1, 0)
                x_high(i + 1, 1)
            shift_out(i, 0)
            shift_out(i, 1)

        bodies(act, NP, body)
        exps(NP - 1, 0)
        exps(NP - 1, 1)
        for b in range(PAIR):
            tanh(NP - 1, b)
        for b in range(PAIR):
            h_high(NP - 1, b)

    @block.tensor
    def _(pe):
        pe.wait_ge(s["preset"], 2)

        def x_transposed(pair, b):
            pe.wait_ge(s["xn"], seq(PAIR, pair, b + 1))
            for c in range(C):
                last = nc.tensor.transpose(ps[X_BANKS[b]][:, c * P:(c + 1) * P], xn[:, b, c * P:(c + 1) * P], ident[:])
            last.then_inc(s["xT_ps"], 1)

        def z_transposed(prev, b):
            pe.wait_ge(s["z"], seq(PAIR, prev, b + 1))
            for c in range(C):
                last = nc.tensor.transpose(ps[Z_BANKS[b]][:, c * P:(c + 1) * P], z[:, b, c * P:(c + 1) * P], ident[:])
            last.then_inc(s["z_ps"], 1)

        def out_rows(prev, b):
            pe.wait_ge(s["h_lo"], seq(PAIR, prev, b + 1))
            run(project_rows(nc, w_hi, w_lo, O, h_hi, h_lo, b, ps[O_BANKS[b]], C, ones,
                             bias_rows[:, BO, :])).then_inc(s["o_ps"], 1)

        def projected(i, n, chunks):
            for f in chunks:
                dst = ps[QK_BANKS[n][f // 2]][:, (f % 2) * PAIR * P:(f % 2 + 1) * PAIR * P]
                done = project_features(nc, w_hi, w_lo, n, f, xT_hi, xT_lo, dst, C, True)
                if f % 2:
                    done.then_inc(s["qk_ps"], 1)

        def value_rows(i, b):
            run(project_rows(nc, w_hi, w_lo, V, xT_hi, xT_lo, b, ps[V_BANKS[b]], C, ones,
                             bias_rows[:, BV, :])).then_inc(s["v_ps"], 1)

        def weight_scores(prev, b):
            pe.wait_ge(s[f"shift{b}"], seq(16, prev, 16))
            for j in range(C):
                if b == 0 and j < 2:
                    pe.wait_ge(s["out"], seq(PAIR, prev, j + 1))
                if b == 0 and j == 2:
                    pe.wait_ge(s["top_T"], seq(PAIR, prev, PAIR))
                if b == 1:
                    pe.wait_ge(s["prob"], seq(PAIR * C, prev, j + 1))
                for a in range(HC):
                    last = nc.tensor.matmul(ps[W_BANKS[j]][:, a * P:(a + 1) * P], stack[0:K_SHIFTED, 1, a, j, b, :],
                                            stack[0:K_SHIFTED, 0, a, j, b, :], start=True, stop=True)
                last.then_inc(s["w_ps"], 1)

        def mixed(prev, b):
            pe.wait_ge(s["prob"], seq(PAIR * C, prev, C + 2 * (b + 1)))
            for h in range(H):
                j, a = h // HY, h % HY
                last = nc.tensor.matmul(ps[Y_BANKS[b][j]][:, a * DV:(a + 1) * DV], prob[:, b, h, :], v[:, b, h, :],
                                        start=True, stop=True)
            last.then_inc(s["y_ps"], 1)

        def scores(i, b):
            if b == 0:
                pe.wait_ge(s["stack"], seq(16 * STACK_DMAS, i, 16 * STACK_DMAS))
            for j in range(C):
                if b == 0 and j == 2:
                    pe.wait_ge(s["v"], seq(PAIR, i, 1))
                if b == 1:
                    pe.wait_ge(s["top"], seq(PAIR * C, i, j + 1))
                for a in range(HC):
                    last = nc.tensor.matmul(ps[S_BANKS[j]][:, a * P:(a + 1) * P], stack[0:K_SCORE, 0, a, j, b, :],
                                            stack[0:K_SCORE, 1, a, j, b, :], start=True, stop=True)
                last.then_inc(s["s_ps"], 1)

        def shift_row(i, b, last):
            pe.wait_ge(s["top"], seq(PAIR * C, i, C * (b + 1)))
            if not last:
                pe.wait_ge(s["xT_lo"], seq(PAIR, i + 1, b + 1))
            nc.tensor.transpose(ps[T_BANKS[b]][0:H, 0:P], top[:, b, :], ident[:]).then_inc(s["top_ps"], 1)

        x_transposed(0, 0)
        x_transposed(0, 1)

        def body(i, first, more, last):
            pe.wait_ge(s["xT_lo"], seq(PAIR, i, PAIR))
            projected(i, 1, (0, 1))
            if not first:
                weight_scores(i - 1, 0)
            projected(i, 1, (2, 3))
            if not first:
                weight_scores(i - 1, 1)
            projected(i, 0, range(C))
            if not first:
                mixed(i - 1, 0)
            pe.wait_ge(s["qk_lo"], seq(2 * C, i, 2))
            value_rows(i, 0)
            if not first:
                mixed(i - 1, 1)
                z_transposed(i - 1, 0)
                z_transposed(i - 1, 1)
            scores(i, 0)
            value_rows(i, 1)
            if not last:
                x_transposed(i + 1, 0)
            scores(i, 1)
            if not last:
                pe.wait_ge(s["v"], seq(PAIR, i, PAIR))
                x_transposed(i + 1, 1)
            if not first:
                out_rows(i - 1, 0)
            shift_row(i, 0, last)
            if not first:
                out_rows(i - 1, 1)
            if last:
                pe.wait_ge(s["v"], seq(PAIR, i, PAIR))
            shift_row(i, 1, last)

        bodies(pe, NP, body)
        for b in range(PAIR):
            weight_scores(NP - 1, b)
        for b in range(PAIR):
            mixed(NP - 1, b)
        for b in range(PAIR):
            z_transposed(NP - 1, b)
        for b in range(PAIR):
            out_rows(NP - 1, b)


_INS = ["x", "cond_2048", "mask_BxSx1_fk1", "mask_BxS_ff1", "L0_cond_ln_w", "L0_cond_ln_b", "L0_cond_Wq",
        "L0_cond_bq", "L0_cond_Wk", "L0_cond_bk", "L0_cond_Wv", "L0_cond_bv", "L0_cond_W_emb", "L0_cond_b_emb",
        "L0_cond_ln2_w", "L0_cond_ln2_b", "L0_cond_W_out", "L0_cond_b_out", "L1_cond_norm_w", "L1_cond_norm_b",
        "L1_cond_q_w", "L1_cond_q_b", "L1_cond_k_w", "L1_cond_k_b", "L1_cond_v_w", "L1_cond_v_b",
        "L1_cond_emb_w", "L1_cond_emb_b", "L1_cond_sb_norm_w", "L1_cond_sb_norm_b", "L1_cond_out_w",
        "L1_cond_out_b"]


def kernel(**inputs):
    import numpy as _np
    import concourse.bacc as _bacc
    from concourse import mybir as _mybir
    from concourse.bass_utils import run_bass_kernel_spmd as _run

    nc = _bacc.Bacc("TRN2", target_bir_lowering=False, num_devices=1)
    arrays, tensors = {}, {}
    for name in _INS:
        a = _np.ascontiguousarray(inputs[name])
        arrays[f"in_{name}"] = a
        tensors[name] = nc.dram_tensor(f"in_{name}", a.shape, _mybir.dt.from_np(a.dtype), kind="ExternalInput").ap()
    out = nc.dram_tensor("out", inputs["x"].shape, _mybir.dt.float32, kind="ExternalOutput").ap()
    build(nc, tensors, out)
    r = _run(nc, [arrays], core_ids=[0])
    return r.results[0]["out"]
```

```python
from contextlib import ExitStack
from itertools import islice, zip_longest

import concourse.bass as bass
from concourse import mybir

F32 = mybir.dt.float32
F32R = mybir.dt.float32r
ALU = mybir.AluOpType
ACT = mybir.ActivationFunctionType
AX_X = mybir.AxisListType.X

P = 128
PAIR = 2
RING = 3
RB = 64
BIG = -1000000.0
EPS = 1e-5

ROW_MASK = 96
ROW_SHIFT = 98
K_SCORE = 98
K_SHIFTED = 99


def seq(per, pair, k):
    return pair * per + k


def f32(ap):
    return ap.bitcast(F32)


def build(nc, T, out):
    x_d, cond_d = T["x"], T["cond_2048"]
    B, S, D = x_d.shape
    TE = cond_d.shape[1]
    NP = B // PAIR
    C = D // P
    H0, H1 = 8, 16
    HC = H1 // C
    D0, D1 = D // H0, D // H1
    KE = TE // P
    assert S == P and D1 == 32 and D0 == 64 and NP > 4

    x1_d = nc.dram_tensor("x_between_layers", [B, S, D], F32).ap()
    mask_d = nc.dram_tensor("mask_parts", [2, 2, B, S], F32).ap()

    root = ExitStack()
    with root:
        def sem(name):
            return root.enter_context(nc.semaphore(name))

        def sb(ctx, name, shape, dt=F32):
            return ctx.enter_context(nc.sbuf_tensor(name, shape, dt))

        ps = [root.enter_context(nc.psum_tensor(f"bank{i}", [P, 512], F32)) for i in range(8)]

        w_hi = sb(root, "w_hi", [P, 4, C, D], F32R)
        w_lo = sb(root, "w_lo", [P, 4, C, D], F32R)
        ident = sb(root, "ident", [P, P])
        ones = sb(root, "ones", [RB, P], F32R)
        bias_rows = sb(root, "bias_rows", [RB, 3, D], F32R)
        half_gain = sb(root, "half_gain", [P, 2, C, B])
        half_shift = sb(root, "half_shift", [P, 2, C, B])
        vec = sb(root, "vec", [P, 64])
        mask_col = sb(root, "mask_col", [P, 2, B])
        qk_bias = sb(root, "qk_bias", [P, 2, C])
        eps = sb(root, "eps", [P, 2])
        neg_half = sb(root, "neg_half", [P, 2])

        vec_rows = {}
        at = 0
        for name in ("L0_cond_ln_w", "L0_cond_ln_b", "L0_cond_ln2_w", "L0_cond_ln2_b", "L0_cond_b_emb",
                     "L1_cond_norm_w", "L1_cond_norm_b", "L1_cond_sb_norm_w", "L1_cond_sb_norm_b",
                     "L1_cond_emb_b", "L1_cond_q_b", "L1_cond_k_b"):
            n = T[name].shape[0] // P
            vec_rows[name] = (at, n)
            at += n
        n_vec = at

        def vcol(name, c):
            r = vec_rows[name][0] + c
            return vec[:, r:r + 1]

        mats = [[("L0_cond_Wq", "L0_cond_bq"), ("L0_cond_Wk", "L0_cond_bk"), ("L0_cond_Wv", "L0_cond_bv"),
                 ("L0_cond_W_out", "L0_cond_b_out")],
                [("L1_cond_q_w", "L1_cond_q_b"), ("L1_cond_k_w", "L1_cond_k_b"), ("L1_cond_v_w", "L1_cond_v_b"),
                 ("L1_cond_out_w", "L1_cond_out_b")]]
        raw1_in = [sem(f"raw1_in{n}") for n in range(4)]

        with ExitStack() as both:
            raw1 = [sb(both, f"raw1_{n}", [P, C, D]) for n in range(4)]
            with ExitStack() as ctx:
                key_bias = sb(ctx, "key_bias", [P, D], F32R)
                setup(nc, mats[0], T, sem, sb, ps, ident, ones, w_hi, w_lo, bias_rows, key_bias, half_gain,
                      half_shift, vec, vec_rows, n_vec, vcol, mask_col, mask_d, eps, neg_half, B, D, C, KE)
                layer0(nc, ctx, sem, sb, ps, x_d, x1_d, w_hi, w_lo, ident, ones, bias_rows, key_bias,
                       half_gain, half_shift, mask_col, mask_d, eps, neg_half,
                       [T[w] for w, _ in mats[1]], raw1, raw1_in, B, NP, D, C, H0, D0)
            second_weights(nc, mats[1], T, sem, sb, ps, w_hi, w_lo, raw1, raw1_in, bias_rows, qk_bias, vec,
                           vec_rows, vcol, D, C)

        with ExitStack() as ctx:
            layer1(nc, ctx, sem, sb, ps, x1_d, out, w_hi, w_lo, ident, ones, bias_rows, qk_bias,
                   half_gain, half_shift, mask_col, mask_d, eps, neg_half, B, NP, D, C, HC, H1, D1)


def high_part(nc, w_hi, raw, n, C, gain):
    if gain is None:
        return nc.scalar.activation(w_hi[:, n], raw[n][:], ACT.Copy)
    for c in range(C):
        last = nc.scalar.activation(w_hi[:, n, c, :], raw[n][:, c, :], ACT.Copy, scale=gain(c))
    return last


def low_part_of(nc, w_hi, w_lo, raw, n, C, gain):
    if gain is None:
        return nc.vector.tensor_tensor(w_lo[:, n], raw[n][:], f32(w_hi[:, n]), ALU.subtract)
    for c in range(C):
        last = nc.vector.scalar_tensor_tensor(w_lo[:, n, c, :], raw[n][:, c, :], gain(c), f32(w_hi[:, n, c, :]),
                                              ALU.mult, ALU.subtract)
    return last


def setup(nc, mats, T, sem, sb, ps, ident, ones, w_hi, w_lo, bias_rows, key_bias, half_gain, half_shift,
          vec, vec_rows, n_vec, vcol, mask_col, mask_d, eps, neg_half, B, D, C, KE):
    with ExitStack() as ctx:
        vec_in = sb(ctx, "vec_in", [n_vec, P])
        mask_in = sb(ctx, "mask_in", [B, 2, P])
        mask_top = sb(ctx, "mask_top", [B, 2])
        mask_hi = sb(ctx, "mask_hi", [B, 2, P], F32R)
        mask_lo = sb(ctx, "mask_lo", [B, 2, P], F32R)
        cond = sb(ctx, "cond", [B, KE * P])
        cond_tanh = sb(ctx, "cond_tanh", [B, KE * P])
        cond_T = sb(ctx, "cond_T", [P, KE, B])
        raw = [sb(ctx, f"raw0_{n}", [P, C, D]) for n in range(4)]
        bias_in = sb(ctx, "bias_in0", [1, 4, D])
        EMB_RING, EMB_PARTS = 5, 8
        DE = 2 * 2 * D // EMB_PARTS
        w_emb = sb(ctx, "w_emb", [P, EMB_RING, KE, DE])
        one_scale = sb(ctx, "one_scale", [P, 2, C, B])
        shift = sb(ctx, "shift", [P, 2, C, B])

        small_in = sem("small_in")
        bias_loaded = sem("bias_loaded0")
        raw_in = [sem(f"raw_in0_{n}") for n in range(4)]
        emb_in = [sem(f"emb_in{q}") for q in range(EMB_PARTS)]
        zeroed, cleared = sem("zeroed"), sem("cleared0")
        ident_ready = sem("ident_ready")
        consts_ready = sem("consts_ready")
        vec_ps, vec_ready = sem("vec_ps"), sem("vec_ready")
        mask_ps, mask_step, mask_out = sem("mask_ps"), sem("mask_step"), sem("mask_out")
        tanh_ready, cond_step = sem("tanh_ready"), sem("cond_step")
        cond_ps, cond_ready = sem("cond_ps"), sem("cond_ready")
        bias_ps, bias_step, split = sem("bias_ps0"), sem("bias_step0"), sem("split0")
        emb_ps, emb_step = sem("emb_ps"), sem("emb_step")
        BIAS_BANKS = (3, 6, 7)
        off = vec_rows["L0_cond_ln_b"][0]
        bias_to = [(bias_rows[0:1, 0, :], bias_rows[32:33, 0, :]), (key_bias[0:1, :], key_bias[32:33, :]),
                   (bias_rows[0:1, 1, :], bias_rows[32:33, 1, :]), (bias_rows[0:1, 2, :], bias_rows[32:33, 2, :])]

        def gain(n):
            return None if n == 3 else lambda c: vcol("L0_cond_ln_w", c)

        loads = [(cond[:], T["cond_2048"]),
                 (mask_in[:, 0, :], T["mask_BxSx1_fk1"].rearrange("b s o -> b (s o)")),
                 (mask_in[:, 1, :], T["mask_BxS_ff1"])]
        for name, (r, n) in vec_rows.items():
            loads.append((vec_in[r:r + n, :], T[name].rearrange("(c p) -> c p", p=P)))

        block = ctx.enter_context(nc.Block())

        @block.sync
        def _(sp):
            for dst, src in loads:
                sp.dma_start(dst, src).then_inc(small_in, 16)
            for n, (w, b) in enumerate(mats):
                sp.dma_start(raw[n][:], T[w].rearrange("(c p) n -> p c n", p=P)).then_inc(raw_in[n], 16)
            for n, (w, b) in enumerate(mats):
                sp.dma_start(bias_in[:, n, :], T[b].rearrange("(o d) -> o d", o=1)).then_inc(bias_loaded, 16)
            for q in range(EMB_PARTS):
                name = ("L0_cond_W_emb", "L1_cond_emb_w")[q // 4]
                if q >= EMB_RING:
                    sp.wait_ge(emb_ps, q - EMB_RING + 1)
                sp.dma_start(w_emb[:, q % EMB_RING],
                             T[name][:, (q % 4) * DE:(q % 4 + 1) * DE].rearrange("(k p) n -> p k n", p=P))\
                    .then_inc(emb_in[q], 16)
            sp.wait_ge(mask_step, 6)
            for n, part in enumerate((mask_hi, mask_lo)):
                sp.dma_start(mask_d[:, n].rearrange("l b t -> b l t"), f32(part[:])).then_inc(mask_out, 16)
            sp.wait_ge(mask_out, 32)

        @block.gpsimd
        def _(pool):
            nc.gpsimd.memset(ident[:], 0.0).then_inc(zeroed, 1)
            pool.wait_ge(zeroed, 1)
            nc.gpsimd.affine_select(out=ident[:], in_=ident[:], compare_op=ALU.not_equal, fill=1.0, base=0,
                                    pattern=[[-1, P]], channel_multiplier=1).then_inc(ident_ready, 1)
            nc.gpsimd.memset(eps[:], EPS)
            nc.gpsimd.memset(neg_half[:], -0.5)
            nc.gpsimd.memset(f32(ones[:]), 1.0).then_inc(consts_ready, 1)
            nc.gpsimd.memset(f32(bias_rows[:]), 0.0).then_inc(cleared, 1)
            nc.gpsimd.memset(f32(key_bias[:]), 0.0).then_inc(cleared, 1)
            pool.wait_ge(cleared, 2)
            nc.gpsimd.memset(f32(key_bias[64:65, :]), 1.0)
            nc.gpsimd.memset(f32(key_bias[96:97, :]), 1.0).then_inc(cleared, 1)

        @block.scalar
        def _(act):
            act.wait_ge(small_in, 16 * len(loads))
            nc.scalar.activation(cond_tanh[:], cond[:], ACT.Tanh, scale=0.5).then_inc(tanh_ready, 1)
            act.wait_ge(vec_ps, 1)
            nc.scalar.activation(vec[:, 0:n_vec], ps[0][:, 0:n_vec], ACT.Copy).then_inc(vec_ready, 1)
            act.wait_ge(mask_ps, 1)
            nc.scalar.activation(mask_col[:], ps[1][:, 0:2 * B].rearrange("p (l b) -> p l b", l=2), ACT.Copy)
            act.wait_ge(cond_ps, 1)
            nc.scalar.activation(cond_T[:], ps[2][:, 0:KE * B].rearrange("p (k b) -> p k b", k=KE),
                                 ACT.Copy, scale=0.5).then_inc(cond_ready, 1)
            act.wait_ge(vec_ready, 1)
            for n in range(4):
                act.wait_ge(raw_in[n], 16)
                high_part(nc, w_hi, raw, n, C, gain(n)).then_inc(split, 1)

        @block.vector
        def _(dve):
            dve.wait_ge(small_in, 16 * len(loads))
            dve.wait_ge(tanh_ready, 1)
            nc.vector.scalar_tensor_tensor(cond_tanh[:], cond_tanh[:], 1.0, cond[:], ALU.add,
                                           ALU.mult).then_inc(cond_step, 1)
            dve.wait_ge(mask_ps, 1)
            nc.vector.tensor_scalar(mask_in[:], mask_in[:], -1.0, 1.0, ALU.mult, ALU.add).then_inc(mask_step, 1)
            dve.wait_ge(mask_step, 1)
            nc.vector.tensor_scalar(mask_in[:], mask_in[:], BIG, None, ALU.mult).then_inc(mask_step, 1)
            dve.wait_ge(mask_step, 2)
            nc.vector.reduce_max(mask_top[:], mask_in[:], AX_X).then_inc(mask_step, 1)
            dve.wait_ge(mask_step, 3)
            for n in range(2):
                last = nc.vector.tensor_scalar(mask_in[:, n, :], mask_in[:, n, :], mask_top[:, n:n + 1], None,
                                               ALU.subtract)
            last.then_inc(mask_step, 1)
            dve.wait_ge(mask_step, 4)
            nc.vector.tensor_copy(mask_hi[:], mask_in[:]).then_inc(mask_step, 1)
            dve.wait_ge(mask_step, 5)
            nc.vector.tensor_tensor(mask_lo[:], mask_in[:], f32(mask_hi[:]), ALU.subtract).then_inc(mask_step, 1)
            dve.wait_ge(vec_ready, 1)
            for n in range(4):
                dve.wait_ge(split, n + 1)
                low_part_of(nc, w_hi, w_lo, raw, n, C, gain(n))
            dve.wait_ge(bias_loaded, 64)
            dve.wait_ge(cleared, 3)
            for n in range(3):
                dve.wait_ge(bias_ps, n + 1)
                last = nc.vector.tensor_tensor(bias_in[:, n, :], ps[BIAS_BANKS[n]][0:1, :], bias_in[:, n, :], ALU.add)
            last.then_inc(bias_step, 1)
            dve.wait_ge(bias_step, 1)
            for n, (hi, lo) in enumerate(bias_to):
                last = nc.vector.tensor_copy(hi, bias_in[:, n, :])
            last.then_inc(bias_step, 1)
            dve.wait_ge(bias_step, 2)
            for n, (hi, lo) in enumerate(bias_to):
                nc.vector.tensor_tensor(lo, bias_in[:, n, :], f32(hi), ALU.subtract)
            for n, pre in enumerate((("L0_cond_b_emb", "L0_cond_ln2_w", "L0_cond_ln2_b"),
                                     ("L1_cond_emb_b", "L1_cond_sb_norm_w", "L1_cond_sb_norm_b"))):
                be, gw, gb = pre
                dve.wait_ge(emb_ps, 4 * (n + 1))
                for c in range(C):
                    nc.vector.tensor_scalar(one_scale[:, n, c, :], ps[4 + n][:, c * B:(c + 1) * B], vcol(be, c),
                                            1.0, ALU.add, ALU.add)
                    last = nc.vector.tensor_scalar(shift[:, n, c, :], ps[4 + n][:, (C + c) * B:(C + c + 1) * B],
                                                   vcol(be, C + c), None, ALU.add)
                last.then_inc(emb_step, 1)
                dve.wait_ge(emb_step, 3 * n + 1)
                for c in range(C):
                    nc.vector.tensor_scalar(half_gain[:, n, c, :], one_scale[:, n, c, :], vcol(gw, c), 0.5,
                                            ALU.mult, ALU.mult)
                    last = nc.vector.scalar_tensor_tensor(shift[:, n, c, :], one_scale[:, n, c, :], vcol(gb, c),
                                                          shift[:, n, c, :], ALU.mult, ALU.add)
                last.then_inc(emb_step, 1)
                dve.wait_ge(emb_step, 3 * n + 2)
                nc.vector.tensor_scalar(half_shift[:, n], shift[:, n], 0.5, None, ALU.mult).then_inc(emb_step, 1)

        @block.tensor
        def _(pe):
            pe.wait_ge(ident_ready, 1)
            pe.wait_ge(small_in, 16 * len(loads))
            nc.tensor.transpose(ps[0][:, 0:n_vec], vec_in[:], ident[0:n_vec, 0:n_vec]).then_inc(vec_ps, 1)
            for n in range(2):
                last = nc.tensor.transpose(ps[1][:, n * B:(n + 1) * B], mask_in[:, n, :], ident[0:B, 0:B])
            last.then_inc(mask_ps, 1)
            pe.wait_ge(cond_step, 1)
            for k in range(KE):
                last = nc.tensor.transpose(ps[2][:, k * B:(k + 1) * B], cond_tanh[:, k * P:(k + 1) * P],
                                           ident[0:B, 0:B])
            last.then_inc(cond_ps, 1)
            pe.wait_ge(vec_ready, 1)
            for n in range(3):
                pe.wait_ge(raw_in[n], 16)
                for c in range(C):
                    last = nc.tensor.matmul(ps[BIAS_BANKS[n]][0:1, :], vec[:, off + c:off + c + 1], raw[n][:, c, :],
                                            start=(c == 0), stop=(c == C - 1))
                last.then_inc(bias_ps, 1)
            pe.wait_ge(cond_ready, 1)
            for q in range(EMB_PARTS):
                pe.wait_ge(emb_in[q], 16)
                for f in range(DE // P):
                    at = ((q % 4) * (DE // P) + f) * B
                    for k in range(KE):
                        last = nc.tensor.matmul(ps[4 + q // 4][:, at:at + B],
                                                w_emb[:, q % EMB_RING, k, f * P:(f + 1) * P], cond_T[:, k, :],
                                                start=(k == 0), stop=(k == KE - 1))
                last.then_inc(emb_ps, 1)


def second_weights(nc, mats, T, sem, sb, ps, w_hi, w_lo, raw, raw_in, bias_rows, qk_bias, vec, vec_rows, vcol, D, C):
    with ExitStack() as ctx:
        bias_in = sb(ctx, "bias_in1", [1, 2, D])
        bias_loaded = sem("bias_loaded1")
        bias_ps, bias_step, split = sem("bias_ps1"), sem("bias_step1"), sem("split1")
        off = vec_rows["L1_cond_norm_b"][0]

        def gain(n):
            return None if n == 3 else lambda c: vcol("L1_cond_norm_w", c)

        block = ctx.enter_context(nc.Block())

        @block.sync
        def _(sp):
            for n, (w, b) in enumerate(mats[2:]):
                sp.dma_start(bias_in[:, n, :], T[b].rearrange("(o d) -> o d", o=1)).then_inc(bias_loaded, 16)

        @block.tensor
        def _(pe):
            for n in range(3):
                pe.wait_ge(raw_in[n], 16)
                if n < 2:
                    for f in range(C):
                        for c in range(C):
                            last = nc.tensor.matmul(ps[n][:, f:f + 1], raw[n][:, c, f * P:(f + 1) * P],
                                                    vec[:, off + c:off + c + 1], start=(c == 0), stop=(c == C - 1))
                else:
                    for c in range(C):
                        last = nc.tensor.matmul(ps[n][0:1, :], vec[:, off + c:off + c + 1], raw[n][:, c, :],
                                                start=(c == 0), stop=(c == C - 1))
                last.then_inc(bias_ps, 1)

        @block.scalar
        def _(act):
            for n in (1, 0, 2, 3):
                act.wait_ge(raw_in[n], 16)
                high_part(nc, w_hi, raw, n, C, gain(n)).then_inc(split, 1)

        @block.vector
        def _(dve):
            for k, n in enumerate((1, 0, 2, 3)):
                dve.wait_ge(raw_in[n], 16)
                dve.wait_ge(split, k + 1)
                low_part_of(nc, w_hi, w_lo, raw, n, C, gain(n))
            for n in range(2):
                dve.wait_ge(bias_ps, n + 1)
                r = vec_rows[mats[n][1]][0]
                nc.vector.tensor_tensor(qk_bias[:, n, :], ps[n][:, 0:C], vec[:, r:r + C], ALU.add)
            dve.wait_ge(bias_loaded, 32)
            dve.wait_ge(bias_ps, 3)
            nc.vector.tensor_tensor(bias_in[:, 0, :], ps[2][0:1, :], bias_in[:, 0, :], ALU.add).then_inc(bias_step, 1)
            dve.wait_ge(bias_step, 1)
            nc.vector.tensor_copy(bias_rows[0:1, 1:3, :], bias_in[:]).then_inc(bias_step, 1)
            dve.wait_ge(bias_step, 2)
            nc.vector.tensor_tensor(bias_rows[32:33, 1:3, :], bias_in[:], f32(bias_rows[0:1, 1:3, :]), ALU.subtract)


def project_rows(nc, w_hi, w_lo, m, a_hi, a_lo, b, bank, C, ones, bias):
    yield nc.tensor.matmul(bank[:, :], ones[:], bias, start=True, stop=False)
    for c in range(C):
        yield nc.tensor.matmul(bank[:, :], a_hi[:, c, b, :], w_hi[:, m, c, :], start=False, stop=False)
        yield nc.tensor.matmul(bank[:, :], a_lo[:, c, b, :], w_hi[:, m, c, :], start=False, stop=False)
        yield nc.tensor.matmul(bank[:, :], a_hi[:, c, b, :], w_lo[:, m, c, :], start=False, stop=(c == C - 1))


def project_features(nc, w_hi, w_lo, m, f, a_hi, a_lo, dst, C, first):
    fs = slice(f * P, (f + 1) * P)
    for c in range(C):
        yield nc.tensor.matmul(dst, w_hi[:, m, c, fs], a_hi[:, c], start=(first and c == 0), stop=False)
        yield nc.tensor.matmul(dst, w_hi[:, m, c, fs], a_lo[:, c], start=False, stop=False)
        yield nc.tensor.matmul(dst, w_lo[:, m, c, fs], a_hi[:, c], start=False, stop=(c == C - 1))


def run(steps):
    last = None
    for last in steps:
        pass
    return last


def several(n, steps):
    while list(islice(steps, n)):
        yield


def woven(one, other, n=None):
    for _ in islice(zip_longest(one, other), n):
        pass


def bodies(eng, NP, body):
    body(0, True, True, False)
    with eng.Fori(1, NP - 2) as i:
        body(i, False, True, False)
    body(NP - 2, False, False, False)
    body(NP - 1, False, False, True)


def layer0(nc, ctx, sem, sb, ps, x_d, x1_d, w_hi, w_lo, ident, ones, bias_rows, key_bias,
           half_gain, half_shift, mask_col, mask_d, eps, neg_half, next_w, next_raw, next_in, B, NP, D, C, H, DH):
    Q, K, V, O = range(4)
    BQ, BV, BO = range(3)
    HB = 2
    DV = P + 1
    DY = P + HB
    xr = sb(ctx, "xr", [P, RING, PAIR, D])
    xn = sb(ctx, "xn", [P, PAIR, D])
    xT_hi = sb(ctx, "xT_hi", [P, C, PAIR, P], F32R)
    xT_lo = sb(ctx, "xT_lo", [P, C, PAIR, P], F32R)
    k_neg = sb(ctx, "k_neg", [P, C, PAIR])
    k_exp = sb(ctx, "k_exp", [P, C, PAIR, P])
    q_max = sb(ctx, "q_max", [P, PAIR, H])
    q_exp = sb(ctx, "q_exp", [P, PAIR, D])
    qT = sb(ctx, "qT", [P, PAIR, C, P])
    k_rows = sb(ctx, "k_rows", [P, PAIR, C, P])
    v = sb(ctx, "v", [P, PAIR, C, DV])
    k_sum = sb(ctx, "k_sum", [P, PAIR, C])
    q_sum = sb(ctx, "q_sum", [P, PAIR, H])
    att = sb(ctx, "att", [P, PAIR, C, DY])
    z = sb(ctx, "z", [P, PAIR, D])
    g = sb(ctx, "g", [P, PAIR, C, P])
    th = sb(ctx, "th", [P, PAIR, C, P])
    hs = sb(ctx, "hs", [P, PAIR, C, P])
    h_hi = sb(ctx, "h_hi", [P, C, PAIR, P], F32R)
    h_lo = sb(ctx, "h_lo", [P, C, PAIR, P], F32R)
    x1 = sb(ctx, "x1", [P, PAIR, D])
    stats = sb(ctx, "stats", [P, PAIR, 6])
    stats_y = sb(ctx, "stats_y", [P, PAIR, 6])
    mv = sb(ctx, "mv", [P, PAIR, 2])
    mv_y = sb(ctx, "mv_y", [P, PAIR, 2])
    ve = sb(ctx, "ve", [P, PAIR])
    ve_y = sb(ctx, "ve_y", [P, PAIR])
    rstd = sb(ctx, "rstd", [P, PAIR])
    rstd_y = sb(ctx, "rstd_y", [P, PAIR])
    gains = sb(ctx, "gains", [P, 2, C, PAIR])
    mask_now = sb(ctx, "mask_now", [P, PAIR])
    mask_rows = sb(ctx, "mask_rows", [P, RING, PAIR * P], F32R)
    seen = sb(ctx, "seen", [P, 1])

    s = {n: sem("l0_" + n) for n in (
        "preset", "rows_preset", "masks", "x_in", "stats", "var", "var_eps", "rstd", "xn", "xT_ps", "xT_hi", "xT_lo",
        "kT_ps", "k_neg", "k_exp", "q_ps", "q_max", "q_less", "q_exp", "v_ps", "v", "q_tr", "k_tr", "qT", "k_rows",
        "att_ps", "k_sum", "att", "y_ps", "q_sum", "y", "y_stats", "y_var", "y_var_eps", "y_rstd", "z", "z_ps", "gains",
        "g", "tanh", "silu", "h_hi", "h_lo", "o_ps", "x1", "stored")}

    block = ctx.enter_context(nc.Block())

    @block.sync
    def _(sp):
        sp.wait_ge(s["rows_preset"], 1)

        def load(pair, slot):
            sp.dma_start(xr[:, slot], x_d[bass.ds(pair * PAIR, PAIR)].rearrange("b t d -> t b d")).then_inc(s["x_in"], 16)
            for n, r in enumerate((64, 96)):
                sp.dma_start(f32(mask_rows[r:r + 1, slot, :]),
                             mask_d[0, n, bass.ds(pair * PAIR, PAIR)].rearrange("b t -> (b t)").unsqueeze(0))\
                    .then_inc(s["x_in"], 16)

        load(0, 0)
        load(1, 1)
        for w, dst, arrived in zip(next_w, next_raw, next_in):
            sp.dma_start(dst[:], w.rearrange("(c p) n -> p c n", p=P)).then_inc(arrived, 16)

        def store(prev):
            for b in range(PAIR):
                sp.wait_ge(s["x1"], seq(PAIR, prev, b + 1))
                sp.dma_start(x1_d[prev * PAIR + b], x1[:, b]).then_inc(s["stored"], 16)
            sp.wait_ge(s["stored"], seq(16 * PAIR, prev, 16 * PAIR))

        def body(i, first, more, last):
            if not first:
                store(i - 1)
            if more:
                sp.wait_ge(s["x_in"], seq(48, i, 96))
                load(i + 2, (i + 2) % RING)

        bodies(sp, NP, body)
        store(NP - 1)

    @block.gpsimd
    def _(pool):
        nc.gpsimd.memset(f32(mask_rows[:]), 1.0).then_inc(s["rows_preset"], 1)

        def inverse_root(n, var, e, to, var_eps_sem, rstd_sem, pair):
            nc.gpsimd.tensor_tensor(e[:], var[:, :, 1], eps[:], ALU.add).then_inc(var_eps_sem, 1)
            pool.wait_ge(var_eps_sem, seq(1, pair, 1))
            nc.gpsimd.tensor_tensor(to[:], e[:], neg_half[:], ALU.pow).then_inc(rstd_sem, 1)

        def end(prev):
            pool.wait_ge(s["y_var"], seq(1, prev, 1))
            inverse_root(0, mv_y, ve_y, rstd_y, s["y_var_eps"], s["y_rstd"], prev)
            nc.gpsimd.tensor_copy(gains[:, 0], half_gain[:, 0, :, bass.ds(prev * PAIR, PAIR)])
            nc.gpsimd.tensor_copy(gains[:, 1], half_shift[:, 0, :, bass.ds(prev * PAIR, PAIR)]).then_inc(s["gains"], 1)

        def norm(pair):
            pool.wait_ge(s["var"], seq(1, pair, 1))
            inverse_root(1, mv, ve, rstd, s["var_eps"], s["rstd"], pair)

        def low_parts(prev):
            for b in range(PAIR):
                pool.wait_ge(s["h_hi"], seq(PAIR, prev, b + 1))
                nc.gpsimd.tensor_tensor(h_lo[:, :, b, :], hs[:, b], f32(h_hi[:, :, b, :]),
                                        ALU.subtract).then_inc(s["h_lo"], 1)

        norm(0)

        def body(i, first, more, last):
            if not first:
                end(i - 1)
            if not last:
                norm(i + 1)
            if not first:
                low_parts(i - 1)

        bodies(pool, NP, body)
        end(NP - 1)
        low_parts(NP - 1)

    @block.vector
    def _(dve):
        nc.vector.memset(v[:], 1.0)
        nc.vector.memset(att[:], 0.0).then_inc(s["preset"], 1)
        dve.wait_ge(s["preset"], 1)
        nc.vector.memset(att[0:64, :, :, P:P + 1], 1.0)
        nc.vector.memset(att[64:128, :, :, P + 1:P + 2], 1.0).then_inc(s["preset"], 1)

        def row_stats(pair, slot):
            dve.wait_ge(s["x_in"], seq(48, pair, 48) if not isinstance(pair, int) or pair > 0 else 96)
            for b in range(PAIR):
                nc.vector.bn_stats(stats[:, b], xr[:, slot, b]).then_inc(s["stats"], 1)
            dve.wait_ge(s["stats"], seq(PAIR, pair, PAIR))
            nc.vector.tensor_copy(seen[:], eps[:, 0:1])
            for b in range(PAIR):
                last = nc.vector.bn_aggr(mv[:, b], stats[:, b])
            last.then_inc(s["var"], 1)

        def norm(pair, slot):
            dve.wait_ge(s["rstd"], seq(1, pair, 1))
            for b in range(PAIR):
                nc.vector.tensor_scalar(xn[:, b], xr[:, slot, b], mv[:, b, 0:1], rstd[:, b:b + 1], ALU.subtract,
                                        ALU.mult).then_inc(s["xn"], 1)

        def x_low(pair, banks):
            for b in range(PAIR):
                dve.wait_ge(s["xT_hi"], seq(PAIR, pair, b + 1))
                nc.vector.tensor_tensor(xT_lo[:, :, b, :], banks[b][:, :].rearrange("p (c t) -> p c t", c=C),
                                        f32(xT_hi[:, :, b, :]), ALU.subtract).then_inc(s["xT_lo"], 1)

        def end_norm(prev):
            dve.wait_ge(s["y_rstd"], seq(1, prev, 1))
            for b in range(PAIR):
                nc.vector.tensor_scalar(z[:, b], z[:, b], mv_y[:, b, 0:1], rstd_y[:, b:b + 1], ALU.subtract,
                                        ALU.mult).then_inc(s["z"], 1)

        def end_gates(prev):
            dve.wait_ge(s["gains"], seq(1, prev, 1))
            for b in range(PAIR):
                dve.wait_ge(s["z_ps"], seq(PAIR, prev, b + 1))
                for c in range(C):
                    last = nc.vector.tensor_scalar(g[:, b, c, :], ps[6 + b][:, c * P:(c + 1) * P],
                                                   gains[:, 0, c, b:b + 1], gains[:, 1, c, b:b + 1], ALU.mult, ALU.add)
                last.then_inc(s["g"], 1)

        def end_silus(prev):
            for b in range(PAIR):
                dve.wait_ge(s["tanh"], seq(PAIR, prev, b + 1))
                nc.vector.scalar_tensor_tensor(hs[:, b], th[:, b], 1.0, g[:, b], ALU.add,
                                               ALU.mult).then_inc(s["silu"], 1)

        def end_add(prev, slot, b):
            if isinstance(prev, int) and prev > 0 and b == 0:
                dve.wait_ge(s["stored"], seq(16 * PAIR, prev - 1, 16 * PAIR))
            dve.wait_ge(s["o_ps"], seq(PAIR, prev, b + 1))
            nc.vector.tensor_tensor(x1[:, b], ps[b][:, :], xr[:, slot, b], ALU.add).then_inc(s["x1"], 1)

        def key_maxima(i):
            for j in range(2):
                dve.wait_ge(s["kT_ps"], seq(2, i, j + 1))
                nc.vector.tensor_reduce(k_neg[:, 2 * j:2 * j + 2, :],
                                        ps[j][:, :].rearrange("p (c b t) -> p c b t", c=2, b=PAIR), AX_X, ALU.max,
                                        negate=True).then_inc(s["k_neg"], 1)

        def query_shift(i, b):
            q3 = ps[2 + b][:, :].rearrange("p (h d) -> p h d", h=H)
            dve.wait_ge(s["q_ps"], seq(PAIR, i, b + 1))
            nc.vector.reduce_max(q_max[:, b], q3, AX_X).then_inc(s["q_max"], 1)
            dve.wait_ge(s["q_max"], seq(PAIR, i, b + 1))
            nc.vector.tensor_tensor(q_exp[:, b].rearrange("p (h d) -> p h d", h=H), q3,
                                    q_max[:, b].unsqueeze(2).broadcast_to([P, H, DH]),
                                    ALU.subtract).then_inc(s["q_less"], 1)

        def key_rows(i, b):
            dve.wait_ge(s["k_tr"], seq(PAIR, i, b + 1))
            nc.vector.tensor_copy(k_rows[:, b], ps[(7, 5)[b]][:, :].rearrange("p (c t) -> p c t", c=C))\
                .then_inc(s["k_rows"], 1)

        def weights_of(i):
            for b in range(PAIR):
                banks = ((0, 1), (6, 7))[b]
                dve.wait_ge(s["att_ps"], seq(PAIR, i, b + 1))
                for j in range(2):
                    a = ps[banks[j]][:, 0:2 * DV].rearrange("p (c d) -> p c d", c=2)
                    last = nc.vector.reciprocal(k_sum[:, b, 2 * j:2 * j + 2], a[:, :, P])
                last.then_inc(s["k_sum"], 1)
                dve.wait_ge(s["k_sum"], seq(PAIR, i, b + 1))
                for j in range(2):
                    a = ps[banks[j]][:, 0:2 * DV].rearrange("p (c d) -> p c d", c=2)
                    for r in range(2):
                        rows, cols = slice(64 * r, 64 * r + 64), slice(64 * r, 64 * r + 64)
                        last = nc.vector.tensor_tensor(
                            att[rows, b, 2 * j:2 * j + 2, cols], a[rows, :, cols],
                            k_sum[rows, b, 2 * j:2 * j + 2].unsqueeze(2).broadcast_to([64, 2, 64]), ALU.mult)
                last.then_inc(s["att"], 1)

        def outputs(i):
            for b in range(PAIR):
                banks = ((4, 5), (2, 3))[b]
                dve.wait_ge(s["y_ps"], seq(PAIR, i, b + 1))
                for j in range(2):
                    a = ps[banks[j]][:, 0:2 * DY].rearrange("p (c d) -> p c d", c=2)
                    last = nc.vector.reciprocal(q_sum[:, b, 4 * j:4 * j + 4].rearrange("p (c r) -> p c r", c=2),
                                                a[:, :, P:P + 2])
                last.then_inc(s["q_sum"], 1)
                dve.wait_ge(s["q_sum"], seq(PAIR, i, b + 1))
                for j in range(2):
                    a = ps[banks[j]][:, 0:2 * DY].rearrange("p (c d) -> p c d", c=2)
                    for c in range(2):
                        last = nc.vector.tensor_tensor(
                            z[:, b, (2 * j + c) * P:(2 * j + c + 1) * P].rearrange("p (r d) -> p r d", r=2),
                            a[:, c, 0:P].rearrange("p (r d) -> p r d", r=2),
                            q_sum[:, b, 4 * j + 2 * c:4 * j + 2 * c + 2].unsqueeze(2).broadcast_to([P, 2, DH]),
                            ALU.mult)
                last.then_inc(s["y"], 1)
                dve.wait_ge(s["y"], seq(PAIR, i, b + 1))
                nc.vector.bn_stats(stats_y[:, b], z[:, b]).then_inc(s["y_stats"], 1)
            dve.wait_ge(s["y_stats"], seq(PAIR, i, PAIR))
            nc.vector.tensor_copy(seen[:], eps[:, 0:1])
            for b in range(PAIR):
                last = nc.vector.bn_aggr(mv_y[:, b], stats_y[:, b])
            last.then_inc(s["y_var"], 1)

        row_stats(0, 0)
        norm(0, 0)
        x_low(0, (ps[2], ps[3]))

        def body(i, first, more, last):
            if not first:
                end_norm(i - 1)
            key_maxima(i)
            if not last:
                row_stats(i + 1, (i + 1) % RING)
            query_shift(i, 0)
            if not first:
                end_gates(i - 1)
            query_shift(i, 1)
            if not first:
                end_silus(i - 1)
            if not last:
                norm(i + 1, (i + 1) % RING)
                x_low(i + 1, (ps[2], ps[3]))
            for b in range(PAIR):
                if not first:
                    end_add(i - 1, (i - 1) % RING, b)
                key_rows(i, b)
            weights_of(i)
            outputs(i)

        bodies(dve, NP, body)
        end_norm(NP - 1)
        end_gates(NP - 1)
        end_silus(NP - 1)
        for b in range(PAIR):
            end_add(NP - 1, (NP - 1) % RING, b)

    @block.scalar
    def _(act):
        def x_high(pair, banks):
            for b in range(PAIR):
                act.wait_ge(s["xT_ps"], seq(PAIR, pair, b + 1))
                nc.scalar.activation(xT_hi[:, :, b, :], banks[b][:, :].rearrange("p (c t) -> p c t", c=C),
                                     ACT.Copy).then_inc(s["xT_hi"], 1)

        def key_exps(i):
            for j in range(2):
                act.wait_ge(s["k_neg"], seq(2, i, j + 1))
                for c in (2 * j, 2 * j + 1):
                    for b in range(PAIR):
                        at = (c - 2 * j) * PAIR * P + b * P
                        last = nc.scalar.activation(k_exp[:, c, b, :], ps[j][:, at:at + P], ACT.Exp,
                                                    bias=k_neg[:, c, b:b + 1])
                last.then_inc(s["k_exp"], 1)

        def query_exps(i, b):
            act.wait_ge(s["q_less"], seq(PAIR, i, b + 1))
            nc.scalar.activation(q_exp[:, b], q_exp[:, b], ACT.Exp).then_inc(s["q_exp"], 1)

        def tanhs(prev):
            for b in range(PAIR):
                act.wait_ge(s["g"], seq(PAIR, prev, b + 1))
                nc.scalar.activation(th[:, b], g[:, b], ACT.Tanh).then_inc(s["tanh"], 1)

        def h_high(prev):
            for b in range(PAIR):
                act.wait_ge(s["silu"], seq(PAIR, prev, b + 1))
                nc.scalar.activation(h_hi[:, :, b, :], hs[:, b], ACT.Copy).then_inc(s["h_hi"], 1)

        def values(i, b):
            act.wait_ge(s["v_ps"], seq(PAIR, i, b + 1))
            nc.scalar.activation(v[:, b, :, 0:P], ps[4 + b][:, :].rearrange("p (c d) -> p c d", c=C), ACT.Copy,
                                 scale=mask_now[:, b:b + 1]).then_inc(s["v"], 1)

        def query_T(i):
            for b in range(PAIR):
                act.wait_ge(s["q_tr"], seq(PAIR, i, b + 1))
                nc.scalar.activation(qT[:, b], ps[(6, 4)[b]][:, :].rearrange("p (c t) -> p c t", c=C),
                                     ACT.Copy).then_inc(s["qT"], 1)

        act.wait_ge(s["preset"], 2)
        x_high(0, (ps[2], ps[3]))

        def body(i, first, more, last):
            nc.scalar.activation(mask_now[:], mask_col[:, 0, bass.ds(i * PAIR, PAIR)], ACT.Copy)\
                .then_inc(s["masks"], 1)
            key_exps(i)
            query_exps(i, 0)
            if not first:
                tanhs(i - 1)
            query_exps(i, 1)
            act.wait_ge(s["masks"], seq(1, i, 1))
            values(i, 0)
            if not first:
                h_high(i - 1)
            values(i, 1)
            if not last:
                x_high(i + 1, (ps[2], ps[3]))
            query_T(i)

        bodies(act, NP, body)
        tanhs(NP - 1)
        h_high(NP - 1)

    @block.tensor
    def _(pe):
        pe.wait_ge(s["preset"], 2)

        def x_transposed(pair):
            for b in range(PAIR):
                pe.wait_ge(s["xn"], seq(PAIR, pair, b + 1))
                for c in range(C):
                    last = nc.tensor.transpose(ps[2 + b][:, c * P:(c + 1) * P], xn[:, b, c * P:(c + 1) * P], ident[:])
                last.then_inc(s["xT_ps"], 1)

        def z_transposed(prev):
            for b in range(PAIR):
                pe.wait_ge(s["z"], seq(PAIR, prev, b + 1))
                for c in range(C):
                    last = nc.tensor.transpose(ps[6 + b][:, c * P:(c + 1) * P], z[:, b, c * P:(c + 1) * P], ident[:])
                last.then_inc(s["z_ps"], 1)

        def out_rows(prev, b):
            pe.wait_ge(s["h_lo"], seq(PAIR, prev, b + 1))
            run(project_rows(nc, w_hi, w_lo, O, h_hi, h_lo, b, ps[b], C, ones,
                             bias_rows[:, BO, :])).then_inc(s["o_ps"], 1)

        def weights_turned(i, b):
            pe.wait_ge(s["q_exp"], seq(PAIR, i, b + 1))
            pe.wait_ge(s["v"], seq(PAIR, i, PAIR))
            for c in range(C):
                done = nc.tensor.transpose(ps[(6, 4)[b]][:, c * P:(c + 1) * P], q_exp[:, b, c * P:(c + 1) * P],
                                           ident[:])
            done.then_inc(s["q_tr"], 1)
            for c in range(C):
                done = nc.tensor.transpose(ps[(7, 5)[b]][:, c * P:(c + 1) * P], k_exp[:, c, b, :], ident[:])
            done.then_inc(s["k_tr"], 1)

        x_transposed(0)

        def body(i, first, more, last):
            pe.wait_ge(s["xT_lo"], seq(PAIR, i, PAIR))
            for f in range(C):
                dst = ps[f // 2][:, (f % 2) * PAIR * P:(f % 2 + 1) * PAIR * P]
                nc.tensor.matmul(dst, key_bias[:, f * P:(f + 1) * P], mask_rows[:, i % RING, :],
                                 start=True, stop=False)
                done = run(project_features(nc, w_hi, w_lo, K, f, xT_hi, xT_lo, dst, C, False))
                if f % 2:
                    done.then_inc(s["kT_ps"], 1)
            if not first:
                pe.wait_ge(s["y"], seq(PAIR, i - 1, PAIR))
            for b in range(PAIR):
                if b == 1 and not first:
                    z_transposed(i - 1)
                run(project_rows(nc, w_hi, w_lo, Q, xT_hi, xT_lo, b, ps[2 + b], C, ones,
                                 bias_rows[:, BQ, :])).then_inc(s["q_ps"], 1)
            for b in range(PAIR):
                run(project_rows(nc, w_hi, w_lo, V, xT_hi, xT_lo, b, ps[4 + b], C, ones,
                                 bias_rows[:, BV, :])).then_inc(s["v_ps"], 1)
            pe.wait_ge(s["k_exp"], seq(2, i, 2))
            if not last:
                pe.wait_ge(s["q_less"], seq(PAIR, i, PAIR))
                x_transposed(i + 1)
            for b in range(PAIR):
                if not first:
                    out_rows(i - 1, b)
                weights_turned(i, b)
            for b in range(PAIR):
                banks = ((0, 1), (6, 7))[b]
                if b == 0 and not first:
                    pe.wait_ge(s["x1"], seq(PAIR, i - 1, PAIR))
                pe.wait_ge(s["k_rows"], seq(PAIR, i, b + 1))
                pe.wait_ge(s["qT"], seq(PAIR, i, b + 1))
                for c in range(C):
                    done = nc.tensor.matmul(ps[banks[c // 2]][:, (c % 2) * DV:(c % 2 + 1) * DV], k_rows[:, b, c, :],
                                            v[:, b, c, :], start=True, stop=True)
                done.then_inc(s["att_ps"], 1)
            for b in range(PAIR):
                banks = ((4, 5), (2, 3))[b]
                if b == 1 and not last:
                    pe.wait_ge(s["xT_lo"], seq(PAIR, i + 1, PAIR))
                pe.wait_ge(s["att"], seq(PAIR, i, b + 1))
                for c in range(C):
                    done = nc.tensor.matmul(ps[banks[c // 2]][:, (c % 2) * DY:(c % 2 + 1) * DY], qT[:, b, c, :],
                                            att[:, b, c, :], start=True, stop=True)
                done.then_inc(s["y_ps"], 1)

        bodies(pe, NP, body)
        z_transposed(NP - 1)
        for b in range(PAIR):
            out_rows(NP - 1, b)


def layer1(nc, ctx, sem, sb, ps, x1_d, out, w_hi, w_lo, ident, ones, bias_rows, qk_bias,
           half_gain, half_shift, mask_col, mask_d, eps, neg_half, B, NP, D, C, HC, H, DH):
    Q, K, V, O = range(4)
    BV, BO = 1, 2
    DV = DH + 1
    HB = 512 // P
    HY = H // 2
    xr = sb(ctx, "xr1", [P, RING, PAIR, D])
    xn = sb(ctx, "xn1", [P, PAIR, D])
    xT_hi = sb(ctx, "xT_hi1", [P, C, PAIR, P], F32R)
    xT_lo = sb(ctx, "xT_lo1", [P, C, PAIR, P], F32R)
    parts = sb(ctx, "parts", [P, 4, C, PAIR, P], F32R)
    Q_LO, Q_HI, K_HI, K_LO = range(4)
    HI, LO = (Q_HI, K_HI), (Q_LO, K_LO)
    stack = sb(ctx, "stack", [P, 2, HC, C, PAIR, P], F32R)
    v = sb(ctx, "v1", [P, PAIR, H, DV])
    top = sb(ctx, "top", [P, PAIR, H])
    top_T = sb(ctx, "top_T", [H, PAIR, P], F32R)
    prob = sb(ctx, "prob", [P, PAIR, H, P])
    p_sum = sb(ctx, "p_sum", [P, PAIR, H])
    z = sb(ctx, "z1", [P, PAIR, D])
    g = sb(ctx, "g1", [P, PAIR, C, P])
    th = sb(ctx, "th1", [P, PAIR, C, P])
    hs = sb(ctx, "hs1", [P, PAIR, C, P])
    h_hi = sb(ctx, "h_hi1", [P, C, PAIR, P], F32R)
    h_lo = sb(ctx, "h_lo1", [P, C, PAIR, P], F32R)
    y_out = sb(ctx, "y_out", [P, PAIR, D])
    stats = sb(ctx, "stats1", [P, PAIR, 6])
    stats_y = sb(ctx, "stats_y1", [P, PAIR, 6])
    mv = sb(ctx, "mv1", [P, PAIR, 2])
    mv_y = sb(ctx, "mv_y1", [P, PAIR, 2])
    ve = sb(ctx, "ve1", [P, PAIR])
    ve_y = sb(ctx, "ve_y1", [P, PAIR])
    rstd = sb(ctx, "rstd1", [P, PAIR])
    rstd_y = sb(ctx, "rstd_y1", [P, PAIR])
    gains = sb(ctx, "gains1", [P, 2, C, PAIR])
    mask_now = sb(ctx, "mask_now1", [P, PAIR])
    seen = sb(ctx, "seen1", [P, 1])

    s = {n: sem("l1_" + n) for n in (
        "preset", "rows_preset", "x_in", "stats", "var", "var_eps", "rstd", "xn", "xT_ps", "xT_hi", "xT_lo", "masks",
        "qk_ps", "qk_hi", "qk_lo", "stack", "v_ps", "v", "s_ps", "top", "top_ps", "top_T",
        "shift0", "shift1", "w_ps", "prob", "y_ps", "p_sum", "y", "y_stats", "y_var", "y_var_eps", "y_rstd", "z",
        "z_ps", "gains", "g", "tanh", "silu", "h_hi", "h_lo0", "h_lo1", "o_ps", "out", "stored")}
    STACK_DMAS = HC * 3 + 1
    QK_BANKS = ((2, 3), (0, 1))
    W_BANKS = (4, 5, 6, 7)
    Y_BANKS = ((4, 5), (6, 7))
    V_BANKS = (0, 1)
    S_BANKS = (0, 1, 2, 3)
    Z_BANKS = (4, 5)
    O_BANKS = (4, 5)
    X_BANKS = (7, 6)
    T_BANKS = (7, 6)
    Z_AFTER = 10

    block = ctx.enter_context(nc.Block())

    @block.sync
    def _(sp):
        def load(pair, slot):
            sp.dma_start(xr[:, slot], x1_d[bass.ds(pair * PAIR, PAIR)].rearrange("b t d -> t b d")).then_inc(s["x_in"], 16)

        load(0, 0)
        load(1, 1)
        sp.wait_ge(s["rows_preset"], 1)

        def restack(i, first):
            if not first:
                sp.wait_ge(s["w_ps"], seq(PAIR * C, i - 1, PAIR * C))
            sp.dma_start(f32(stack[ROW_MASK:ROW_MASK + 2, 1]).rearrange("r a c b t -> r (a c) (b t)"),
                         mask_d[1, :, bass.ds(i * PAIR, PAIR)].rearrange("r b t -> r (b t)").unsqueeze(1)
                         .broadcast_to([2, H, PAIR * P])).then_inc(s["stack"], 16)
            sp.wait_ge(s["qk_lo"], seq(2 * C, i, 2 * C))
            for a in range(HC):
                rows = slice(DH * a, DH * a + DH)
                for r, (q, k) in enumerate(((Q_HI, K_HI), (Q_LO, K_HI), (Q_HI, K_LO))):
                    sp.dma_start(f32(stack[DH * r:DH * r + DH, :, a]),
                                 f32(parts[rows, q:k + 1:k - q])).then_inc(s["stack"], 16)

        def store(prev, b):
            sp.wait_ge(s["out"], seq(PAIR, prev + 1, b + 1))
            sp.dma_start(out[prev * PAIR + b], y_out[:, b]).then_inc(s["stored"], 16)

        def body(i, first, more, last):
            restack(i, first)
            if not first:
                store(i - 1, 0)
                store(i - 1, 1)
                sp.wait_ge(s["stored"], seq(16 * PAIR, i - 1, 16 * PAIR))
            if more:
                sp.wait_ge(s["x_in"], seq(16, i, 32))
                load(i + 2, (i + 2) % RING)

        bodies(sp, NP, body)
        store(NP - 1, 0)
        store(NP - 1, 1)
        sp.wait_ge(s["stored"], seq(16 * PAIR, NP - 1, 16 * PAIR))

    @block.gpsimd
    def _(pool):
        def end_rstd(prev, b):
            pool.wait_ge(s["y_var"], seq(PAIR, prev, b + 1))
            nc.gpsimd.tensor_tensor(ve_y[:, b:b + 1], mv_y[:, b, 1:2], eps[:, 0:1], ALU.add).then_inc(s["y_var_eps"], 1)
            pool.wait_ge(s["y_var_eps"], seq(PAIR, prev, b + 1))
            nc.gpsimd.tensor_tensor(rstd_y[:, b:b + 1], ve_y[:, b:b + 1], neg_half[:, 0:1],
                                    ALU.pow).then_inc(s["y_rstd"], 1)

        def end_gains(prev):
            nc.gpsimd.tensor_copy(gains[:, 0], half_gain[:, 1, :, bass.ds(prev * PAIR, PAIR)])
            nc.gpsimd.tensor_copy(gains[:, 1], half_shift[:, 1, :, bass.ds(prev * PAIR, PAIR)]).then_inc(s["gains"], 1)

        def norm(pair):
            pool.wait_ge(s["var"], seq(1, pair, 1))
            nc.gpsimd.tensor_tensor(ve[:], mv[:, :, 1], eps[:], ALU.add).then_inc(s["var_eps"], 1)
            pool.wait_ge(s["var_eps"], seq(1, pair, 1))
            nc.gpsimd.tensor_tensor(rstd[:], ve[:], neg_half[:], ALU.pow).then_inc(s["rstd"], 1)

        def low_part(prev, b):
            pool.wait_ge(s["h_hi"], seq(PAIR, prev, b + 1))
            nc.gpsimd.tensor_tensor(h_lo[:, :, b, :], hs[:, b], f32(h_hi[:, :, b, :]),
                                    ALU.subtract).then_inc(s["h_lo1"], 1)

        norm(0)
        pool.wait_ge(s["rstd"], 1)
        nc.gpsimd.memset(f32(stack[ROW_MASK:ROW_MASK + 3]), 1.0).then_inc(s["rows_preset"], 1)
        pool.wait_ge(s["rows_preset"], 1)

        def body(i, first, more, last):
            if not last:
                norm(i + 1)
            if not first:
                end_rstd(i - 1, 0)
                end_gains(i - 1)
                end_rstd(i - 1, 1)
                low_part(i - 1, 1)

        bodies(pool, NP, body)
        end_rstd(NP - 1, 0)
        end_gains(NP - 1)
        end_rstd(NP - 1, 1)
        low_part(NP - 1, 1)

    @block.vector
    def _(dve):
        nc.vector.memset(v[:], 1.0).then_inc(s["preset"], 1)
        nc.vector.memset(seen[:], 0.0).then_inc(s["out"], PAIR)

        def row_stats(pair, slot):
            dve.wait_ge(s["x_in"], seq(16, pair, 16) if not isinstance(pair, int) or pair > 0 else 32)
            for b in range(PAIR):
                nc.vector.bn_stats(stats[:, b], xr[:, slot, b]).then_inc(s["stats"], 1)
            dve.wait_ge(s["stats"], seq(PAIR, pair, PAIR))
            nc.vector.tensor_copy(seen[:], eps[:, 0:1])
            for b in range(PAIR):
                last = nc.vector.bn_aggr(mv[:, b], stats[:, b])
            last.then_inc(s["var"], 1)

        def norm(pair, slot):
            dve.wait_ge(s["rstd"], seq(1, pair, 1))
            for b in range(PAIR):
                nc.vector.tensor_scalar(xn[:, b], xr[:, slot, b], mv[:, b, 0:1], rstd[:, b:b + 1], ALU.subtract,
                                        ALU.mult).then_inc(s["xn"], 1)

        def x_low(pair, b):
            dve.wait_ge(s["xT_hi"], seq(PAIR, pair, b + 1))
            nc.vector.tensor_tensor(xT_lo[:, :, b, :], ps[X_BANKS[b]][:, :].rearrange("p (c t) -> p c t", c=C),
                                    f32(xT_hi[:, :, b, :]), ALU.subtract).then_inc(s["xT_lo"], 1)

        def qk_low(i, n):
            for c in range(C):
                if c % 2 == 0:
                    dve.wait_ge(s["qk_hi"], seq(2 * C, i, (1 - n) * C + c + 2))
                at = (c % 2) * PAIR * P
                nc.vector.scalar_tensor_tensor(
                    parts[:, LO[n], c].rearrange("p b t -> p (b t)"), ps[QK_BANKS[n][c // 2]][:, at:at + PAIR * P],
                    qk_bias[:, n, c:c + 1], f32(parts[:, HI[n], c]).rearrange("p b t -> p (b t)"), ALU.add,
                    ALU.subtract).then_inc(s["qk_lo"], 1)

        def maxima(i, b, banks):
            for j in banks:
                dve.wait_ge(s["s_ps"], seq(PAIR * C, i, b * C + j + 1))
                nc.vector.tensor_reduce(top[:, b, :].rearrange("p (a c) -> p a c", c=C)[:, :, j],
                                        ps[S_BANKS[j]][:, :].rearrange("p (h t) -> p h t", h=HB), AX_X, ALU.max,
                                        negate=True).then_inc(s["top"], 1)

        def end_outputs(prev, b):
            banks = Y_BANKS[b]
            dve.wait_ge(s["y_ps"], seq(PAIR, prev, b + 1))
            for j in range(2):
                a = ps[banks[j]][:, 0:HY * DV].rearrange("p (h d) -> p h d", h=HY)
                last = nc.vector.reciprocal(p_sum[:, b, HY * j:HY * j + HY], a[:, :, DH])
            last.then_inc(s["p_sum"], 1)
            dve.wait_ge(s["p_sum"], seq(PAIR, prev, b + 1))
            for j in range(2):
                a = ps[banks[j]][:, 0:HY * DV].rearrange("p (h d) -> p h d", h=HY)
                last = nc.vector.tensor_tensor(
                    z[:, b, HY * DH * j:HY * DH * (j + 1)].rearrange("p (h d) -> p h d", h=HY), a[:, :, 0:DH],
                    p_sum[:, b, HY * j:HY * j + HY].unsqueeze(2).broadcast_to([P, HY, DH]), ALU.mult)
            last.then_inc(s["y"], 1)
            dve.wait_ge(s["y"], seq(PAIR, prev, b + 1))
            nc.vector.bn_stats(stats_y[:, b], z[:, b]).then_inc(s["y_stats"], 1)
            dve.wait_ge(s["y_stats"], seq(PAIR, prev, b + 1))
            nc.vector.tensor_copy(seen[:], eps[:, 0:1])
            nc.vector.bn_aggr(mv_y[:, b], stats_y[:, b]).then_inc(s["y_var"], 1)

        def end_norm(prev, b):
            dve.wait_ge(s["y_rstd"], seq(PAIR, prev, b + 1))
            nc.vector.tensor_scalar(z[:, b], z[:, b], mv_y[:, b, 0:1], rstd_y[:, b:b + 1], ALU.subtract,
                                    ALU.mult).then_inc(s["z"], 1)

        def end_silu(prev, b):
            dve.wait_ge(s["tanh"], seq(PAIR, prev, b + 1))
            nc.vector.scalar_tensor_tensor(hs[:, b], th[:, b], 1.0, g[:, b], ALU.add, ALU.mult).then_inc(s["silu"], 1)

        def low_part(prev, b):
            dve.wait_ge(s["h_hi"], seq(PAIR, prev, b + 1))
            nc.vector.tensor_tensor(h_lo[:, :, b, :], hs[:, b], f32(h_hi[:, :, b, :]),
                                    ALU.subtract).then_inc(s["h_lo0"], 1)

        def end_add(prev, slot, b):
            if isinstance(prev, int) and prev > 0:
                dve.wait_ge(s["stored"], seq(16 * PAIR, prev - 1, 16 * PAIR))
            dve.wait_ge(s["o_ps"], seq(PAIR, prev, b + 1))
            nc.vector.tensor_tensor(y_out[:, b], ps[O_BANKS[b]][:, :], xr[:, slot, b], ALU.add).then_inc(s["out"], 1)

        row_stats(0, 0)
        norm(0, 0)
        x_low(0, 0)
        x_low(0, 1)

        def body(i, first, more, last):
            qk_low(i, 1)
            if not last:
                row_stats(i + 1, (i + 1) % RING)
            qk_low(i, 0)
            if not first:
                end_outputs(i - 1, 0)
            if not last:
                norm(i + 1, (i + 1) % RING)
            if not first:
                end_norm(i - 1, 0)
                end_outputs(i - 1, 1)
                end_silu(i - 1, 0)
                end_norm(i - 1, 1)
                low_part(i - 1, 0)
            maxima(i, 0, (0,))
            if not first:
                end_silu(i - 1, 1)
            maxima(i, 0, (1, 2))
            if not last:
                x_low(i + 1, 0)
            maxima(i, 0, (3,))
            if not first:
                end_add(i - 1, (i - 1) % RING, 0)
            maxima(i, 1, (0,))
            if not last:
                x_low(i + 1, 1)
            maxima(i, 1, (1, 2, 3))
            if not first:
                end_add(i - 1, (i - 1) % RING, 1)

        bodies(dve, NP, body)
        for b in range(PAIR):
            end_outputs(NP - 1, b)
            end_norm(NP - 1, b)
        for b in range(PAIR):
            end_silu(NP - 1, b)
        low_part(NP - 1, 0)
        for b in range(PAIR):
            end_add(NP - 1, (NP - 1) % RING, b)

    @block.scalar
    def _(act):
        def x_high(pair, b):
            act.wait_ge(s["xT_ps"], seq(PAIR, pair, b + 1))
            nc.scalar.activation(xT_hi[:, :, b, :], ps[X_BANKS[b]][:, :].rearrange("p (c t) -> p c t", c=C),
                                 ACT.Copy).then_inc(s["xT_hi"], 1)

        def qk_high(i, n, chunks):
            for c in chunks:
                if c % 2 == 0:
                    act.wait_ge(s["qk_ps"], seq(C, i, (1 - n) * 2 + c // 2 + 1))
                at = (c % 2) * PAIR * P
                nc.scalar.activation(parts[:, HI[n], c].rearrange("p b t -> p (b t)"),
                                     ps[QK_BANKS[n][c // 2]][:, at:at + PAIR * P], ACT.Identity,
                                     bias=qk_bias[:, n, c:c + 1]).then_inc(s["qk_hi"], 1)

        def exps(prev, b):
            for j in range(C):
                act.wait_ge(s["w_ps"], seq(PAIR * C, prev, b * C + j + 1))
                nc.scalar.activation(prob[:, b, HB * j:HB * j + HB, :],
                                     ps[W_BANKS[j]][:, :].rearrange("p (h t) -> p h t", h=HB),
                                     ACT.Exp).then_inc(s["prob"], 1)

        def values(i, b, first):
            act.wait_ge(s["v_ps"], seq(PAIR, i, b + 1))
            if not first:
                act.wait_ge(s["y_ps"], seq(PAIR, i - 1, b + 1))
            nc.scalar.activation(v[:, b, :, 0:DH], ps[V_BANKS[b]][:, :].rearrange("p (h d) -> p h d", h=H), ACT.Copy,
                                 scale=mask_now[:, b:b + 1]).then_inc(s["v"], 1)

        def gate(prev, b):
            if b == 0:
                act.wait_ge(s["gains"], seq(1, prev, 1))
            act.wait_ge(s["z_ps"], seq(PAIR, prev, b + 1))
            for c in range(C):
                last = nc.scalar.activation(g[:, b, c, :], ps[Z_BANKS[b]][:, c * P:(c + 1) * P], ACT.Identity,
                                            scale=gains[:, 0, c, b:b + 1], bias=gains[:, 1, c, b:b + 1])
            last.then_inc(s["g"], 1)

        def tanh(prev, b):
            act.wait_ge(s["g"], seq(PAIR, prev, b + 1))
            nc.scalar.activation(th[:, b], g[:, b], ACT.Tanh).then_inc(s["tanh"], 1)

        def h_high(prev, b):
            act.wait_ge(s["silu"], seq(PAIR, prev, b + 1))
            nc.scalar.activation(h_hi[:, :, b, :], hs[:, b], ACT.Copy).then_inc(s["h_hi"], 1)

        def shift_out(i, b):
            act.wait_ge(s["top_ps"], seq(PAIR, i, b + 1))
            nc.scalar.activation(top_T[:, b, :], ps[T_BANKS[b]][0:H, 0:P], ACT.Copy).then_inc(s["top_T"], 1)
            act.wait_ge(s["top_T"], seq(PAIR, i, b + 1))
            act.dma_start(f32(stack[ROW_SHIFT:ROW_SHIFT + 1, 0, :, :, b, :]).rearrange("o a c t -> o (a c) t"),
                          f32(top_T[:, b, :])).then_inc(s[f"shift{b}"], 16)

        x_high(0, 0)
        x_high(0, 1)

        def body(i, first, more, last):
            nc.scalar.activation(mask_now[:], mask_col[:, 1, bass.ds(i * PAIR, PAIR)], ACT.Copy).then_inc(s["masks"], 1)
            if not first:
                shift_out(i - 1, 1)
            qk_high(i, 1, (0, 1))
            if not first:
                exps(i - 1, 0)
            qk_high(i, 1, (2, 3))
            if not first:
                exps(i - 1, 1)
            qk_high(i, 0, range(C))
            if not first:
                gate(i - 1, 0)
                tanh(i - 1, 0)
            act.wait_ge(s["masks"], seq(1, i, 1))
            if first:
                act.wait_ge(s["preset"], 1)
            values(i, 0, first)
            if not first:
                h_high(i - 1, 0)
            values(i, 1, first)
            if not first:
                gate(i - 1, 1)
                tanh(i - 1, 1)
                h_high(i - 1, 1)
            if not last:
                x_high(i + 1, 0)
                x_high(i + 1, 1)
            shift_out(i, 0)

        bodies(act, NP, body)
        shift_out(NP - 1, 1)
        exps(NP - 1, 0)
        exps(NP - 1, 1)
        for b in range(PAIR):
            gate(NP - 1, b)
            tanh(NP - 1, b)
        for b in range(PAIR):
            h_high(NP - 1, b)

    @block.tensor
    def _(pe):
        def x_transposed(pair, b, first):
            pe.wait_ge(s["xn"], seq(PAIR, pair, b + 1))
            if not first:
                pe.wait_ge(s["y"], seq(PAIR, pair - 2, PAIR))
            for c in range(C):
                last = nc.tensor.transpose(ps[X_BANKS[b]][:, c * P:(c + 1) * P], xn[:, b, c * P:(c + 1) * P], ident[:])
            last.then_inc(s["xT_ps"], 1)

        def z_transposed(prev, b):
            pe.wait_ge(s["z"], seq(PAIR, prev, b + 1))
            for c in range(C):
                last = nc.tensor.transpose(ps[Z_BANKS[b]][:, c * P:(c + 1) * P], z[:, b, c * P:(c + 1) * P], ident[:])
            last.then_inc(s["z_ps"], 1)

        def out_rows(prev, b):
            pe.wait_ge(s[f"h_lo{b}"], seq(1, prev, 1))
            done = None
            for done in project_rows(nc, w_hi, w_lo, O, h_hi, h_lo, b, ps[O_BANKS[b]], C, ones,
                                     bias_rows[:, BO, :]):
                yield
            done.then_inc(s["o_ps"], 1)

        def projected(i, n, chunks):
            for f in chunks:
                dst = ps[QK_BANKS[n][f // 2]][:, (f % 2) * PAIR * P:(f % 2 + 1) * PAIR * P]
                done = None
                for done in project_features(nc, w_hi, w_lo, n, f, xT_hi, xT_lo, dst, C, True):
                    yield
                if f % 2:
                    done.then_inc(s["qk_ps"], 1)

        def value_rows(i, b):
            pe.wait_ge(s["qk_lo"], seq(2 * C, i, 2 * (b + 1)))
            done = None
            for done in project_rows(nc, w_hi, w_lo, V, xT_hi, xT_lo, b, ps[V_BANKS[b]], C, ones,
                                     bias_rows[:, BV, :]):
                yield
            done.then_inc(s["v_ps"], 1)

        def weight_scores(prev, b):
            pe.wait_ge(s[f"shift{b}"], seq(16, prev, 16))
            for j in range(C):
                if b == 0 and j < 2:
                    pe.wait_ge(s["out"], seq(PAIR, prev, j + 1))
                if b == 0 and j == 2:
                    pe.wait_ge(s["top_T"], seq(PAIR, prev, PAIR))
                if b == 1:
                    pe.wait_ge(s["prob"], seq(PAIR * C, prev, j + 1))
                for a in range(HC):
                    last = nc.tensor.matmul(ps[W_BANKS[j]][:, a * P:(a + 1) * P], stack[0:K_SHIFTED, 1, a, j, b, :],
                                            stack[0:K_SHIFTED, 0, a, j, b, :], start=True, stop=True)
                last.then_inc(s["w_ps"], 1)

        def mixed(prev, b):
            pe.wait_ge(s["prob"], seq(PAIR * C, prev, C + 2 * (b + 1)))
            for h in range(H):
                j, a = h // HY, h % HY
                last = nc.tensor.matmul(ps[Y_BANKS[b][j]][:, a * DV:(a + 1) * DV], prob[:, b, h, :], v[:, b, h, :],
                                        start=True, stop=True)
                yield
            last.then_inc(s["y_ps"], 1)

        def scores(i, b, banks):
            if b == 0 and banks[0] == 0:
                pe.wait_ge(s["stack"], seq(16 * STACK_DMAS, i, 16 * STACK_DMAS))
            for j in banks:
                if b == 0 and j < 2:
                    pe.wait_ge(s["v"], seq(PAIR, i, j + 1))
                if b == 1:
                    pe.wait_ge(s["top"], seq(PAIR * C, i, j + 1))
                for a in range(HC):
                    last = nc.tensor.matmul(ps[S_BANKS[j]][:, a * P:(a + 1) * P], stack[0:K_SCORE, 0, a, j, b, :],
                                            stack[0:K_SCORE, 1, a, j, b, :], start=True, stop=True)
                    if a == HC - 1:
                        last.then_inc(s["s_ps"], 1)
                    if a % 2:
                        yield

        def shift_row(i, b):
            pe.wait_ge(s["top"], seq(PAIR * C, i, C * (b + 1)))
            nc.tensor.transpose(ps[T_BANKS[b]][0:H, 0:P], top[:, b, :], ident[:]).then_inc(s["top_ps"], 1)

        x_transposed(0, 0, True)
        x_transposed(0, 1, True)

        def body(i, first, more, last):
            pe.wait_ge(s["xT_lo"], seq(PAIR, i, PAIR))
            for f in range(C):
                if not first and f % 2 == 0:
                    pe.wait_ge(s["top"], seq(PAIR * C, i - 1, C + f // 2 + 1))
                run(projected(i, 1, (f,)))
                if not first and f == 0:
                    shift_row(i - 1, 1)
                if not first and f % 2:
                    weight_scores(i - 1, f // 2)
            run(projected(i, 0, (0, 1)))
            if first:
                run(projected(i, 0, (2, 3)))
            else:
                woven(several(2, projected(i, 0, (2, 3))), mixed(i - 1, 0))
            outputs1, values0 = () if first else mixed(i - 1, 1), value_rows(i, 0)
            woven(outputs1, values0, Z_AFTER)
            if not first:
                z_transposed(i - 1, 0)
            woven(outputs1, values0)
            run(value_rows(i, 1))
            if not last:
                x_transposed(i + 1, 0, first)
                x_transposed(i + 1, 1, first)
            if not first:
                z_transposed(i - 1, 1)
            else:
                pe.wait_ge(s["preset"], 1)
            outputs0 = () if first else out_rows(i - 1, 0)
            run(islice(outputs0, 3))
            woven(outputs0, scores(i, 0, range(C)))
            outputs1, scores1 = () if first else out_rows(i - 1, 1), scores(i, 1, range(C))
            woven(outputs1, scores1, 6)
            if not last:
                pe.wait_ge(s["xT_lo"], seq(PAIR, i + 1, 1))
            shift_row(i, 0)
            woven(outputs1, scores1)

        bodies(pe, NP, body)
        shift_row(NP - 1, 1)
        for b in range(PAIR):
            weight_scores(NP - 1, b)
        for b in range(PAIR):
            run(mixed(NP - 1, b))
        for b in range(PAIR):
            z_transposed(NP - 1, b)
        for b in range(PAIR):
            run(out_rows(NP - 1, b))


_INS = ["x", "cond_2048", "mask_BxSx1_fk1", "mask_BxS_ff1", "L0_cond_ln_w", "L0_cond_ln_b", "L0_cond_Wq",
        "L0_cond_bq", "L0_cond_Wk", "L0_cond_bk", "L0_cond_Wv", "L0_cond_bv", "L0_cond_W_emb", "L0_cond_b_emb",
        "L0_cond_ln2_w", "L0_cond_ln2_b", "L0_cond_W_out", "L0_cond_b_out", "L1_cond_norm_w", "L1_cond_norm_b",
        "L1_cond_q_w", "L1_cond_q_b", "L1_cond_k_w", "L1_cond_k_b", "L1_cond_v_w", "L1_cond_v_b",
        "L1_cond_emb_w", "L1_cond_emb_b", "L1_cond_sb_norm_w", "L1_cond_sb_norm_b", "L1_cond_out_w",
        "L1_cond_out_b"]


def kernel(**inputs):
    import numpy as _np
    import concourse.bacc as _bacc
    from concourse import mybir as _mybir
    from concourse.bass_utils import run_bass_kernel_spmd as _run

    nc = _bacc.Bacc("TRN2", target_bir_lowering=False, num_devices=1)
    arrays, tensors = {}, {}
    for name in _INS:
        a = _np.ascontiguousarray(inputs[name])
        arrays[f"in_{name}"] = a
        tensors[name] = nc.dram_tensor(f"in_{name}", a.shape, _mybir.dt.from_np(a.dtype), kind="ExternalInput").ap()
    out = nc.dram_tensor("out", inputs["x"].shape, _mybir.dt.float32, kind="ExternalOutput").ap()
    build(nc, tensors, out)
    r = _run(nc, [arrays], core_ids=[0])
    return r.results[0]["out"]
```

```python
from contextlib import ExitStack
from itertools import islice, zip_longest

import concourse.bass as bass
from concourse import mybir

F32 = mybir.dt.float32
F32R = mybir.dt.float32r
ALU = mybir.AluOpType
ACT = mybir.ActivationFunctionType
AX_X = mybir.AxisListType.X

P = 128
PAIR = 2
RING = 3
BIG = -1000000.0
EPS = 1e-5

ROW_MASK = 96
ROW_SHIFT = 98
K_SCORE = 98
K_SHIFTED = 99


def load_rows(sp, x, xr, pair, slot, arrived):
    sp.dma_start(xr[:, slot], x[bass.ds(pair * PAIR, PAIR)].rearrange("b t d -> t b d")).then_inc(arrived, 16)


def seq(per, pair, k):
    return pair * per + k


def f32(ap):
    return ap.bitcast(F32)


def build(nc, T, out):
    x_d, cond_d = T["x"], T["cond_2048"]
    B, S, D = x_d.shape
    TE = cond_d.shape[1]
    NP = B // PAIR
    C = D // P
    H0, H1 = 8, 16
    HC = H1 // C
    D0, D1 = D // H0, D // H1
    KE = TE // P
    assert S == P and D1 == 32 and D0 == 64 and NP > 4

    x1_d = nc.dram_tensor("x_between_layers", [B, S, D], F32).ap()
    mask_d = nc.dram_tensor("mask_parts", [2, 2, B, S], F32).ap()

    root = ExitStack()
    with root:
        def sem(name):
            return root.enter_context(nc.semaphore(name))

        def sb(ctx, name, shape, dt=F32):
            return ctx.enter_context(nc.sbuf_tensor(name, shape, dt))

        ps = [root.enter_context(nc.psum_tensor(f"bank{i}", [P, 512], F32)) for i in range(8)]

        w_hi = sb(root, "w_hi", [P, 4, C, D], F32R)
        w_lo = sb(root, "w_lo", [P, 4, C, D], F32R)
        ident = sb(root, "ident", [P, P])
        ones = sb(root, "ones", [1, P])
        bias_all = sb(root, "bias_all", [P, 3, D])
        half_gain = sb(root, "half_gain", [P, 2, C, B])
        half_shift = sb(root, "half_shift", [P, 2, C, B])
        vec = sb(root, "vec", [P, 64])
        mask_col = sb(root, "mask_col", [P, 2, B])
        qk_bias = sb(root, "qk_bias", [P, 2, C])
        xr = sb(root, "xr", [P, RING, PAIR, D])
        x_in = [sem("l0_x_in"), sem("l1_x_in")]
        eps = sb(root, "eps", [P, 2])
        neg_half = sb(root, "neg_half", [P, 2])

        vec_rows = {}
        at = 0
        for name in ("L0_cond_ln_w", "L0_cond_ln_b", "L0_cond_ln2_w", "L0_cond_ln2_b", "L0_cond_b_emb",
                     "L1_cond_norm_w", "L1_cond_norm_b", "L1_cond_sb_norm_w", "L1_cond_sb_norm_b",
                     "L1_cond_emb_b", "L1_cond_q_b", "L1_cond_k_b"):
            n = T[name].shape[0] // P
            vec_rows[name] = (at, n)
            at += n
        n_vec = at

        def vcol(name, c):
            r = vec_rows[name][0] + c
            return vec[:, r:r + 1]

        mats = [[("L0_cond_Wq", "L0_cond_bq"), ("L0_cond_Wk", "L0_cond_bk"), ("L0_cond_Wv", "L0_cond_bv"),
                 ("L0_cond_W_out", "L0_cond_b_out")],
                [("L1_cond_q_w", "L1_cond_q_b"), ("L1_cond_k_w", "L1_cond_k_b"), ("L1_cond_v_w", "L1_cond_v_b"),
                 ("L1_cond_out_w", "L1_cond_out_b")]]
        raw1_in = [sem(f"raw1_in{n}") for n in range(4)]
        bias1_ps, stored0 = sem("bias1_ps"), sem("l0_stored")

        with ExitStack() as both:
            raw1 = [sb(both, f"raw1_{n}", [P, C, D]) for n in range(4)]
            with ExitStack() as ctx:
                key_bias = sb(ctx, "key_bias", [P, D], F32R)
                setup(nc, mats[0], T, sem, sb, ps, ident, ones, w_hi, w_lo, bias_all, key_bias, half_gain,
                      half_shift, vec, vec_rows, n_vec, vcol, mask_col, mask_d, eps, neg_half, x_d, xr, x_in[0],
                      B, D, C, KE)
                layer0(nc, ctx, sem, sb, ps, x_d, x1_d, xr, x_in[0], w_hi, w_lo, ident, bias_all, key_bias,
                       half_gain, half_shift, mask_col, mask_d, eps, neg_half,
                       [T[w] for w, _ in mats[1]], raw1, raw1_in, bias1_ps,
                       [vcol("L1_cond_norm_b", c) for c in range(C)], stored0, B, NP, D, C, H0, D0)
            second_weights(nc, mats[1], T, sem, sb, ps, w_hi, w_lo, raw1, raw1_in, ones, bias_all, qk_bias, vec,
                           vec_rows, vcol, x1_d, xr, x_in[1], bias1_ps, stored0, B, D, C)

        with ExitStack() as ctx:
            layer1(nc, ctx, sem, sb, ps, x1_d, out, xr, x_in[1], w_hi, w_lo, ident, bias_all, qk_bias,
                   half_gain, half_shift, mask_col, mask_d, eps, neg_half, B, NP, D, C, HC, H1, D1)


def high_part(nc, w_hi, raw, n, C, gain):
    if gain is None:
        return nc.scalar.activation(w_hi[:, n], raw[n][:], ACT.Copy)
    for c in range(C):
        last = nc.scalar.activation(w_hi[:, n, c, :], raw[n][:, c, :], ACT.Copy, scale=gain(c))
    return last


def low_part_of(nc, w_hi, w_lo, raw, n, C, gain):
    if gain is None:
        return nc.vector.tensor_tensor(w_lo[:, n], raw[n][:], f32(w_hi[:, n]), ALU.subtract)
    for c in range(C):
        last = nc.vector.scalar_tensor_tensor(w_lo[:, n, c, :], raw[n][:, c, :], gain(c), f32(w_hi[:, n, c, :]),
                                              ALU.mult, ALU.subtract)
    return last


def setup(nc, mats, T, sem, sb, ps, ident, ones, w_hi, w_lo, bias_all, key_bias, half_gain, half_shift,
          vec, vec_rows, n_vec, vcol, mask_col, mask_d, eps, neg_half, x_d, xr, x_in, B, D, C, KE):
    with ExitStack() as ctx:
        vec_in = sb(ctx, "vec_in", [2 * C, P])
        vec_in2 = sb(ctx, "vec_in2", [n_vec - 2 * C, P])
        mask_in = sb(ctx, "mask_in", [B, 2, P])
        mask_top = sb(ctx, "mask_top", [B, 2])
        mask_hi = sb(ctx, "mask_hi", [B, 2, P], F32R)
        mask_lo = sb(ctx, "mask_lo", [B, 2, P], F32R)
        cond = sb(ctx, "cond", [B, KE * P])
        cond_tanh = sb(ctx, "cond_tanh", [B, KE * P])
        cond_T = sb(ctx, "cond_T", [P, KE, B])
        raw = [sb(ctx, f"raw0_{n}", [P, C, D]) for n in range(4)]
        bias_in = sb(ctx, "bias_in0", [1, 4, D])
        EMB_RING, EMB_PARTS = 3, 8
        DE = 2 * 2 * D // EMB_PARTS
        w_emb = sb(ctx, "w_emb", [P, EMB_RING, KE, DE])
        one_scale = sb(ctx, "one_scale", [P, 2, C, B])
        shift = sb(ctx, "shift", [P, 2, C, B])

        small_in, small_in2 = sem("small_in"), sem("small_in2")
        bias_loaded = sem("bias_loaded0")
        raw_in = [sem(f"raw_in0_{n}") for n in range(4)]
        emb_in = [sem(f"emb_in{q}") for q in range(EMB_PARTS)]
        zeroed, cleared = sem("zeroed"), sem("cleared0")
        ident_ready = sem("ident_ready")
        consts_ready = sem("consts_ready")
        vec_ps, vec_ready = sem("vec_ps"), sem("vec_ready")
        mask_ps, mask_step, mask_out = sem("mask_ps"), sem("mask_step"), sem("mask_out")
        tanh_ready, cond_step = sem("tanh_ready"), sem("cond_step")
        cond_ps, cond_ready = sem("cond_ps"), sem("cond_ready")
        bias_ps, bias_step, split = sem("bias_ps0"), sem("bias_step0"), sem("split0")
        bias_all_ps = sem("bias_all_ps0")
        emb_ps, emb_step = sem("emb_ps"), sem("emb_step")
        BIAS_BANKS = (3, 6, 7)
        off = vec_rows["L0_cond_ln_b"][0]
        def gain(n):
            return None if n == 3 else lambda c: vcol("L0_cond_ln_w", c)

        loads = [(cond[:], T["cond_2048"]),
                 (mask_in[:, 0, :], T["mask_BxSx1_fk1"].rearrange("b s o -> b (s o)")),
                 (mask_in[:, 1, :], T["mask_BxS_ff1"])]
        loads2 = []
        for name, (r, n) in vec_rows.items():
            if r < 2 * C:
                loads.append((vec_in[r:r + n, :], T[name].rearrange("(c p) -> c p", p=P)))
            else:
                loads2.append((vec_in2[r - 2 * C:r - 2 * C + n, :], T[name].rearrange("(c p) -> c p", p=P)))

        block = ctx.enter_context(nc.Block())

        @block.sync
        def _(sp):
            for dst, src in loads:
                sp.dma_start(dst, src).then_inc(small_in, 16)
            for n, (w, b) in enumerate(mats):
                sp.dma_start(raw[n][:], T[w].rearrange("(c p) n -> p c n", p=P)).then_inc(raw_in[n], 16)
            for n, (w, b) in enumerate(mats):
                sp.dma_start(bias_in[:, n, :], T[b].rearrange("(o d) -> o d", o=1)).then_inc(bias_loaded, 16)
            for dst, src in loads2:
                sp.dma_start(dst, src).then_inc(small_in2, 16)
            for q in range(EMB_PARTS):
                name = ("L0_cond_W_emb", "L1_cond_emb_w")[q // 4]
                if q >= EMB_RING:
                    sp.wait_ge(emb_ps, q - EMB_RING + 1)
                sp.dma_start(w_emb[:, q % EMB_RING],
                             T[name][:, (q % 4) * DE:(q % 4 + 1) * DE].rearrange("(k p) n -> p k n", p=P))\
                    .then_inc(emb_in[q], 16)
            for pair in range(2):
                load_rows(sp, x_d, xr, pair, pair, x_in)
            sp.wait_ge(mask_step, 6)
            for n, part in enumerate((mask_hi, mask_lo)):
                sp.dma_start(mask_d[:, n].rearrange("l b t -> b l t"), f32(part[:])).then_inc(mask_out, 16)
            sp.wait_ge(mask_out, 32)

        @block.gpsimd
        def _(pool):
            nc.gpsimd.memset(ident[:], 0.0).then_inc(zeroed, 1)
            pool.wait_ge(zeroed, 1)
            nc.gpsimd.affine_select(out=ident[:], in_=ident[:], compare_op=ALU.not_equal, fill=1.0, base=0,
                                    pattern=[[-1, P]], channel_multiplier=1).then_inc(ident_ready, 1)
            nc.gpsimd.memset(eps[:], EPS)
            nc.gpsimd.memset(neg_half[:], -0.5)
            nc.gpsimd.memset(ones[:], 1.0).then_inc(consts_ready, 1)
            nc.gpsimd.memset(f32(key_bias[:]), 0.0).then_inc(cleared, 1)
            pool.wait_ge(cleared, 1)
            nc.gpsimd.memset(f32(key_bias[64:65, :]), 1.0)
            nc.gpsimd.memset(f32(key_bias[96:97, :]), 1.0).then_inc(cleared, 1)

        @block.scalar
        def _(act):
            act.wait_ge(small_in, 16 * len(loads))
            nc.scalar.activation(cond_tanh[:], cond[:], ACT.Tanh, scale=0.5).then_inc(tanh_ready, 1)
            act.wait_ge(vec_ps, 1)
            nc.scalar.activation(vec[:, 0:2 * C], ps[0][:, 0:2 * C], ACT.Copy).then_inc(vec_ready, 1)
            act.wait_ge(mask_ps, 1)
            nc.scalar.activation(mask_col[:], ps[1][:, 0:2 * B].rearrange("p (l b) -> p l b", l=2), ACT.Copy)
            act.wait_ge(cond_ps, 1)
            nc.scalar.activation(cond_T[:], ps[2][:, 0:KE * B].rearrange("p (k b) -> p k b", k=KE),
                                 ACT.Copy, scale=0.5).then_inc(cond_ready, 1)
            act.wait_ge(vec_ready, 1)
            for n in range(4):
                act.wait_ge(raw_in[n], 16)
                high_part(nc, w_hi, raw, n, C, gain(n)).then_inc(split, 1)
            act.wait_ge(vec_ps, 2)
            nc.scalar.activation(vec[:, 2 * C:n_vec], ps[0][:, 2 * C:n_vec], ACT.Copy).then_inc(vec_ready, 1)
            for k in range(3):
                act.wait_ge(bias_all_ps, k + 1)
                nc.scalar.activation(bias_all[:, k, :], ps[BIAS_BANKS[k]][:, :], ACT.Copy)

        @block.vector
        def _(dve):
            dve.wait_ge(small_in, 16 * len(loads))
            dve.wait_ge(tanh_ready, 1)
            nc.vector.scalar_tensor_tensor(cond_tanh[:], cond_tanh[:], 1.0, cond[:], ALU.add,
                                           ALU.mult).then_inc(cond_step, 1)
            dve.wait_ge(mask_ps, 1)
            nc.vector.tensor_scalar(mask_in[:], mask_in[:], -1.0, 1.0, ALU.mult, ALU.add).then_inc(mask_step, 1)
            dve.wait_ge(mask_step, 1)
            nc.vector.tensor_scalar(mask_in[:], mask_in[:], BIG, None, ALU.mult).then_inc(mask_step, 1)
            dve.wait_ge(mask_step, 2)
            nc.vector.reduce_max(mask_top[:], mask_in[:], AX_X).then_inc(mask_step, 1)
            dve.wait_ge(mask_step, 3)
            for n in range(2):
                last = nc.vector.tensor_scalar(mask_in[:, n, :], mask_in[:, n, :], mask_top[:, n:n + 1], None,
                                               ALU.subtract)
            last.then_inc(mask_step, 1)
            dve.wait_ge(mask_step, 4)
            nc.vector.tensor_copy(mask_hi[:], mask_in[:]).then_inc(mask_step, 1)
            dve.wait_ge(mask_step, 5)
            nc.vector.tensor_tensor(mask_lo[:], mask_in[:], f32(mask_hi[:]), ALU.subtract).then_inc(mask_step, 1)
            dve.wait_ge(vec_ready, 1)
            for n in range(4):
                dve.wait_ge(split, n + 1)
                low_part_of(nc, w_hi, w_lo, raw, n, C, gain(n))
            dve.wait_ge(bias_loaded, 64)
            dve.wait_ge(cleared, 2)
            for n in range(3):
                dve.wait_ge(bias_ps, n + 1)
                last = nc.vector.tensor_tensor(bias_in[:, n, :], ps[BIAS_BANKS[n]][0:1, :], bias_in[:, n, :], ALU.add)
            last.then_inc(bias_step, 1)
            dve.wait_ge(bias_step, 1)
            nc.vector.tensor_copy(key_bias[0:1, :], bias_in[:, 1, :]).then_inc(bias_step, 1)
            dve.wait_ge(bias_step, 2)
            nc.vector.tensor_tensor(key_bias[32:33, :], bias_in[:, 1, :], f32(key_bias[0:1, :]), ALU.subtract)
            for n, pre in enumerate((("L0_cond_b_emb", "L0_cond_ln2_w", "L0_cond_ln2_b"),
                                     ("L1_cond_emb_b", "L1_cond_sb_norm_w", "L1_cond_sb_norm_b"))):
                be, gw, gb = pre
                dve.wait_ge(vec_ready, 2)
                dve.wait_ge(emb_ps, 4 * (n + 1))
                for c in range(C):
                    nc.vector.tensor_scalar(one_scale[:, n, c, :], ps[4 + n][:, c * B:(c + 1) * B], vcol(be, c),
                                            1.0, ALU.add, ALU.add)
                    last = nc.vector.tensor_scalar(shift[:, n, c, :], ps[4 + n][:, (C + c) * B:(C + c + 1) * B],
                                                   vcol(be, C + c), None, ALU.add)
                last.then_inc(emb_step, 1)
                dve.wait_ge(emb_step, 3 * n + 1)
                for c in range(C):
                    nc.vector.tensor_scalar(half_gain[:, n, c, :], one_scale[:, n, c, :], vcol(gw, c), 0.5,
                                            ALU.mult, ALU.mult)
                    last = nc.vector.scalar_tensor_tensor(shift[:, n, c, :], one_scale[:, n, c, :], vcol(gb, c),
                                                          shift[:, n, c, :], ALU.mult, ALU.add)
                last.then_inc(emb_step, 1)
                dve.wait_ge(emb_step, 3 * n + 2)
                nc.vector.tensor_scalar(half_shift[:, n], shift[:, n], 0.5, None, ALU.mult).then_inc(emb_step, 1)

        @block.tensor
        def _(pe):
            pe.wait_ge(ident_ready, 1)
            pe.wait_ge(small_in, 16 * len(loads))
            nc.tensor.transpose(ps[0][:, 0:2 * C], vec_in[:], ident[0:2 * C, 0:2 * C]).then_inc(vec_ps, 1)
            for n in range(2):
                last = nc.tensor.transpose(ps[1][:, n * B:(n + 1) * B], mask_in[:, n, :], ident[0:B, 0:B])
            last.then_inc(mask_ps, 1)
            pe.wait_ge(cond_step, 1)
            for k in range(KE):
                last = nc.tensor.transpose(ps[2][:, k * B:(k + 1) * B], cond_tanh[:, k * P:(k + 1) * P],
                                           ident[0:B, 0:B])
            last.then_inc(cond_ps, 1)
            pe.wait_ge(vec_ready, 1)
            for n in range(3):
                pe.wait_ge(raw_in[n], 16)
                for c in range(C):
                    last = nc.tensor.matmul(ps[BIAS_BANKS[n]][0:1, :], vec[:, off + c:off + c + 1], raw[n][:, c, :],
                                            start=(c == 0), stop=(c == C - 1))
                last.then_inc(bias_ps, 1)
            pe.wait_ge(small_in2, 16 * len(loads2))
            rest = n_vec - 2 * C
            nc.tensor.transpose(ps[0][:, 2 * C:n_vec], vec_in2[:], ident[0:rest, 0:rest]).then_inc(vec_ps, 1)
            pe.wait_ge(cond_ready, 1)
            for q in range(EMB_PARTS):
                pe.wait_ge(emb_in[q], 16)
                for f in range(DE // P):
                    at = ((q % 4) * (DE // P) + f) * B
                    for k in range(KE):
                        last = nc.tensor.matmul(ps[4 + q // 4][:, at:at + B],
                                                w_emb[:, q % EMB_RING, k, f * P:(f + 1) * P], cond_T[:, k, :],
                                                start=(k == 0), stop=(k == KE - 1))
                last.then_inc(emb_ps, 1)
            pe.wait_ge(bias_step, 1)
            pe.wait_ge(consts_ready, 1)
            for k, n in enumerate((0, 2, 3)):
                nc.tensor.matmul(ps[BIAS_BANKS[k]][:, :], ones[:], bias_in[:, n, :], start=True,
                                 stop=True).then_inc(bias_all_ps, 1)


def second_weights(nc, mats, T, sem, sb, ps, w_hi, w_lo, raw, raw_in, ones, bias_all, qk_bias, vec, vec_rows, vcol,
                   x1_d, xr, x_in, bias_ps, rows_stored, B, D, C):
    with ExitStack() as ctx:
        bias_in = sb(ctx, "bias_in1", [1, 2, D])
        bias_loaded = sem("bias_loaded1")
        bias_step, split = sem("bias_step1"), sem("split1")
        bias_all_ps = sem("bias_all_ps1")
        off = vec_rows["L1_cond_norm_b"][0]

        def gain(n):
            return None if n == 3 else lambda c: vcol("L1_cond_norm_w", c)

        block = ctx.enter_context(nc.Block())

        @block.sync
        def _(sp):
            sp.wait_ge(rows_stored, 16 * B)
            for pair in range(2):
                load_rows(sp, x1_d, xr, pair, pair, x_in)
            for n, (w, b) in enumerate(mats[2:]):
                sp.dma_start(bias_in[:, n, :], T[b].rearrange("(o d) -> o d", o=1)).then_inc(bias_loaded, 16)

        @block.tensor
        def _(pe):
            for c in range(C):
                last = nc.tensor.matmul(ps[4][0:1, :], vec[:, off + c:off + c + 1], raw[2][:, c, :],
                                        start=(c == 0), stop=(c == C - 1))
            last.then_inc(bias_ps, 1)
            pe.wait_ge(bias_step, 1)
            for k in range(2):
                nc.tensor.matmul(ps[5 + k][:, :], ones[:], bias_in[:, k, :], start=True, stop=True)\
                    .then_inc(bias_all_ps, 1)

        @block.scalar
        def _(act):
            for n in (3, 1, 0, 2):
                act.wait_ge(raw_in[n], 16)
                high_part(nc, w_hi, raw, n, C, gain(n)).then_inc(split, 1)
            for k in range(2):
                act.wait_ge(bias_all_ps, k + 1)
                nc.scalar.activation(bias_all[:, 1 + k, :], ps[5 + k][:, :], ACT.Copy)

        @block.gpsimd
        def _(pool):
            pool.wait_ge(raw_in[3], 16)
            pool.wait_ge(split, 1)
            nc.gpsimd.tensor_tensor(w_lo[:, 3], raw[3][:], f32(w_hi[:, 3]), ALU.subtract)

        @block.vector
        def _(dve):
            for n in range(2):
                dve.wait_ge(bias_ps, n + 1)
                r = vec_rows[mats[n][1]][0]
                nc.vector.tensor_tensor(qk_bias[:, n, :], ps[2 + n][:, 0:C], vec[:, r:r + C], ALU.add)
            for k, n in enumerate((1, 0, 2)):
                dve.wait_ge(raw_in[n], 16)
                dve.wait_ge(split, k + 2)
                low_part_of(nc, w_hi, w_lo, raw, n, C, gain(n))
                if k == 0:
                    dve.wait_ge(bias_loaded, 32)
                    dve.wait_ge(bias_ps, 3)
                    nc.vector.tensor_tensor(bias_in[:, 0, :], ps[4][0:1, :], bias_in[:, 0, :],
                                            ALU.add).then_inc(bias_step, 1)


def project_rows(nc, w_hi, w_lo, m, a_hi, a_lo, b, bank, C):
    for c in range(C):
        yield nc.tensor.matmul(bank[:, :], a_hi[:, c, b, :], w_hi[:, m, c, :], start=(c == 0), stop=False)
        yield nc.tensor.matmul(bank[:, :], a_lo[:, c, b, :], w_hi[:, m, c, :], start=False, stop=False)
        yield nc.tensor.matmul(bank[:, :], a_hi[:, c, b, :], w_lo[:, m, c, :], start=False, stop=(c == C - 1))


def project_features(nc, w_hi, w_lo, m, f, a_hi, a_lo, dst, C, first):
    fs = slice(f * P, (f + 1) * P)
    for c in range(C):
        yield nc.tensor.matmul(dst, w_hi[:, m, c, fs], a_hi[:, c], start=(first and c == 0), stop=False)
        yield nc.tensor.matmul(dst, w_hi[:, m, c, fs], a_lo[:, c], start=False, stop=False)
        yield nc.tensor.matmul(dst, w_lo[:, m, c, fs], a_hi[:, c], start=False, stop=(c == C - 1))


def run(steps):
    last = None
    for last in steps:
        pass
    return last


def several(n, steps):
    while list(islice(steps, n)):
        yield


def woven(one, other, n=None):
    for _ in islice(zip_longest(one, other), n):
        pass


def bodies(eng, NP, body):
    body(0, True, True, False)
    with eng.Fori(1, NP - 2) as i:
        body(i, False, True, False)
    body(NP - 2, False, False, False)
    body(NP - 1, False, False, True)


def layer0(nc, ctx, sem, sb, ps, x_d, x1_d, xr, x_in, w_hi, w_lo, ident, bias_all, key_bias,
           half_gain, half_shift, mask_col, mask_d, eps, neg_half, next_w, next_raw, next_in, next_bias_ps,
           next_norm_b, stored, B, NP, D, C, H, DH):
    Q, K, V, O = range(4)
    BQ, BV, BO = range(3)
    HB = 2
    DV = P + 1
    DY = P + HB
    xn = sb(ctx, "xn", [P, PAIR, D])
    xT_hi = sb(ctx, "xT_hi", [P, C, PAIR, P], F32R)
    xT_lo = sb(ctx, "xT_lo", [P, C, PAIR, P], F32R)
    k_neg = sb(ctx, "k_neg", [P, C, PAIR])
    k_exp = sb(ctx, "k_exp", [P, C, PAIR, P])
    q_max = sb(ctx, "q_max", [P, PAIR, H])
    q_exp = sb(ctx, "q_exp", [P, PAIR, D])
    qT = sb(ctx, "qT", [P, PAIR, C, P])
    k_rows = sb(ctx, "k_rows", [P, PAIR, C, P])
    v = sb(ctx, "v", [P, PAIR, C, DV])
    k_sum = sb(ctx, "k_sum", [P, PAIR, C])
    q_sum = sb(ctx, "q_sum", [P, PAIR, H])
    att = sb(ctx, "att", [P, PAIR, C, DY])
    z = sb(ctx, "z", [P, PAIR, D])
    g = sb(ctx, "g", [P, PAIR, C, P])
    th = sb(ctx, "th", [P, PAIR, C, P])
    hs = sb(ctx, "hs", [P, PAIR, C, P])
    h_hi = sb(ctx, "h_hi", [P, C, PAIR, P], F32R)
    h_lo = sb(ctx, "h_lo", [P, C, PAIR, P], F32R)
    x1 = sb(ctx, "x1", [P, PAIR, D])
    stats = sb(ctx, "stats", [P, PAIR, 6])
    stats_y = sb(ctx, "stats_y", [P, PAIR, 6])
    mv = sb(ctx, "mv", [P, PAIR, 2])
    mv_y = sb(ctx, "mv_y", [P, PAIR, 2])
    ve = sb(ctx, "ve", [P, PAIR])
    ve_y = sb(ctx, "ve_y", [P, PAIR])
    rstd = sb(ctx, "rstd", [P, PAIR])
    rstd_y = sb(ctx, "rstd_y", [P, PAIR])
    gains = sb(ctx, "gains", [P, 2, C, PAIR])
    mask_now = sb(ctx, "mask_now", [P, PAIR])
    v_bias = sb(ctx, "v_bias", [P, PAIR, D])
    mask_rows = sb(ctx, "mask_rows", [P, RING, PAIR * P], F32R)
    seen = sb(ctx, "seen", [P, 1])

    s = {n: sem("l0_" + n) for n in (
        "preset", "rows_preset", "masks_in", "masks", "v_bias", "x_biased", "stats", "var", "var_eps", "rstd", "xn", "xT_ps", "xT_hi", "xT_lo",
        "kT_ps", "k_neg", "k_exp", "q_ps", "q", "q_max", "q_less", "q_exp", "v_ps", "v", "q_tr", "k_tr", "qT", "k_rows",
        "att_ps", "k_sum", "att", "y_ps", "q_sum", "y", "y_stats", "y_var", "y_var_eps", "y_rstd", "z", "z_ps", "gains",
        "g", "tanh", "silu", "h_hi", "h_lo", "o_ps", "x1")}

    block = ctx.enter_context(nc.Block())

    @block.sync
    def _(sp):
        sp.wait_ge(s["rows_preset"], 1)

        def load_masks(pair, slot):
            for n, r in enumerate((64, 96)):
                sp.dma_start(f32(mask_rows[r:r + 1, slot, :]),
                             mask_d[0, n, bass.ds(pair * PAIR, PAIR)].rearrange("b t -> (b t)").unsqueeze(0))\
                    .then_inc(s["masks_in"], 16)

        load_masks(0, 0)
        load_masks(1, 1)
        for w, dst, arrived in zip(next_w, next_raw, next_in):
            sp.dma_start(dst[:], w.rearrange("(c p) n -> p c n", p=P)).then_inc(arrived, 16)

        def store(prev):
            for b in range(PAIR):
                sp.wait_ge(s["x1"], seq(PAIR, prev, b + 1))
                sp.dma_start(x1_d[prev * PAIR + b], x1[:, b]).then_inc(stored, 16)

        def body(i, first, more, last):
            if not first:
                store(i - 1)
                sp.wait_ge(stored, seq(16 * PAIR, i - 1, 16 * PAIR))
            if more:
                sp.wait_ge(x_in, seq(16, i, 32))
                sp.wait_ge(s["masks_in"], seq(32, i, 64))
                load_rows(sp, x_d, xr, i + 2, (i + 2) % RING, x_in)
                load_masks(i + 2, (i + 2) % RING)

        bodies(sp, NP, body)
        store(NP - 1)

    @block.gpsimd
    def _(pool):
        nc.gpsimd.memset(f32(mask_rows[:]), 1.0).then_inc(s["rows_preset"], 1)

        def inverse_root(n, var, e, to, var_eps_sem, rstd_sem, pair):
            nc.gpsimd.tensor_tensor(e[:], var[:, :, 1], eps[:], ALU.add).then_inc(var_eps_sem, 1)
            pool.wait_ge(var_eps_sem, seq(1, pair, 1))
            nc.gpsimd.tensor_tensor(to[:], e[:], neg_half[:], ALU.pow).then_inc(rstd_sem, 1)

        def end(prev):
            pool.wait_ge(s["y_var"], seq(1, prev, 1))
            inverse_root(0, mv_y, ve_y, rstd_y, s["y_var_eps"], s["y_rstd"], prev)
            nc.gpsimd.tensor_copy(gains[:, 0], half_gain[:, 0, :, bass.ds(prev * PAIR, PAIR)])
            nc.gpsimd.tensor_copy(gains[:, 1], half_shift[:, 0, :, bass.ds(prev * PAIR, PAIR)]).then_inc(s["gains"], 1)

        def norm(pair):
            pool.wait_ge(s["var"], seq(1, pair, 1))
            inverse_root(1, mv, ve, rstd, s["var_eps"], s["rstd"], pair)

        def low_parts(prev):
            for b in range(PAIR):
                pool.wait_ge(s["h_hi"], seq(PAIR, prev, b + 1))
                nc.gpsimd.tensor_tensor(h_lo[:, :, b, :], hs[:, b], f32(h_hi[:, :, b, :]),
                                        ALU.subtract).then_inc(s["h_lo"], 1)

        def biases(pair, slot, first):
            pool.wait_ge(s["xn"], seq(PAIR, pair, PAIR))
            for b in range(PAIR):
                last = nc.gpsimd.tensor_tensor(xr[:, slot, b], xr[:, slot, b], bias_all[:, BO, :], ALU.add)
            last.then_inc(s["x_biased"], 1)
            if not first:
                pool.wait_ge(s["v"], seq(PAIR, pair - 1, PAIR))
            nc.gpsimd.tensor_copy(mask_now[:], mask_col[:, 0, bass.ds(pair * PAIR, PAIR)]).then_inc(s["masks"], 1)
            pool.wait_ge(s["masks"], seq(1, pair, 1))
            for b in range(PAIR):
                last = nc.gpsimd.tensor_tensor(v_bias[:, b], bias_all[:, BV, :],
                                               mask_now[:, b:b + 1].broadcast_to([P, D]), ALU.mult)
            last.then_inc(s["v_bias"], 1)

        norm(0)
        biases(0, 0, True)

        def body(i, first, more, last):
            if not first:
                end(i - 1)
            if not last:
                norm(i + 1)
            if not first:
                low_parts(i - 1)
            if not last:
                biases(i + 1, (i + 1) % RING, False)

        bodies(pool, NP, body)
        end(NP - 1)
        low_parts(NP - 1)

    @block.vector
    def _(dve):
        nc.vector.memset(v[:], 1.0)
        nc.vector.memset(att[:], 0.0).then_inc(s["preset"], 1)
        dve.wait_ge(s["preset"], 1)
        nc.vector.memset(att[0:64, :, :, P:P + 1], 1.0)
        nc.vector.memset(att[64:128, :, :, P + 1:P + 2], 1.0).then_inc(s["preset"], 1)

        def row_stats(pair, slot):
            dve.wait_ge(x_in, seq(16, pair, 16) if not isinstance(pair, int) or pair > 0 else 32)
            for b in range(PAIR):
                nc.vector.bn_stats(stats[:, b], xr[:, slot, b]).then_inc(s["stats"], 1)
            dve.wait_ge(s["stats"], seq(PAIR, pair, PAIR))
            nc.vector.tensor_copy(seen[:], eps[:, 0:1])
            for b in range(PAIR):
                last = nc.vector.bn_aggr(mv[:, b], stats[:, b])
            last.then_inc(s["var"], 1)

        def norm(pair, slot):
            dve.wait_ge(s["rstd"], seq(1, pair, 1))
            for b in range(PAIR):
                nc.vector.tensor_scalar(xn[:, b], xr[:, slot, b], mv[:, b, 0:1], rstd[:, b:b + 1], ALU.subtract,
                                        ALU.mult).then_inc(s["xn"], 1)

        def x_low(pair, banks):
            for b in range(PAIR):
                dve.wait_ge(s["xT_hi"], seq(PAIR, pair, b + 1))
                nc.vector.tensor_tensor(xT_lo[:, :, b, :], banks[b][:, :].rearrange("p (c t) -> p c t", c=C),
                                        f32(xT_hi[:, :, b, :]), ALU.subtract).then_inc(s["xT_lo"], 1)

        def end_norm(prev):
            dve.wait_ge(s["y_rstd"], seq(1, prev, 1))
            for b in range(PAIR):
                nc.vector.tensor_scalar(z[:, b], z[:, b], mv_y[:, b, 0:1], rstd_y[:, b:b + 1], ALU.subtract,
                                        ALU.mult).then_inc(s["z"], 1)

        def end_silus(prev):
            for b in range(PAIR):
                dve.wait_ge(s["tanh"], seq(PAIR, prev, b + 1))
                nc.vector.scalar_tensor_tensor(hs[:, b], th[:, b], 1.0, g[:, b], ALU.add,
                                               ALU.mult).then_inc(s["silu"], 1)

        def end_add(prev, slot, b):
            if isinstance(prev, int) and prev > 0 and b == 0:
                dve.wait_ge(stored, seq(16 * PAIR, prev - 1, 16 * PAIR))
            dve.wait_ge(s["o_ps"], seq(PAIR, prev, b + 1))
            dve.wait_ge(s["x_biased"], seq(1, prev, 1))
            nc.vector.tensor_tensor(x1[:, b], ps[b][:, :], xr[:, slot, b], ALU.add).then_inc(s["x1"], 1)

        def key_maxima(i):
            for j in range(2):
                dve.wait_ge(s["kT_ps"], seq(2, i, j + 1))
                nc.vector.tensor_reduce(k_neg[:, 2 * j:2 * j + 2, :],
                                        ps[j][:, :].rearrange("p (c b t) -> p c b t", c=2, b=PAIR), AX_X, ALU.max,
                                        negate=True).then_inc(s["k_neg"], 1)

        def query_shift(i, b):
            q3 = q_exp[:, b].rearrange("p (h d) -> p h d", h=H)
            dve.wait_ge(s["q_ps"], seq(PAIR, i, b + 1))
            nc.vector.tensor_tensor(q_exp[:, b], ps[2 + b][:, :], bias_all[:, BQ, :], ALU.add).then_inc(s["q"], 1)
            dve.wait_ge(s["q"], seq(PAIR, i, b + 1))
            nc.vector.reduce_max(q_max[:, b], q3, AX_X).then_inc(s["q_max"], 1)
            dve.wait_ge(s["q_max"], seq(PAIR, i, b + 1))
            nc.vector.tensor_tensor(q3, q3, q_max[:, b].unsqueeze(2).broadcast_to([P, H, DH]),
                                    ALU.subtract).then_inc(s["q_less"], 1)

        def values(i, b):
            dve.wait_ge(s["v_bias"], seq(1, i, 1))
            dve.wait_ge(s["v_ps"], seq(PAIR, i, b + 1))
            nc.vector.scalar_tensor_tensor(v[:, b, :, 0:P], ps[4 + b][:, :].rearrange("p (c d) -> p c d", c=C),
                                           mask_now[:, b:b + 1], v_bias[:, b].rearrange("p (c d) -> p c d", c=C),
                                           ALU.mult, ALU.add).then_inc(s["v"], 1)

        def key_rows(i, b):
            dve.wait_ge(s["k_tr"], seq(PAIR, i, b + 1))
            nc.vector.tensor_copy(k_rows[:, b], ps[(7, 5)[b]][:, :].rearrange("p (c t) -> p c t", c=C))\
                .then_inc(s["k_rows"], 1)

        def weights_of(i):
            for b in range(PAIR):
                banks = ((6, 7), (2, 3))[b]
                dve.wait_ge(s["att_ps"], seq(PAIR, i, b + 1))
                for j in range(2):
                    a = ps[banks[j]][:, 0:2 * DV].rearrange("p (c d) -> p c d", c=2)
                    last = nc.vector.reciprocal(k_sum[:, b, 2 * j:2 * j + 2], a[:, :, P])
                last.then_inc(s["k_sum"], 1)
                dve.wait_ge(s["k_sum"], seq(PAIR, i, b + 1))
                for j in range(2):
                    a = ps[banks[j]][:, 0:2 * DV].rearrange("p (c d) -> p c d", c=2)
                    for r in range(2):
                        rows, cols = slice(64 * r, 64 * r + 64), slice(64 * r, 64 * r + 64)
                        last = nc.vector.tensor_tensor(
                            att[rows, b, 2 * j:2 * j + 2, cols], a[rows, :, cols],
                            k_sum[rows, b, 2 * j:2 * j + 2].unsqueeze(2).broadcast_to([64, 2, 64]), ALU.mult)
                last.then_inc(s["att"], 1)

        def outputs(i):
            for b in range(PAIR):
                banks = ((4, 5), (6, 7))[b]
                dve.wait_ge(s["y_ps"], seq(PAIR, i, b + 1))
                for j in range(2):
                    a = ps[banks[j]][:, 0:2 * DY].rearrange("p (c d) -> p c d", c=2)
                    last = nc.vector.reciprocal(q_sum[:, b, 4 * j:4 * j + 4].rearrange("p (c r) -> p c r", c=2),
                                                a[:, :, P:P + 2])
                last.then_inc(s["q_sum"], 1)
                dve.wait_ge(s["q_sum"], seq(PAIR, i, b + 1))
                for j in range(2):
                    a = ps[banks[j]][:, 0:2 * DY].rearrange("p (c d) -> p c d", c=2)
                    for c in range(2):
                        last = nc.vector.tensor_tensor(
                            z[:, b, (2 * j + c) * P:(2 * j + c + 1) * P].rearrange("p (r d) -> p r d", r=2),
                            a[:, c, 0:P].rearrange("p (r d) -> p r d", r=2),
                            q_sum[:, b, 4 * j + 2 * c:4 * j + 2 * c + 2].unsqueeze(2).broadcast_to([P, 2, DH]),
                            ALU.mult)
                last.then_inc(s["y"], 1)
                dve.wait_ge(s["y"], seq(PAIR, i, b + 1))
                nc.vector.bn_stats(stats_y[:, b], z[:, b]).then_inc(s["y_stats"], 1)
            dve.wait_ge(s["y_stats"], seq(PAIR, i, PAIR))
            nc.vector.tensor_copy(seen[:], eps[:, 0:1])
            for b in range(PAIR):
                last = nc.vector.bn_aggr(mv_y[:, b], stats_y[:, b])
            last.then_inc(s["y_var"], 1)

        row_stats(0, 0)
        norm(0, 0)
        x_low(0, (ps[2], ps[3]))

        def body(i, first, more, last):
            if not first:
                end_norm(i - 1)
            key_maxima(i)
            if not last:
                row_stats(i + 1, (i + 1) % RING)
            query_shift(i, 0)
            query_shift(i, 1)
            if not first:
                end_silus(i - 1)
            if not last:
                norm(i + 1, (i + 1) % RING)
            values(i, 0)
            values(i, 1)
            if not last:
                x_low(i + 1, (ps[2], ps[3]))
            if not first:
                end_add(i - 1, (i - 1) % RING, 0)
            key_rows(i, 0)
            key_rows(i, 1)
            weights_of(i)
            if not first:
                end_add(i - 1, (i - 1) % RING, 1)
            outputs(i)

        bodies(dve, NP, body)
        end_norm(NP - 1)
        end_silus(NP - 1)
        for b in range(PAIR):
            end_add(NP - 1, (NP - 1) % RING, b)

    @block.scalar
    def _(act):
        def x_high(pair, banks):
            for b in range(PAIR):
                act.wait_ge(s["xT_ps"], seq(PAIR, pair, b + 1))
                nc.scalar.activation(xT_hi[:, :, b, :], banks[b][:, :].rearrange("p (c t) -> p c t", c=C),
                                     ACT.Copy).then_inc(s["xT_hi"], 1)

        def key_exps(i):
            for j in range(2):
                act.wait_ge(s["k_neg"], seq(2, i, j + 1))
                for c in (2 * j, 2 * j + 1):
                    for b in range(PAIR):
                        at = (c - 2 * j) * PAIR * P + b * P
                        last = nc.scalar.activation(k_exp[:, c, b, :], ps[j][:, at:at + P], ACT.Exp,
                                                    bias=k_neg[:, c, b:b + 1])
                last.then_inc(s["k_exp"], 1)

        def query_exps(i, b):
            act.wait_ge(s["q_less"], seq(PAIR, i, b + 1))
            nc.scalar.activation(q_exp[:, b], q_exp[:, b], ACT.Exp).then_inc(s["q_exp"], 1)

        def gates(prev):
            act.wait_ge(s["gains"], seq(1, prev, 1))
            for b in range(PAIR):
                act.wait_ge(s["z_ps"], seq(PAIR, prev, b + 1))
                for c in range(C):
                    last = nc.scalar.activation(g[:, b, c, :], ps[6 + b][:, c * P:(c + 1) * P], ACT.Identity,
                                                scale=gains[:, 0, c, b:b + 1], bias=gains[:, 1, c, b:b + 1])
                last.then_inc(s["g"], 1)

        def tanhs(prev):
            for b in range(PAIR):
                act.wait_ge(s["g"], seq(PAIR, prev, b + 1))
                nc.scalar.activation(th[:, b], g[:, b], ACT.Tanh).then_inc(s["tanh"], 1)

        def h_high(prev):
            for b in range(PAIR):
                act.wait_ge(s["silu"], seq(PAIR, prev, b + 1))
                nc.scalar.activation(h_hi[:, :, b, :], hs[:, b], ACT.Copy).then_inc(s["h_hi"], 1)

        def query_T(i):
            for b in range(PAIR):
                act.wait_ge(s["q_tr"], seq(PAIR, i, b + 1))
                nc.scalar.activation(qT[:, b], ps[(6, 4)[b]][:, :].rearrange("p (c t) -> p c t", c=C),
                                     ACT.Copy).then_inc(s["qT"], 1)

        act.wait_ge(s["preset"], 2)
        x_high(0, (ps[2], ps[3]))

        def body(i, first, more, last):
            key_exps(i)
            query_exps(i, 0)
            if not first:
                gates(i - 1)
                tanhs(i - 1)
            query_exps(i, 1)
            if not first:
                h_high(i - 1)
            if not last:
                x_high(i + 1, (ps[2], ps[3]))
            query_T(i)

        bodies(act, NP, body)
        gates(NP - 1)
        tanhs(NP - 1)
        h_high(NP - 1)

    @block.tensor
    def _(pe):
        pe.wait_ge(s["preset"], 2)

        def x_transposed(pair):
            for b in range(PAIR):
                pe.wait_ge(s["xn"], seq(PAIR, pair, b + 1))
                for c in range(C):
                    last = nc.tensor.transpose(ps[2 + b][:, c * P:(c + 1) * P], xn[:, b, c * P:(c + 1) * P], ident[:])
                last.then_inc(s["xT_ps"], 1)

        def z_transposed(prev):
            for b in range(PAIR):
                pe.wait_ge(s["z"], seq(PAIR, prev, b + 1))
                for c in range(C):
                    last = nc.tensor.transpose(ps[6 + b][:, c * P:(c + 1) * P], z[:, b, c * P:(c + 1) * P], ident[:])
                last.then_inc(s["z_ps"], 1)

        def out_rows(prev, b):
            pe.wait_ge(s["h_lo"], seq(PAIR, prev, b + 1))
            done = None
            for done in project_rows(nc, w_hi, w_lo, O, h_hi, h_lo, b, ps[b], C):
                yield
            done.then_inc(s["o_ps"], 1)

        def weights_turned(i, b):
            pe.wait_ge(s["q_exp"], seq(PAIR, i, b + 1))
            pe.wait_ge(s["v"], seq(PAIR, i, PAIR))
            for c in range(C):
                done = nc.tensor.transpose(ps[(6, 4)[b]][:, c * P:(c + 1) * P], q_exp[:, b, c * P:(c + 1) * P],
                                           ident[:])
            done.then_inc(s["q_tr"], 1)
            for c in range(C):
                done = nc.tensor.transpose(ps[(7, 5)[b]][:, c * P:(c + 1) * P], k_exp[:, c, b, :], ident[:])
            done.then_inc(s["k_tr"], 1)

        x_transposed(0)

        def body(i, first, more, last):
            pe.wait_ge(s["masks_in"], 64 if first else seq(32, i, 32))
            for f in range(C):
                dst = ps[f // 2][:, (f % 2) * PAIR * P:(f % 2 + 1) * PAIR * P]
                nc.tensor.matmul(dst, key_bias[:, f * P:(f + 1) * P], mask_rows[:, i % RING, :],
                                 start=True, stop=False)
                if f == 0:
                    pe.wait_ge(s["xT_lo"], seq(PAIR, i, PAIR))
                done = run(project_features(nc, w_hi, w_lo, K, f, xT_hi, xT_lo, dst, C, False))
                if f % 2:
                    done.then_inc(s["kT_ps"], 1)
            for b in range(PAIR):
                if b == 1 and not first:
                    z_transposed(i - 1)
                run(project_rows(nc, w_hi, w_lo, Q, xT_hi, xT_lo, b, ps[2 + b], C)).then_inc(s["q_ps"], 1)
            for b in range(PAIR):
                run(project_rows(nc, w_hi, w_lo, V, xT_hi, xT_lo, b, ps[4 + b], C)).then_inc(s["v_ps"], 1)
            pe.wait_ge(s["k_exp"], seq(2, i, 2))
            if not last:
                pe.wait_ge(s["q_less"], seq(PAIR, i, PAIR))
                x_transposed(i + 1)
            if not first:
                run(out_rows(i - 1, 0))
            weights_turned(i, 0)
            weights_turned(i, 1)
            outputs1 = () if first else out_rows(i - 1, 1)
            run(islice(outputs1, 7))
            for b in range(PAIR):
                banks = ((6, 7), (2, 3))[b]
                if b == 1 and not last:
                    pe.wait_ge(s["xT_lo"], seq(PAIR, i + 1, PAIR))
                pe.wait_ge(s["k_rows"], seq(PAIR, i, b + 1))
                pe.wait_ge(s["qT"], seq(PAIR, i, b + 1))
                for c in range(C):
                    done = nc.tensor.matmul(ps[banks[c // 2]][:, (c % 2) * DV:(c % 2 + 1) * DV], k_rows[:, b, c, :],
                                            v[:, b, c, :], start=True, stop=True)
                done.then_inc(s["att_ps"], 1)
            run(outputs1)
            for b in range(PAIR):
                banks = ((4, 5), (6, 7))[b]
                pe.wait_ge(s["att"], seq(PAIR, i, b + 1))
                for c in range(C):
                    done = nc.tensor.matmul(ps[banks[c // 2]][:, (c % 2) * DY:(c % 2 + 1) * DY], qT[:, b, c, :],
                                            att[:, b, c, :], start=True, stop=True)
                done.then_inc(s["y_ps"], 1)
            if not first:
                pe.wait_ge(s["x1"], seq(PAIR, i - 1, PAIR))

        def next_bias(n):
            pe.wait_ge(next_in[n], 16)
            for f in range(C):
                for c in range(C):
                    last = nc.tensor.matmul(ps[2 + n][:, f:f + 1], next_raw[n][:, c, f * P:(f + 1) * P],
                                            next_norm_b[c], start=(c == 0), stop=(c == C - 1))
            last.then_inc(next_bias_ps, 1)

        bodies(pe, NP, body)
        next_bias(0)
        z_transposed(NP - 1)
        next_bias(1)
        for b in range(PAIR):
            run(out_rows(NP - 1, b))


def layer1(nc, ctx, sem, sb, ps, x1_d, out, xr, x_in, w_hi, w_lo, ident, bias_all, qk_bias,
           half_gain, half_shift, mask_col, mask_d, eps, neg_half, B, NP, D, C, HC, H, DH):
    Q, K, V, O = range(4)
    BV, BO = 1, 2
    DV = DH + 1
    HB = 512 // P
    HY = H // 2
    xn = sb(ctx, "xn1", [P, PAIR, D])
    xT_hi = sb(ctx, "xT_hi1", [P, C, PAIR, P], F32R)
    xT_lo = sb(ctx, "xT_lo1", [P, C, PAIR, P], F32R)
    parts = sb(ctx, "parts", [P, 4, C, PAIR, P], F32R)
    Q_LO, Q_HI, K_HI, K_LO = range(4)
    HI, LO = (Q_HI, K_HI), (Q_LO, K_LO)
    stack = sb(ctx, "stack", [P, 2, HC, C, PAIR, P], F32R)
    v = sb(ctx, "v1", [P, PAIR, H, DV])
    top = sb(ctx, "top", [P, PAIR, H])
    top_T = sb(ctx, "top_T", [H, PAIR, P], F32R)
    prob = sb(ctx, "prob", [P, PAIR, H, P])
    p_sum = sb(ctx, "p_sum", [P, PAIR, H])
    z = sb(ctx, "z1", [P, PAIR, D])
    g = sb(ctx, "g1", [P, PAIR, C, P])
    th = sb(ctx, "th1", [P, PAIR, C, P])
    hs = sb(ctx, "hs1", [P, PAIR, C, P])
    h_hi = sb(ctx, "h_hi1", [P, C, PAIR, P], F32R)
    h_lo = sb(ctx, "h_lo1", [P, C, PAIR, P], F32R)
    y_out = sb(ctx, "y_out", [P, PAIR, D])
    stats = sb(ctx, "stats1", [P, PAIR, 6])
    stats_y = sb(ctx, "stats_y1", [P, PAIR, 6])
    mv = sb(ctx, "mv1", [P, PAIR, 2])
    mv_y = sb(ctx, "mv_y1", [P, PAIR, 2])
    ve = sb(ctx, "ve1", [P, PAIR])
    ve_y = sb(ctx, "ve_y1", [P, PAIR])
    rstd = sb(ctx, "rstd1", [P, PAIR])
    rstd_y = sb(ctx, "rstd_y1", [P, PAIR])
    gains = sb(ctx, "gains1", [P, 2, C, PAIR])
    mask_now = sb(ctx, "mask_now1", [P, PAIR])
    v_bias = sb(ctx, "v_bias1", [P, PAIR, D])
    seen = sb(ctx, "seen1", [P, 1])

    s = {n: sem("l1_" + n) for n in (
        "preset", "rows_preset", "stats", "var", "var_eps", "rstd", "xn", "xT_ps", "xT_hi", "xT_lo", "masks", "v_bias", "x_biased",
        "qk_ps", "qk_hi", "qk_lo", "stack", "v_ps", "v", "s_ps", "top", "top_ps", "top_T",
        "shift0", "shift1", "w_ps", "prob", "y_ps", "p_sum", "y", "y_stats", "y_var", "y_var_eps", "y_rstd", "z",
        "z_ps", "gains", "g", "tanh", "silu", "h_hi", "h_lo", "o_ps", "out", "stored")}
    STACK_DMAS = HC * 3 + 1
    QK_BANKS = ((2, 3), (0, 1))
    W_BANKS = (4, 5, 6, 7)
    Y_BANKS = ((4, 5), (6, 7))
    V_BANKS = (0, 1)
    S_BANKS = (0, 1, 2, 3)
    Z_BANKS = (4, 5)
    O_BANKS = (4, 5)
    X_BANKS = (7, 6)
    T_BANKS = (7, 6)
    Z_AFTER = 11

    block = ctx.enter_context(nc.Block())

    @block.sync
    def _(sp):
        sp.wait_ge(s["rows_preset"], 1)

        def restack(i, first):
            if not first:
                sp.wait_ge(s["w_ps"], seq(PAIR * C, i - 1, PAIR * C))
            sp.dma_start(f32(stack[ROW_MASK:ROW_MASK + 2, 1]).rearrange("r a c b t -> r (a c) (b t)"),
                         mask_d[1, :, bass.ds(i * PAIR, PAIR)].rearrange("r b t -> r (b t)").unsqueeze(1)
                         .broadcast_to([2, H, PAIR * P])).then_inc(s["stack"], 16)
            sp.wait_ge(s["qk_hi"], seq(2 * C, i, 2 * C))
            for r, q, k in ((0, Q_HI, K_HI), (1, Q_LO, K_HI), (2, Q_HI, K_LO)):
                if r == 1:
                    sp.wait_ge(s["qk_lo"], seq(2 * C, i, 2 * C))
                for a in range(HC):
                    sp.dma_start(f32(stack[DH * r:DH * r + DH, :, a]),
                                 f32(parts[DH * a:DH * a + DH, q:k + 1:k - q])).then_inc(s["stack"], 16)

        def store(prev, b):
            sp.wait_ge(s["out"], seq(PAIR, prev + 1, b + 1))
            sp.dma_start(out[prev * PAIR + b], y_out[:, b]).then_inc(s["stored"], 16)

        def body(i, first, more, last):
            restack(i, first)
            if not first:
                store(i - 1, 0)
                store(i - 1, 1)
                sp.wait_ge(s["stored"], seq(16 * PAIR, i - 1, 16 * PAIR))
            if more:
                sp.wait_ge(x_in, seq(16, i, 32))
                load_rows(sp, x1_d, xr, i + 2, (i + 2) % RING, x_in)

        bodies(sp, NP, body)
        store(NP - 1, 0)
        store(NP - 1, 1)
        sp.wait_ge(s["stored"], seq(16 * PAIR, NP - 1, 16 * PAIR))

    @block.gpsimd
    def _(pool):
        def end_rstd(prev, b):
            pool.wait_ge(s["y_var"], seq(PAIR, prev, b + 1))
            nc.gpsimd.tensor_tensor(ve_y[:, b:b + 1], mv_y[:, b, 1:2], eps[:, 0:1], ALU.add).then_inc(s["y_var_eps"], 1)
            pool.wait_ge(s["y_var_eps"], seq(PAIR, prev, b + 1))
            nc.gpsimd.tensor_tensor(rstd_y[:, b:b + 1], ve_y[:, b:b + 1], neg_half[:, 0:1],
                                    ALU.pow).then_inc(s["y_rstd"], 1)

        def end_gains(prev):
            nc.gpsimd.tensor_copy(gains[:, 0], half_gain[:, 1, :, bass.ds(prev * PAIR, PAIR)])
            nc.gpsimd.tensor_copy(gains[:, 1], half_shift[:, 1, :, bass.ds(prev * PAIR, PAIR)]).then_inc(s["gains"], 1)

        def norm(pair):
            pool.wait_ge(s["var"], seq(1, pair, 1))
            nc.gpsimd.tensor_tensor(ve[:], mv[:, :, 1], eps[:], ALU.add).then_inc(s["var_eps"], 1)
            pool.wait_ge(s["var_eps"], seq(1, pair, 1))
            nc.gpsimd.tensor_tensor(rstd[:], ve[:], neg_half[:], ALU.pow).then_inc(s["rstd"], 1)

        def biases(pair, slot, first):
            pool.wait_ge(s["xn"], seq(PAIR, pair, PAIR))
            for b in range(PAIR):
                last = nc.gpsimd.tensor_tensor(xr[:, slot, b], xr[:, slot, b], bias_all[:, BO, :], ALU.add)
            last.then_inc(s["x_biased"], 1)
            if not first:
                pool.wait_ge(s["v"], seq(PAIR, pair - 1, PAIR))
            nc.gpsimd.tensor_copy(mask_now[:], mask_col[:, 1, bass.ds(pair * PAIR, PAIR)]).then_inc(s["masks"], 1)
            pool.wait_ge(s["masks"], seq(1, pair, 1))
            for b in range(PAIR):
                last = nc.gpsimd.tensor_tensor(v_bias[:, b], bias_all[:, BV, :],
                                               mask_now[:, b:b + 1].broadcast_to([P, D]), ALU.mult)
            last.then_inc(s["v_bias"], 1)

        norm(0)
        pool.wait_ge(s["rstd"], 1)
        nc.gpsimd.memset(f32(stack[ROW_MASK:ROW_MASK + 3]), 1.0).then_inc(s["rows_preset"], 1)
        pool.wait_ge(s["rows_preset"], 1)
        biases(0, 0, True)

        def body(i, first, more, last):
            if not last:
                norm(i + 1)
            if not first:
                end_rstd(i - 1, 0)
                end_gains(i - 1)
                end_rstd(i - 1, 1)
            if not last:
                biases(i + 1, (i + 1) % RING, False)

        bodies(pool, NP, body)
        end_rstd(NP - 1, 0)
        end_gains(NP - 1)
        end_rstd(NP - 1, 1)

    @block.vector
    def _(dve):
        def row_stats(pair, slot):
            dve.wait_ge(x_in, seq(16, pair, 16) if not isinstance(pair, int) or pair > 0 else 32)
            for b in range(PAIR):
                nc.vector.bn_stats(stats[:, b], xr[:, slot, b]).then_inc(s["stats"], 1)
            dve.wait_ge(s["stats"], seq(PAIR, pair, PAIR))
            nc.vector.tensor_copy(seen[:], eps[:, 0:1])
            for b in range(PAIR):
                last = nc.vector.bn_aggr(mv[:, b], stats[:, b])
            last.then_inc(s["var"], 1)

        def norm(pair, slot):
            dve.wait_ge(s["rstd"], seq(1, pair, 1))
            for b in range(PAIR):
                nc.vector.tensor_scalar(xn[:, b], xr[:, slot, b], mv[:, b, 0:1], rstd[:, b:b + 1], ALU.subtract,
                                        ALU.mult).then_inc(s["xn"], 1)

        def x_low(pair, b):
            dve.wait_ge(s["xT_hi"], seq(PAIR, pair, b + 1))
            nc.vector.tensor_tensor(xT_lo[:, :, b, :], ps[X_BANKS[b]][:, :].rearrange("p (c t) -> p c t", c=C),
                                    f32(xT_hi[:, :, b, :]), ALU.subtract).then_inc(s["xT_lo"], 1)

        def qk_low(i, n):
            for c in range(C):
                if c % 2 == 0:
                    dve.wait_ge(s["qk_hi"], seq(2 * C, i, (1 - n) * C + c + 2))
                at = (c % 2) * PAIR * P
                nc.vector.scalar_tensor_tensor(
                    parts[:, LO[n], c].rearrange("p b t -> p (b t)"), ps[QK_BANKS[n][c // 2]][:, at:at + PAIR * P],
                    qk_bias[:, n, c:c + 1], f32(parts[:, HI[n], c]).rearrange("p b t -> p (b t)"), ALU.add,
                    ALU.subtract).then_inc(s["qk_lo"], 1)

        def maxima(i, b, banks):
            for j in banks:
                dve.wait_ge(s["s_ps"], seq(PAIR * C, i, b * C + j + 1))
                nc.vector.tensor_reduce(top[:, b, :].rearrange("p (a c) -> p a c", c=C)[:, :, j],
                                        ps[S_BANKS[j]][:, :].rearrange("p (h t) -> p h t", h=HB), AX_X, ALU.max,
                                        negate=True).then_inc(s["top"], 1)

        def end_outputs(prev, b):
            banks = Y_BANKS[b]
            dve.wait_ge(s["y_ps"], seq(PAIR, prev, b + 1))
            for j in range(2):
                a = ps[banks[j]][:, 0:HY * DV].rearrange("p (h d) -> p h d", h=HY)
                last = nc.vector.reciprocal(p_sum[:, b, HY * j:HY * j + HY], a[:, :, DH])
            last.then_inc(s["p_sum"], 1)
            dve.wait_ge(s["p_sum"], seq(PAIR, prev, b + 1))
            for j in range(2):
                a = ps[banks[j]][:, 0:HY * DV].rearrange("p (h d) -> p h d", h=HY)
                last = nc.vector.tensor_tensor(
                    z[:, b, HY * DH * j:HY * DH * (j + 1)].rearrange("p (h d) -> p h d", h=HY), a[:, :, 0:DH],
                    p_sum[:, b, HY * j:HY * j + HY].unsqueeze(2).broadcast_to([P, HY, DH]), ALU.mult)
            last.then_inc(s["y"], 1)
            dve.wait_ge(s["y"], seq(PAIR, prev, b + 1))
            nc.vector.bn_stats(stats_y[:, b], z[:, b]).then_inc(s["y_stats"], 1)
            dve.wait_ge(s["y_stats"], seq(PAIR, prev, b + 1))
            nc.vector.tensor_copy(seen[:], eps[:, 0:1])
            nc.vector.bn_aggr(mv_y[:, b], stats_y[:, b]).then_inc(s["y_var"], 1)

        def values(i, b, first):
            dve.wait_ge(s["v_bias"], seq(1, i, 1))
            dve.wait_ge(s["v_ps"], seq(PAIR, i, b + 1))
            if not first:
                dve.wait_ge(s["y_ps"], seq(PAIR, i - 1, b + 1))
            nc.vector.scalar_tensor_tensor(v[:, b, :, 0:DH], ps[V_BANKS[b]][:, :].rearrange("p (h d) -> p h d", h=H),
                                           mask_now[:, b:b + 1], v_bias[:, b].rearrange("p (h d) -> p h d", h=H),
                                           ALU.mult, ALU.add).then_inc(s["v"], 1)

        def end_norm(prev, b):
            dve.wait_ge(s["y_rstd"], seq(PAIR, prev, b + 1))
            nc.vector.tensor_scalar(z[:, b], z[:, b], mv_y[:, b, 0:1], rstd_y[:, b:b + 1], ALU.subtract,
                                    ALU.mult).then_inc(s["z"], 1)

        def end_silu(prev, b):
            dve.wait_ge(s["tanh"], seq(PAIR, prev, b + 1))
            nc.vector.scalar_tensor_tensor(hs[:, b], th[:, b], 1.0, g[:, b], ALU.add, ALU.mult).then_inc(s["silu"], 1)

        def low_part(prev, b):
            dve.wait_ge(s["h_hi"], seq(PAIR, prev, b + 1))
            nc.vector.tensor_tensor(h_lo[:, :, b, :], hs[:, b], f32(h_hi[:, :, b, :]),
                                    ALU.subtract).then_inc(s["h_lo"], 1)

        def end_add(prev, slot, b):
            if isinstance(prev, int) and prev > 0:
                dve.wait_ge(s["stored"], seq(16 * PAIR, prev - 1, 16 * PAIR))
            dve.wait_ge(s["o_ps"], seq(PAIR, prev, b + 1))
            dve.wait_ge(s["x_biased"], seq(1, prev, 1))
            nc.vector.tensor_tensor(y_out[:, b], ps[O_BANKS[b]][:, :], xr[:, slot, b], ALU.add).then_inc(s["out"], 1)

        row_stats(0, 0)
        nc.vector.memset(v[:], 1.0).then_inc(s["preset"], 1)
        nc.vector.memset(p_sum[:], 1.0).then_inc(s["out"], PAIR)
        norm(0, 0)
        x_low(0, 0)
        x_low(0, 1)

        def body(i, first, more, last):
            qk_low(i, 1)
            if not last:
                row_stats(i + 1, (i + 1) % RING)
            qk_low(i, 0)
            if not first:
                end_outputs(i - 1, 0)
            if not last:
                norm(i + 1, (i + 1) % RING)
            if not first:
                end_norm(i - 1, 0)
                end_outputs(i - 1, 1)
                end_silu(i - 1, 0)
                end_norm(i - 1, 1)
                low_part(i - 1, 0)
            values(i, 0, first)
            values(i, 1, first)
            if not first:
                end_silu(i - 1, 1)
            maxima(i, 0, (0,))
            if not first:
                low_part(i - 1, 1)
            maxima(i, 0, (1, 2))
            if not last:
                x_low(i + 1, 0)
            maxima(i, 0, (3,))
            if not first:
                end_add(i - 1, (i - 1) % RING, 0)
            maxima(i, 1, (0,))
            if not last:
                x_low(i + 1, 1)
            maxima(i, 1, (1, 2, 3))
            if not first:
                end_add(i - 1, (i - 1) % RING, 1)

        bodies(dve, NP, body)
        for b in range(PAIR):
            end_outputs(NP - 1, b)
            end_norm(NP - 1, b)
        for b in range(PAIR):
            end_silu(NP - 1, b)
        for b in range(PAIR):
            low_part(NP - 1, b)
        for b in range(PAIR):
            end_add(NP - 1, (NP - 1) % RING, b)

    @block.scalar
    def _(act):
        def x_high(pair, b):
            act.wait_ge(s["xT_ps"], seq(PAIR, pair, b + 1))
            nc.scalar.activation(xT_hi[:, :, b, :], ps[X_BANKS[b]][:, :].rearrange("p (c t) -> p c t", c=C),
                                 ACT.Copy).then_inc(s["xT_hi"], 1)

        def qk_high(i, n, chunks):
            for c in chunks:
                if c % 2 == 0:
                    act.wait_ge(s["qk_ps"], seq(C, i, (1 - n) * 2 + c // 2 + 1))
                at = (c % 2) * PAIR * P
                nc.scalar.activation(parts[:, HI[n], c].rearrange("p b t -> p (b t)"),
                                     ps[QK_BANKS[n][c // 2]][:, at:at + PAIR * P], ACT.Identity,
                                     bias=qk_bias[:, n, c:c + 1]).then_inc(s["qk_hi"], 1)

        def exps(prev, b):
            for j in range(C):
                act.wait_ge(s["w_ps"], seq(PAIR * C, prev, b * C + j + 1))
                nc.scalar.activation(prob[:, b, HB * j:HB * j + HB, :],
                                     ps[W_BANKS[j]][:, :].rearrange("p (h t) -> p h t", h=HB),
                                     ACT.Exp).then_inc(s["prob"], 1)

        def gate(prev, b):
            if b == 0:
                act.wait_ge(s["gains"], seq(1, prev, 1))
            act.wait_ge(s["z_ps"], seq(PAIR, prev, b + 1))
            for c in range(C):
                last = nc.scalar.activation(g[:, b, c, :], ps[Z_BANKS[b]][:, c * P:(c + 1) * P], ACT.Identity,
                                            scale=gains[:, 0, c, b:b + 1], bias=gains[:, 1, c, b:b + 1])
            last.then_inc(s["g"], 1)

        def tanh(prev, b):
            act.wait_ge(s["g"], seq(PAIR, prev, b + 1))
            nc.scalar.activation(th[:, b], g[:, b], ACT.Tanh).then_inc(s["tanh"], 1)

        def h_high(prev, b):
            act.wait_ge(s["silu"], seq(PAIR, prev, b + 1))
            nc.scalar.activation(h_hi[:, :, b, :], hs[:, b], ACT.Copy).then_inc(s["h_hi"], 1)

        def shift_out(i, b):
            act.wait_ge(s["top_ps"], seq(PAIR, i, b + 1))
            nc.scalar.activation(top_T[:, b, :], ps[T_BANKS[b]][0:H, 0:P], ACT.Copy).then_inc(s["top_T"], 1)
            act.wait_ge(s["top_T"], seq(PAIR, i, b + 1))
            act.dma_start(f32(stack[ROW_SHIFT:ROW_SHIFT + 1, 0, :, :, b, :]).rearrange("o a c t -> o (a c) t"),
                          f32(top_T[:, b, :])).then_inc(s[f"shift{b}"], 16)

        x_high(0, 0)
        x_high(0, 1)

        def body(i, first, more, last):
            if not first:
                shift_out(i - 1, 1)
            qk_high(i, 1, (0, 1))
            if not first:
                exps(i - 1, 0)
            qk_high(i, 1, (2, 3))
            if not first:
                exps(i - 1, 1)
            qk_high(i, 0, range(C))
            if not first:
                gate(i - 1, 0)
                tanh(i - 1, 0)
            if not first:
                h_high(i - 1, 0)
            if not first:
                gate(i - 1, 1)
                tanh(i - 1, 1)
                h_high(i - 1, 1)
            if not last:
                x_high(i + 1, 0)
                x_high(i + 1, 1)
            shift_out(i, 0)

        bodies(act, NP, body)
        shift_out(NP - 1, 1)
        exps(NP - 1, 0)
        exps(NP - 1, 1)
        for b in range(PAIR):
            gate(NP - 1, b)
            tanh(NP - 1, b)
        for b in range(PAIR):
            h_high(NP - 1, b)

    @block.tensor
    def _(pe):
        def x_transposed(pair, b, first):
            pe.wait_ge(s["xn"], seq(PAIR, pair, b + 1))
            if not first:
                pe.wait_ge(s["y"], seq(PAIR, pair - 2, PAIR))
            for c in range(C):
                last = nc.tensor.transpose(ps[X_BANKS[b]][:, c * P:(c + 1) * P], xn[:, b, c * P:(c + 1) * P], ident[:])
            last.then_inc(s["xT_ps"], 1)

        def z_transposed(prev, b):
            pe.wait_ge(s["z"], seq(PAIR, prev, b + 1))
            for c in range(C):
                last = nc.tensor.transpose(ps[Z_BANKS[b]][:, c * P:(c + 1) * P], z[:, b, c * P:(c + 1) * P], ident[:])
            last.then_inc(s["z_ps"], 1)

        def out_rows(prev, b):
            pe.wait_ge(s["h_lo"], seq(PAIR, prev, b + 1))
            done = None
            for done in project_rows(nc, w_hi, w_lo, O, h_hi, h_lo, b, ps[O_BANKS[b]], C):
                yield
            done.then_inc(s["o_ps"], 1)

        def projected(i, n, chunks):
            for f in chunks:
                dst = ps[QK_BANKS[n][f // 2]][:, (f % 2) * PAIR * P:(f % 2 + 1) * PAIR * P]
                done = None
                for done in project_features(nc, w_hi, w_lo, n, f, xT_hi, xT_lo, dst, C, True):
                    yield
                if f % 2:
                    done.then_inc(s["qk_ps"], 1)

        def value_rows(i, b):
            pe.wait_ge(s["qk_lo"], seq(2 * C, i, 2 * (b + 1)))
            done = None
            for done in project_rows(nc, w_hi, w_lo, V, xT_hi, xT_lo, b, ps[V_BANKS[b]], C):
                yield
            done.then_inc(s["v_ps"], 1)

        def weight_scores(prev, b):
            pe.wait_ge(s[f"shift{b}"], seq(16, prev, 16))
            for j in range(C):
                if b == 0 and j < 2:
                    pe.wait_ge(s["out"], seq(PAIR, prev, j + 1))
                if b == 0 and j == 2:
                    pe.wait_ge(s["top_T"], seq(PAIR, prev, PAIR))
                if b == 1:
                    pe.wait_ge(s["prob"], seq(PAIR * C, prev, j + 1))
                for a in range(HC):
                    last = nc.tensor.matmul(ps[W_BANKS[j]][:, a * P:(a + 1) * P], stack[0:K_SHIFTED, 1, a, j, b, :],
                                            stack[0:K_SHIFTED, 0, a, j, b, :], start=True, stop=True)
                last.then_inc(s["w_ps"], 1)

        def mixed(prev, b):
            pe.wait_ge(s["prob"], seq(PAIR * C, prev, C + 2 * (b + 1)))
            for h in range(H):
                j, a = h // HY, h % HY
                last = nc.tensor.matmul(ps[Y_BANKS[b][j]][:, a * DV:(a + 1) * DV], prob[:, b, h, :], v[:, b, h, :],
                                        start=True, stop=True)
                yield
            last.then_inc(s["y_ps"], 1)

        def scores(i, b, banks):
            if b == 0 and banks[0] == 0:
                pe.wait_ge(s["stack"], seq(16 * STACK_DMAS, i, 16 * STACK_DMAS))
            for j in banks:
                if b == 0 and j < 2:
                    pe.wait_ge(s["v"], seq(PAIR, i, j + 1))
                if b == 1:
                    pe.wait_ge(s["top"], seq(PAIR * C, i, j + 1))
                for a in range(HC):
                    last = nc.tensor.matmul(ps[S_BANKS[j]][:, a * P:(a + 1) * P], stack[0:K_SCORE, 0, a, j, b, :],
                                            stack[0:K_SCORE, 1, a, j, b, :], start=True, stop=True)
                    if a == HC - 1:
                        last.then_inc(s["s_ps"], 1)
                    if a % 2:
                        yield

        def shift_row(i, b):
            pe.wait_ge(s["top"], seq(PAIR * C, i, C * (b + 1)))
            nc.tensor.transpose(ps[T_BANKS[b]][0:H, 0:P], top[:, b, :], ident[:]).then_inc(s["top_ps"], 1)

        x_transposed(0, 0, True)
        x_transposed(0, 1, True)

        def body(i, first, more, last):
            pe.wait_ge(s["xT_lo"], seq(PAIR, i, PAIR))
            for f in range(C):
                if not first and f % 2 == 0:
                    pe.wait_ge(s["top"], seq(PAIR * C, i - 1, C + f // 2 + 1))
                keys = projected(i, 1, (f,))
                if not first and f == 1:
                    run(islice(keys, 4))
                    shift_row(i - 1, 1)
                run(keys)
                if not first and f % 2:
                    weight_scores(i - 1, f // 2)
            run(projected(i, 0, (0, 1)))
            if first:
                run(projected(i, 0, (2, 3)))
            else:
                woven(several(2, projected(i, 0, (2, 3))), mixed(i - 1, 0))
            outputs1, values0 = () if first else mixed(i - 1, 1), value_rows(i, 0)
            woven(outputs1, values0, Z_AFTER)
            if not first:
                z_transposed(i - 1, 0)
            run(outputs1)
            run(values0)
            run(value_rows(i, 1))
            if not last:
                x_transposed(i + 1, 0, first)
                x_transposed(i + 1, 1, first)
            if first:
                pe.wait_ge(s["preset"], 1)
            outputs0, scores0 = () if first else out_rows(i - 1, 0), scores(i, 0, range(C))
            if not first:
                z_transposed(i - 1, 1)
            run(islice(outputs0, 3))
            woven(outputs0, scores0)
            outputs1, scores1 = () if first else out_rows(i - 1, 1), scores(i, 1, range(C))
            woven(outputs1, scores1, 6)
            if not last:
                pe.wait_ge(s["xT_lo"], seq(PAIR, i + 1, 1))
            shift_row(i, 0)
            woven(outputs1, scores1)

        bodies(pe, NP, body)
        shift_row(NP - 1, 1)
        for b in range(PAIR):
            weight_scores(NP - 1, b)
        for b in range(PAIR):
            run(mixed(NP - 1, b))
        for b in range(PAIR):
            z_transposed(NP - 1, b)
        for b in range(PAIR):
            run(out_rows(NP - 1, b))


_INS = ["x", "cond_2048", "mask_BxSx1_fk1", "mask_BxS_ff1", "L0_cond_ln_w", "L0_cond_ln_b", "L0_cond_Wq",
        "L0_cond_bq", "L0_cond_Wk", "L0_cond_bk", "L0_cond_Wv", "L0_cond_bv", "L0_cond_W_emb", "L0_cond_b_emb",
        "L0_cond_ln2_w", "L0_cond_ln2_b", "L0_cond_W_out", "L0_cond_b_out", "L1_cond_norm_w", "L1_cond_norm_b",
        "L1_cond_q_w", "L1_cond_q_b", "L1_cond_k_w", "L1_cond_k_b", "L1_cond_v_w", "L1_cond_v_b",
        "L1_cond_emb_w", "L1_cond_emb_b", "L1_cond_sb_norm_w", "L1_cond_sb_norm_b", "L1_cond_out_w",
        "L1_cond_out_b"]


def kernel(**inputs):
    import numpy as _np
    import concourse.bacc as _bacc
    from concourse import mybir as _mybir
    from concourse.bass_utils import run_bass_kernel_spmd as _run

    nc = _bacc.Bacc("TRN2", target_bir_lowering=False, num_devices=1)
    arrays, tensors = {}, {}
    for name in _INS:
        a = _np.ascontiguousarray(inputs[name])
        arrays[f"in_{name}"] = a
        tensors[name] = nc.dram_tensor(f"in_{name}", a.shape, _mybir.dt.from_np(a.dtype), kind="ExternalInput").ap()
    out = nc.dram_tensor("out", inputs["x"].shape, _mybir.dt.float32, kind="ExternalOutput").ap()
    build(nc, tensors, out)
    r = _run(nc, [arrays], core_ids=[0])
    return r.results[0]["out"]
```
